# Optimizing a Trainium2 kernel written in Bass

```python
import numpy as np
import jax
import jax.numpy as jnp

def _softmax(x, axis=-1):
    return jax.nn.softmax(x, axis=axis)

def _gelu(x):
    return jax.nn.gelu(x, approximate=True)

def _silu(x):
    return jax.nn.silu(x)

def _sigmoid(x):
    return jax.nn.sigmoid(x)

def _layernorm(x, axis=-1, eps=1e-05):
    m = jnp.mean(x, axis=axis, keepdims=True)
    v = jnp.var(x, axis=axis, keepdims=True)
    return (x - m) / jnp.sqrt(v + eps)

def _scatter_add(tgt, idx, src, axis=0):
    return tgt.at[idx].add(src)

def _segment_sum(src, seg, n):
    return jax.ops.segment_sum(src, seg, n)
kernel_name = 'mk_decoder_preln_d2_seqx_r4_65a980'

def setup_inputs(seed: int=0):
    np.random.seed(seed)
    _w = jnp.asarray

    def _rec_inputs():
        import jax
        import jax.numpy as jnp
        _rk = jax.random.key(seed)
        x = -0.0003929 + 0.9999 * jax.random.normal(jax.random.fold_in(_rk, 1), (32, 128, 256), jnp.float32)
        _lenS = 128 - jax.random.randint(jax.random.fold_in(_rk, 7), (32,), 0, max(1, 128 // 4) + 1, jnp.int32)
        _lenS2 = 128 - jax.random.randint(jax.random.fold_in(_rk, 8), (32,), 0, max(1, 128 // 4) + 1, jnp.int32)
        _ctx_1024P = jax.random.normal(jax.random.fold_in(_rk, 11), (32, 16, 256), jnp.float32)
        _ctx_1024c = jax.random.dirichlet(jax.random.fold_in(_rk, 511), 0.3 * jnp.ones((16,), jnp.float32), (32, 128))
        _ctx_1024t = jnp.einsum('bsk,bkd->bsd', _ctx_1024c, _ctx_1024P)
        _ctx_1024t = _ctx_1024t * jax.lax.rsqrt(jnp.mean(jnp.square(_ctx_1024t)) + 1e-12) * 0.953939
        ctx_1024 = 2.81802e-05 + 1.00001 * (_ctx_1024t + 0.3 * jax.random.normal(jax.random.fold_in(_rk, 611), (32, 128, 256), jnp.float32))
        _validS = jnp.arange(128)[None, :] < _lenS[:, None]
        _validS2 = jnp.arange(128)[None, :] < _lenS2[:, None]
        _causal = jnp.tril(jnp.ones((128, 128), dtype=bool))
        mask_SxS2_bk0 = jnp.logical_not(jnp.broadcast_to(_validS2[0:1, :], (128, 128)))
        return (x, ctx_1024, mask_SxS2_bk0)
    x, ctx_1024, mask_SxS2_bk0 = _rec_inputs()

    def _L0_attn_setup():
        import jax, jax.numpy as jnp
        import numpy as np
        import math
        DIM = 256
        N_HEADS = 16
        HEAD_DIM = DIM // N_HEADS

        def get_sin_cos(seq_len, dim):
            theta = 10000.0 ** (-jnp.arange(0, dim, 2, dtype=jnp.float32) / dim)
            position = jnp.arange(seq_len, dtype=jnp.float32)
            freqs = position[:, None] * theta[None, :]
            emb = jnp.concatenate([jnp.sin(freqs), jnp.cos(freqs)], axis=-1)
            sin = emb[None, None]
            cos = emb[None, None]
            return (sin, cos)

        def rotate_half(x):
            x1, x2 = (x[..., ::2], x[..., 1::2])
            return jnp.concatenate([-x2, x1], axis=-1)

        def apply_rope(q, k):
            sin, cos = get_sin_cos(q.shape[2], q.shape[-1])
            q = q * cos + rotate_half(q) * sin
            k = k * cos + rotate_half(k) * sin
            return (q, k)
        key = jax.random.key(seed)
        ks = jax.random.split(key, 3)
        B, L, D = (2, 512, DIM)
        x = jax.random.normal(ks[0], (B, L, D), dtype=jnp.float32)
        Wqkv = jax.random.normal(ks[1], (D, 3 * D), dtype=jnp.float32) * (1.0 / math.sqrt(D))
        bqkv = jnp.zeros((3 * D,), dtype=jnp.float32)
        Wout = jax.random.normal(ks[2], (D, D), dtype=jnp.float32) * (1.0 / math.sqrt(D))
        bout = jnp.zeros((D,), dtype=jnp.float32)
        return {'x': x, 'Wqkv': Wqkv, 'bqkv': bqkv, 'Wout': Wout, 'bout': bout}
    _L0_attn_all = _L0_attn_setup()
    _L0_attn_in = {k: v for k, v in _L0_attn_all.items() if k in ('Wqkv', 'bqkv', 'Wout', 'bout')}
    del _L0_attn_all

    def _L0_xattn_setup():
        import jax, jax.numpy as jnp
        import numpy as np
        import math
        B, S, D = (8, 512, 256)
        key = jax.random.key(seed)
        ks = jax.random.split(key, 8)
        s_in = 1.0 / math.sqrt(D)
        s_ent = 1.0 / math.sqrt(2 * D)
        return {'x': jax.random.normal(ks[0], (B, S, D), dtype=jnp.float32), 'context': jax.random.normal(ks[1], (B, S, D), dtype=jnp.float32), 'Wq': jax.random.normal(ks[2], (D, D), dtype=jnp.float32) * s_in, 'bq': jnp.zeros((D,), jnp.float32), 'Wk': jax.random.normal(ks[3], (D, D), dtype=jnp.float32) * s_in, 'bk': jnp.zeros((D,), jnp.float32), 'Wv': jax.random.normal(ks[4], (D, D), dtype=jnp.float32) * s_in, 'bv': jnp.zeros((D,), jnp.float32), 'We': jax.random.normal(ks[5], (D, 2 * D), dtype=jnp.float32) * s_ent, 'be': jnp.zeros((D,), jnp.float32)}
    _L0_xattn_all = _L0_xattn_setup()
    _L0_xattn_in = {k: v for k, v in _L0_xattn_all.items() if k in ('Wq', 'bq', 'Wk', 'bk', 'Wv', 'bv', 'We', 'be')}
    del _L0_xattn_all

    def _L0_ffn_setup():
        import jax, jax.numpy as jnp
        import numpy as np
        B, S, D, F, E, R = (4, 512, 256, 1024, 8, 4)
        key = jax.random.key(seed)
        ks = jax.random.split(key, 8)
        s_in = 1.0 / np.sqrt(D)
        s_ff = 1.0 / np.sqrt(F)
        return {'hidden_states': jax.random.normal(ks[0], (B, S, D), jnp.float32), 'gate_W': jax.random.normal(ks[1], (E, D), jnp.float32) * s_in, 'gate_b': jnp.zeros((E,), jnp.float32), 'wi_W': jax.random.normal(ks[2], (F, D), jnp.float32) * s_in, 'wi_b': jnp.zeros((F,), jnp.float32), 'wo_W': jax.random.normal(ks[3], (D, F), jnp.float32) * s_ff, 'wo_b': jnp.zeros((D,), jnp.float32), 'lora_A': jax.random.normal(ks[4], (E, R, D), jnp.float32) * s_in, 'lora_B': jax.random.normal(ks[5], (E, F, R), jnp.float32) * 0.02}
    _L0_ffn_all = _L0_ffn_setup()
    _L0_ffn_in = {k: v for k, v in _L0_ffn_all.items() if k in ('gate_W', 'gate_b', 'wi_W', 'wi_b', 'wo_W', 'wo_b', 'lora_A', 'lora_B')}
    del _L0_ffn_all

    def _L1_attn_setup():
        import jax, jax.numpy as jnp
        import numpy as np
        N_HEADS = 16
        INPUT_DIM = 256
        EMBED_DIM = 256
        KEY_DIM = EMBED_DIM // N_HEADS
        BATCH = 4
        SEQ = 512

        def _uniform(key, shape, bound):
            return jax.random.uniform(key, shape, jnp.float32, -bound, bound)
        key = jax.random.key(seed)
        kq, k1, k2, k3, k4 = jax.random.split(key, 5)
        stdv_k = 1.0 / np.sqrt(KEY_DIM)
        stdv_e = 1.0 / np.sqrt(EMBED_DIM)
        return {'q': jax.random.normal(kq, (BATCH, SEQ, INPUT_DIM), jnp.float32), 'W_query': _uniform(k1, (N_HEADS, INPUT_DIM, KEY_DIM), stdv_k), 'W_key': _uniform(k2, (N_HEADS, INPUT_DIM, KEY_DIM), stdv_k), 'W_val': _uniform(k3, (N_HEADS, INPUT_DIM, KEY_DIM), stdv_k), 'W_out': _uniform(k4, (N_HEADS, KEY_DIM, EMBED_DIM), stdv_e)}
    _L1_attn_all = _L1_attn_setup()
    _L1_attn_in = {k: v for k, v in _L1_attn_all.items() if k in ('W_query', 'W_key', 'W_val', 'W_out')}
    del _L1_attn_all

    def _L1_xattn_setup():
        import jax, jax.numpy as jnp
        import numpy as np
        D_MODEL = 256
        NUM_HEADS = 16
        D_K = D_MODEL // NUM_HEADS
        B, S = (4, 512)
        key = jax.random.key(seed)
        ks = jax.random.split(key, 12)
        std = 1.0 / np.sqrt(D_MODEL)
        inp = {'q': jax.random.normal(ks[0], (B, S, D_MODEL), dtype=jnp.float32), 'k': jax.random.normal(ks[1], (B, S, D_MODEL), dtype=jnp.float32), 'v': jax.random.normal(ks[2], (B, S, D_MODEL), dtype=jnp.float32), 'mask': jnp.tril(jnp.ones((S, S), dtype=bool)), 'wq': jax.random.normal(ks[3], (D_MODEL, D_MODEL), dtype=jnp.float32) * std, 'bq': jnp.zeros((D_MODEL,), dtype=jnp.float32), 'wk': jax.random.normal(ks[4], (D_MODEL, D_MODEL), dtype=jnp.float32) * std, 'bk': jnp.zeros((D_MODEL,), dtype=jnp.float32), 'wv': jax.random.normal(ks[5], (D_MODEL, D_MODEL), dtype=jnp.float32) * std, 'bv': jnp.zeros((D_MODEL,), dtype=jnp.float32), 'wo': jax.random.normal(ks[6], (D_MODEL, D_MODEL), dtype=jnp.float32) * std, 'bo': jnp.zeros((D_MODEL,), dtype=jnp.float32)}
        return inp
    _L1_xattn_all = _L1_xattn_setup()
    _L1_xattn_in = {k: v for k, v in _L1_xattn_all.items() if k in ('wq', 'bq', 'wk', 'bk', 'wv', 'bv', 'wo', 'bo')}
    del _L1_xattn_all

    def _L1_ffn_setup():
        import jax, jax.numpy as jnp
        import numpy as np
        EPS = 1e-06
        LN_EPS = 1e-05

        def _absmean_core(W):
            gamma = jnp.mean(jnp.abs(W)) + EPS
            Ws = W / gamma
            Wq = jnp.sign(Ws) * jnp.minimum(jnp.round(jnp.abs(Ws)), 1.0)
            return (Wq, gamma)

        @jax.custom_vjp
        def absmean(W):
            return _absmean_core(W)[0]

        def _absmean_fwd(W):
            Wq, gamma = _absmean_core(W)
            return (Wq, gamma)

        def _absmean_bwd(gamma, g):
            return (g / gamma,)
        absmean.defvjp(_absmean_fwd, _absmean_bwd)

        def layernorm(x, w, b, eps=LN_EPS):
            mu = jnp.mean(x, axis=-1, keepdims=True)
            var = jnp.mean((x - mu) ** 2, axis=-1, keepdims=True)
            return (x - mu) * jax.lax.rsqrt(var + eps) * w + b
        key = jax.random.key(seed)
        k1, k2, k3 = jax.random.split(key, 3)
        d, h = (256, 1024)
        B, T = (8, 512)
        return {'x': jax.random.normal(k1, (B, T, d), jnp.float32), 'W_fc': jax.random.normal(k2, (h, d), jnp.float32), 'ln_w': jnp.ones((h,), jnp.float32), 'ln_b': jnp.zeros((h,), jnp.float32), 'W_proj': jax.random.normal(k3, (d, h), jnp.float32)}
    _L1_ffn_all = _L1_ffn_setup()
    _L1_ffn_in = {k: v for k, v in _L1_ffn_all.items() if k in ('W_fc', 'ln_w', 'ln_b', 'W_proj')}
    del _L1_ffn_all
    return {'x': x, 'ctx_1024': ctx_1024, 'mask_SxS2_bk0': mask_SxS2_bk0, 'L0_attn_Wqkv': _L0_attn_in['Wqkv'], 'L0_attn_bqkv': _L0_attn_in['bqkv'], 'L0_attn_Wout': _L0_attn_in['Wout'], 'L0_attn_bout': _L0_attn_in['bout'], 'L0_xattn_Wq': _L0_xattn_in['Wq'], 'L0_xattn_bq': _L0_xattn_in['bq'], 'L0_xattn_Wk': _L0_xattn_in['Wk'], 'L0_xattn_bk': _L0_xattn_in['bk'], 'L0_xattn_Wv': _L0_xattn_in['Wv'], 'L0_xattn_bv': _L0_xattn_in['bv'], 'L0_xattn_We': _L0_xattn_in['We'], 'L0_xattn_be': _L0_xattn_in['be'], 'L0_ffn_gate_W': _L0_ffn_in['gate_W'], 'L0_ffn_gate_b': _L0_ffn_in['gate_b'], 'L0_ffn_wi_W': _L0_ffn_in['wi_W'], 'L0_ffn_wi_b': _L0_ffn_in['wi_b'], 'L0_ffn_wo_W': _L0_ffn_in['wo_W'], 'L0_ffn_wo_b': _L0_ffn_in['wo_b'], 'L0_ffn_lora_A': _L0_ffn_in['lora_A'], 'L0_ffn_lora_B': _L0_ffn_in['lora_B'], 'L1_attn_W_query': _L1_attn_in['W_query'], 'L1_attn_W_key': _L1_attn_in['W_key'], 'L1_attn_W_val': _L1_attn_in['W_val'], 'L1_attn_W_out': _L1_attn_in['W_out'], 'L1_xattn_wq': _L1_xattn_in['wq'], 'L1_xattn_bq': _L1_xattn_in['bq'], 'L1_xattn_wk': _L1_xattn_in['wk'], 'L1_xattn_bk': _L1_xattn_in['bk'], 'L1_xattn_wv': _L1_xattn_in['wv'], 'L1_xattn_bv': _L1_xattn_in['bv'], 'L1_xattn_wo': _L1_xattn_in['wo'], 'L1_xattn_bo': _L1_xattn_in['bo'], 'L1_ffn_W_fc': _L1_ffn_in['W_fc'], 'L1_ffn_ln_w': _L1_ffn_in['ln_w'], 'L1_ffn_ln_b': _L1_ffn_in['ln_b'], 'L1_ffn_W_proj': _L1_ffn_in['W_proj']}

def reference(x, ctx_1024, mask_SxS2_bk0, L0_attn_Wqkv, L0_attn_bqkv, L0_attn_Wout, L0_attn_bout, L0_xattn_Wq, L0_xattn_bq, L0_xattn_Wk, L0_xattn_bk, L0_xattn_Wv, L0_xattn_bv, L0_xattn_We, L0_xattn_be, L0_ffn_gate_W, L0_ffn_gate_b, L0_ffn_wi_W, L0_ffn_wi_b, L0_ffn_wo_W, L0_ffn_wo_b, L0_ffn_lora_A, L0_ffn_lora_B, L1_attn_W_query, L1_attn_W_key, L1_attn_W_val, L1_attn_W_out, L1_xattn_wq, L1_xattn_bq, L1_xattn_wk, L1_xattn_bk, L1_xattn_wv, L1_xattn_bv, L1_xattn_wo, L1_xattn_bo, L1_ffn_W_fc, L1_ffn_ln_w, L1_ffn_ln_b, L1_ffn_W_proj):
    import jax
    import jax.numpy as jnp

    def _L0_attn_ref(x, Wqkv, bqkv, Wout, bout):
        import jax, jax.numpy as jnp
        import numpy as np
        import math
        DIM = 256
        N_HEADS = 16
        HEAD_DIM = DIM // N_HEADS

        def get_sin_cos(seq_len, dim):
            theta = 10000.0 ** (-jnp.arange(0, dim, 2, dtype=jnp.float32) / dim)
            position = jnp.arange(seq_len, dtype=jnp.float32)
            freqs = position[:, None] * theta[None, :]
            emb = jnp.concatenate([jnp.sin(freqs), jnp.cos(freqs)], axis=-1)
            sin = emb[None, None]
            cos = emb[None, None]
            return (sin, cos)

        def rotate_half(x):
            x1, x2 = (x[..., ::2], x[..., 1::2])
            return jnp.concatenate([-x2, x1], axis=-1)

        def apply_rope(q, k):
            sin, cos = get_sin_cos(q.shape[2], q.shape[-1])
            q = q * cos + rotate_half(q) * sin
            k = k * cos + rotate_half(k) * sin
            return (q, k)
        B, L, D = x.shape
        H, Hd = (N_HEADS, HEAD_DIM)
        qkv = (x @ Wqkv + bqkv).reshape(B, L, 3, H, Hd)
        q, k, v = (qkv[:, :, 0], qkv[:, :, 1], qkv[:, :, 2])
        q = q.transpose(0, 2, 1, 3)
        k = k.transpose(0, 2, 1, 3)
        v = v.transpose(0, 2, 1, 3)
        q, k = apply_rope(q, k)
        scores = jnp.einsum('bhqd,bhkd->bhqk', q, k) / math.sqrt(Hd)
        probs = jax.nn.softmax(scores, axis=-1)
        out = jnp.einsum('bhqk,bhkd->bhqd', probs, v)
        out = out.transpose(0, 2, 1, 3).reshape(B, L, D)
        return out @ Wout + bout

    def _L0_xattn_ref(x, context, Wq, bq, Wk, bk, Wv, bv, We, be):
        import jax, jax.numpy as jnp
        import numpy as np
        import math
        B, S, D = (8, 512, 256)
        q = jnp.einsum('bsd,ed->bse', x, Wq) + bq
        k = jnp.einsum('bsd,ed->bse', context, Wk) + bk
        v = jnp.einsum('bsd,ed->bse', context, Wv) + bv
        entangled = jnp.tanh(jnp.einsum('bsd,ed->bse', jnp.concatenate([q, k], axis=-1), We) + be)
        scale = 1.0 / math.sqrt(x.shape[-1])
        scores = jnp.einsum('bqd,bkd->bqk', entangled, v) * scale
        attn = jax.nn.softmax(scores, axis=-1)
        return jnp.einsum('bqk,bkd->bqd', attn, v)

    def _L0_ffn_ref(hidden_states, gate_W, gate_b, wi_W, wi_b, wo_W, wo_b, lora_A, lora_B):
        import jax, jax.numpy as jnp
        import numpy as np
        B, S, D, F, E, R = (4, 512, 256, 1024, 8, 4)
        x = hidden_states
        logits = jnp.einsum('bsd,ed->bse', x, gate_W) + gate_b
        top1 = jnp.argmax(jax.nn.softmax(logits, axis=-1), axis=-1)
        base = jnp.einsum('bsd,fd->bsf', x, wi_W) + wi_b
        out = jnp.zeros_like(x)
        for i in range(lora_A.shape[0]):
            lora = jnp.einsum('bsr,fr->bsf', jnp.einsum('bsd,rd->bsr', x, lora_A[i]), lora_B[i])
            inter = jax.nn.relu(base + lora)
            expert_out = jnp.einsum('bsf,df->bsd', inter, wo_W) + wo_b
            mask = (top1 == i).astype(x.dtype)[..., None]
            out = out + mask * expert_out
        return out

    def _L1_attn_ref(q, W_query, W_key, W_val, W_out):
        import jax, jax.numpy as jnp
        import numpy as np
        N_HEADS = 16
        INPUT_DIM = 256
        EMBED_DIM = 256
        KEY_DIM = EMBED_DIM // N_HEADS
        BATCH = 4
        SEQ = 512

        def _uniform(key, shape, bound):
            return jax.random.uniform(key, shape, jnp.float32, -bound, bound)
        norm = 1.0 / np.sqrt(KEY_DIM)
        Q = jnp.einsum('bsd,hdk->hbsk', q, W_query)
        K = jnp.einsum('bsd,hdk->hbsk', q, W_key)
        V = jnp.einsum('bsd,hdv->hbsv', q, W_val)
        scores = norm * jnp.einsum('hbqk,hbnk->hbqn', Q, K)
        attn = jax.nn.softmax(scores, axis=-1)
        heads = jnp.einsum('hbqn,hbnv->hbqv', attn, V)
        out = jnp.einsum('hbqv,hve->bqe', heads, W_out)
        return out

    def _L1_xattn_ref(q, k, v, mask, wq, bq, wk, bk, wv, bv, wo, bo):
        import jax, jax.numpy as jnp
        import numpy as np
        D_MODEL = 256
        NUM_HEADS = 16
        D_K = D_MODEL // NUM_HEADS
        B, S = (4, 512)
        b, s, d = q.shape

        def proj(x, w, bias):
            return (x @ w.T + bias).reshape(b, -1, NUM_HEADS, D_K).transpose(0, 2, 1, 3)
        qh = proj(q, wq, bq)
        kh = proj(k, wk, bk)
        vh = proj(v, wv, bv)
        scale = 1.0 / np.sqrt(D_K)
        scores = jnp.einsum('bhqd,bhkd->bhqk', qh, kh) * scale
        scores = jnp.where(mask[None, None, :, :], scores, -1000000000.0)
        probs = jax.nn.softmax(scores, axis=-1)
        out = jnp.einsum('bhqk,bhkd->bhqd', probs, vh)
        out = out.transpose(0, 2, 1, 3).reshape(b, s, d)
        return out @ wo.T + bo

    def _L1_ffn_ref(x, W_fc, ln_w, ln_b, W_proj):
        import jax, jax.numpy as jnp
        import numpy as np
        EPS = 1e-06
        LN_EPS = 1e-05

        def _absmean_core(W):
            gamma = jnp.mean(jnp.abs(W)) + EPS
            Ws = W / gamma
            Wq = jnp.sign(Ws) * jnp.minimum(jnp.round(jnp.abs(Ws)), 1.0)
            return (Wq, gamma)

        @jax.custom_vjp
        def absmean(W):
            return _absmean_core(W)[0]

        def _absmean_fwd(W):
            Wq, gamma = _absmean_core(W)
            return (Wq, gamma)

        def _absmean_bwd(gamma, g):
            return (g / gamma,)
        absmean.defvjp(_absmean_fwd, _absmean_bwd)

        def layernorm(x, w, b, eps=LN_EPS):
            mu = jnp.mean(x, axis=-1, keepdims=True)
            var = jnp.mean((x - mu) ** 2, axis=-1, keepdims=True)
            return (x - mu) * jax.lax.rsqrt(var + eps) * w + b
        h = jnp.einsum('btd,hd->bth', x, absmean(W_fc))
        h = jax.nn.gelu(h, approximate=False)
        h = layernorm(h, ln_w, ln_b)
        return jnp.einsum('bth,dh->btd', h, absmean(W_proj))
    x = x + _L0_attn_ref(_layernorm(x, axis=-1), L0_attn_Wqkv, L0_attn_bqkv, L0_attn_Wout, L0_attn_bout)
    x = x + _L0_xattn_ref(_layernorm(x, axis=-1), ctx_1024, L0_xattn_Wq, L0_xattn_bq, L0_xattn_Wk, L0_xattn_bk, L0_xattn_Wv, L0_xattn_bv, L0_xattn_We, L0_xattn_be)
    x = x + _L0_ffn_ref(_layernorm(x, axis=-1), L0_ffn_gate_W, L0_ffn_gate_b, L0_ffn_wi_W, L0_ffn_wi_b, L0_ffn_wo_W, L0_ffn_wo_b, L0_ffn_lora_A, L0_ffn_lora_B)
    x = x + _L1_attn_ref(_layernorm(x, axis=-1), L1_attn_W_query, L1_attn_W_key, L1_attn_W_val, L1_attn_W_out)
    x = x + _L1_xattn_ref(_layernorm(x, axis=-1), ctx_1024, ctx_1024, mask_SxS2_bk0, L1_xattn_wq, L1_xattn_bq, L1_xattn_wk, L1_xattn_bk, L1_xattn_wv, L1_xattn_bv, L1_xattn_wo, L1_xattn_bo)
    x = x + _L1_ffn_ref(_layernorm(x, axis=-1), L1_ffn_W_fc, L1_ffn_ln_w, L1_ffn_ln_b, L1_ffn_W_proj)
    return x

_drawn_inputs = setup_inputs


def setup_inputs(seed=0):
    import zlib

    import numpy as np

    out = dict(_drawn_inputs(seed))
    spreads = {'L0_attn_bqkv': (0.0, 0.1),
     'L0_attn_bout': (0.0, 0.1),
     'L0_xattn_bq': (0.0, 0.512),
     'L0_xattn_bk': (0.0, 0.522),
     'L0_xattn_bv': (0.0, 0.1),
     'L0_xattn_be': (0.0, 0.391),
     'L0_ffn_gate_b': (0.0, 0.489),
     'L0_ffn_wi_b': (0.0, 0.1),
     'L0_ffn_wo_b': (0.0, 0.1),
     'L1_xattn_bq': (0.0, 0.1),
     'L1_xattn_bk': (0.0, 0.1),
     'L1_xattn_bv': (0.0, 0.1),
     'L1_xattn_bo': (0.0, 0.1),
     'L1_ffn_ln_w': (1.0, 0.2),
     'L1_ffn_ln_b': (0.0, 0.1)}
    factors = {}
    for name, (base, spread) in spreads.items():
        noise = np.random.default_rng([zlib.crc32(name.encode()), seed]).standard_normal(out[name].shape)
        drawn = base * np.exp(spread * noise) if base else spread * noise
        out[name] = jnp.asarray(drawn.astype(out[name].dtype))
    for name, factor in factors.items():
        out[name] = (out[name] * factor).astype(out[name].dtype)
    return out
```

```python
import numpy as np
import concourse.bass as bass
from concourse import mybir
from contextlib import ExitStack

FP32 = mybir.dt.float32
F32R = mybir.dt.float32r
BF16 = mybir.dt.bfloat16
U8 = mybir.dt.uint8
U32 = mybir.dt.uint32
ALU = mybir.AluOpType
ACT = mybir.ActivationFunctionType
AXX = mybir.AxisListType.X

P = 128
NB = 32
D = 256
KC = D // P
PAIR = 2
NG = NB // PAIR
TOK = PAIR * P
H, DH = 16, 16
QH = 4
NQ = H // QH
STEPS = PAIR * NQ
F = 1024
E, R = 8, 4
LN_EPS = 1e-5
LN_LINKS = 2 * PAIR + 1
ABSMEAN_EPS = 1e-6
MASKED = -4.0e9


def at_least(eng, sem, value):
    if not isinstance(value, int) or value > 0:
        eng.wait_ge(sem, value)


def wait_apart(dve, link, value, mark):
    dve.wait_ge(link, value)
    dve.memset(mark[:], 0.0).then_inc(link, 1)


def cx_count(w, parity):
    return (w - parity) * 8 + 16


def f32(ap):
    return ap.bitcast(FP32)


class Names:

    def __init__(self, nc, ctx, stage):
        self.nc, self.ctx, self.stage, self.sems = nc, ctx, stage, []

    def sb(self, name, shape, dt=FP32):
        return self.ctx.enter_context(self.nc.sbuf_tensor(f"{self.stage}_{name}", shape, dt))

    def ps(self, name):
        return self.ctx.enter_context(self.nc.psum_tensor(f"{self.stage}_{name}", [P, 512], FP32))

    def sem(self, name):
        handle = self.ctx.enter_context(self.nc.semaphore(f"{self.stage}_{name}"))
        self.sems.append(handle)
        return handle

    def clear_semaphores(self):
        with self.nc.Block() as block:

            @block.gpsimd
            def _(pool):
                for handle in self.sems:
                    pool.sem_clear(handle)


def three_pass(pe, out, w_hi, w_lo, m_hi, m_lo, chunks):
    last = None
    for k in range(chunks):
        for n, (w, m) in enumerate(((w_hi, m_hi), (w_lo, m_hi), (w_hi, m_lo))):
            last = pe.matmul(out, w(k), m(k), start=(k == 0 and n == 0), stop=(k == chunks - 1 and n == 2))
    return last


def attention_stage(nc, name, x_res, consts, w_dram, rows, ctx_dram=None, mask_dram=None, rope=False,
                    k_bias=False, v_bias=False, o_bias=False, x_dram=None):
    nm_ctx = ExitStack()
    nm = Names(nc, nm_ctx, name)
    sb, sem = nm.sb, nm.sem
    ident, ident_b, neg_ident_b, head_mask = (consts[k] for k in ("ident", "ident_b", "neg_ident_b", "head_mask"))

    NW = 4 * D
    w_raw = sb("w_raw", [P, KC, NW])
    w_hi = sb("w_hi", [P, KC, NW], F32R)
    w_lo = sb("w_lo", [P, KC, NW], F32R)
    WQ, WK, WV, WO = (slice(n * D, (n + 1) * D) for n in range(4))
    bias_cols = sb("bias_cols", [P, 4])
    row_v = sb("row_v", [P, PAIR, D])
    row_o = sb("row_o", [P, PAIR, D])
    q_mul = sb("q_mul", [P, TOK])

    stats = sb("stats", [P, PAIR, 6])
    moments = sb("moments", [P, PAIR, 2])
    var_eps = sb("var_eps", [P, PAIR])
    ln_mark = sb("ln_mark", [P, 1])
    rstd = sb("rstd", [P, PAIR])
    xn = sb("xn", [P, PAIR, D])
    xT_hi = sb("xT_hi", [P, KC, TOK], F32R)
    xT_lo = sb("xT_lo", [P, KC, TOK], F32R)
    q32 = sb("q32", [P, KC, TOK])
    k32 = sb("k32", [P, KC, TOK])
    q_lo = sb("q_lo", [P, KC, TOK])
    q_hi = [sb(f"q_hi{i}", [P, KC, TOK], F32R) for i in range(2)]
    k_hi = [sb(f"k_hi{i}", [P, KC, TOK], F32R) for i in range(2)]
    k_lo = [sb(f"k_lo{i}", [P, KC, TOK], F32R) for i in range(2)]
    qm_hi = [sb(f"qm_hi{i}", [P, KC, PAIR, QH, P], F32R) for i in range(2)]
    qm_lo = [sb(f"qm_lo{i}", [P, KC, PAIR, QH, P], F32R) for i in range(2)]
    km_hi = [sb(f"km_hi{i}", [P, KC, PAIR, QH, P], F32R) for i in range(2)]
    v_pad = [sb(f"v_pad{i}", [P, PAIR, H, 2 * DH]) for i in range(2)]
    row_max = sb("row_max", [P, 4, QH], BF16)
    probs = sb("probs", [P, 4, QH * P])
    inv_den = sb("inv_den", [P, D])
    o32 = sb("o32", [P, KC, P])
    o_hi = sb("o_hi", [P, PAIR, KC, P], F32R)
    o_lo = sb("o_lo", [P, PAIR, KC, P], F32R)

    S1 = [nm.ps(f"S1_{i}") for i in range(2)]
    S2 = [nm.ps(f"S2_{i}") for i in range(2)]
    AV = [nm.ps(f"AV_{i}") for i in range(2)]
    FA, FB = nm.ps("FA"), nm.ps("FB")

    if rope:
        w_turned = sb("w_turned", [P, KC, 2 * D])
        bias_turned = sb("bias_turned", [P, 4])
    row_v_flat = row_v[:].rearrange("p b d -> p (b d)")

    cross = ctx_dram is not None
    if cross:
        mask_link = sem("mask_link")
        cx = [sb(f"cx{i}", [P, PAIR, D]) for i in range(2)]
        cT_hi = sb("cT_hi", [P, KC, TOK], F32R)
        cT_lo = sb("cT_lo", [P, KC, TOK], F32R)
        mask_u8 = sb("mask_u8", [P, P], U8)
        keep = sb("keep", [P, P])
        any_kept = sb("any_kept", [P, 1])
        add_mask32 = sb("add_mask32", [P, P])
        add_mask = sb("add_mask", [P, P], BF16)
        add_maskT = sb("add_maskT", [P, P], BF16)
        cx_in = [sem(f"cx_in{i}") for i in range(2)]
        ctx_full, ctx_hi, ctx_lo = sem("ctx_full"), sem("ctx_hi"), sem("ctx_lo")
    kvT_hi, kvT_lo = (cT_hi, cT_lo) if cross else (xT_hi, xT_lo)

    w_in, x_in, w_fold, hi_ok, w_ok = sem("w_in"), sem("x_in"), sem("w_fold"), sem("hi_ok"), sem("w_ok")
    zeroed, setup, setup_pe = sem("zeroed"), sem("setup"), sem("setup_pe")
    ln_link, var_ok, rstd_ok, xn_ok, biased = sem("ln_link"), sem("var_ok"), sem("rstd_ok"), sem("xn_ok"), sem("biased")
    pt_full, pt_hi, pt_lo = sem("pt_full"), sem("pt_hi"), sem("pt_lo")
    q_full, q_free, qhi_ok, qlo_ok, qmhi_ok, qm_ok = (sem(n) for n in ("q_full", "q_free", "qhi_ok", "qlo_ok", "qmhi_ok", "qm_ok"))
    k_full, k_free, khi_ok, klo_ok, km_ok = (sem(n) for n in ("k_full", "k_free", "khi_ok", "klo_ok", "km_ok"))
    v_full, v_free, out_full, out_free = sem("v_full"), sem("v_free"), sem("out_full"), sem("out_free")
    s1_full, max_ok, s2_full, exp_ok, av_full = (sem(n) for n in ("s1_full", "max_ok", "s2_full", "exp_ok", "av_full"))
    inv_ok, o32_ok, ohi_ok, olo_ok = sem("inv_ok"), sem("o32_ok"), sem("ohi_ok"), sem("olo_ok")

    n_loads = len(w_dram) + len(rows)
    dve_q = rope or cross
    dve_k = rope

    def schedule(eng, group):
        for G in range(-1, 3):
            group(G, G % 2)
        with eng.Fori(1, (NG - 4) // 2) as i:
            group(i * 2 + 1, 1)
            group(i * 2 + 2, 0)
        for G in range(NG - 3, NG + 1):
            group(G, G % 2)

    def has_norm(G):
        return not isinstance(G, int) or G + 2 < NG

    def has_window(G):
        return not isinstance(G, int) or G + 1 < NG

    def has_step(G, t):
        return not isinstance(G, int) or 0 <= STEPS * G + t < STEPS * NG

    def whole(G):
        return not isinstance(G, int) or 0 <= G < NG

    def place(t):
        tt = t % STEPS
        return tt // NQ, (tt % NQ) // 2, tt % 2, t < 0

    def v_places(flat, u):
        v = flat.rearrange("p (b c u v e) -> p (b c) u v e", c=KC, u=2, v=QH, e=2 * DH, b=PAIR)
        return v[:, :, u, :, u * DH:(u + 1) * DH]

    def v_cols(bank, u):
        return bank[:].rearrange("p (b c u v e) -> p (b c) u v e", c=KC, u=2, v=QH, e=DH, b=PAIR)[:, :, u]

    with nc.Block() as block:

        @block.sync
        def _(sp):
            for dst, src in w_dram:
                sp.dma_start(w_raw[:, :, dst * D:dst * D + src.shape[2]], src).then_inc(w_in, 16)
            for which, src in rows:
                dst = {"bias_cols": bias_cols, "row_v": row_v, "row_o": row_o, "q_mul": q_mul}.get(which)
                if which == "mask":
                    dst = mask_u8
                elif which == "w_turned":
                    dst = w_turned
                elif which == "bias_turned":
                    dst = bias_turned
                sp.dma_start(dst[:], src).then_inc(w_in, 16)
            if x_dram is not None:
                for n in range(4):
                    part = slice(n * NB // 4, (n + 1) * NB // 4)
                    sp.dma_start(x_res[:, part, :], x_dram[:, part, :]).then_inc(x_in, 16)
            if cross:
                def load_ctx(w, parity):
                    at_least(sp, ctx_full, w - 1)
                    src = ctx_dram[:, w * PAIR:(w + 1) * PAIR, :] if isinstance(w, int) else \
                        ctx_dram[:, bass.ds(w * PAIR, PAIR), :]
                    sp.dma_start(cx[parity][:], src).then_inc(cx_in[parity], 16)
                load_ctx(0, 0)
                load_ctx(1, 1)
                with sp.Fori(1, NG // 2) as i:
                    load_ctx(i * 2, 0)
                    load_ctx(i * 2 + 1, 1)

        @block.gpsimd
        def _(pool):
            for i in range(2):
                pool.memset(v_pad[i][:], 0.0).then_inc(zeroed, 1)
            if o_bias:
                pool.wait_ge(w_in, 16 * n_loads)

            def window(w):
                pool.wait_ge(ln_link, (w + 1) * LN_LINKS)
                at_least(pool, xn_ok, w)
                pool.tensor_tensor(var_eps[:], moments[:, :, 1], consts["ln_eps"][:], ALU.add).then_inc(var_ok, 1)
                pool.wait_ge(var_ok, w + 1)
                pool.tensor_tensor(rstd[:], var_eps[:], consts["minus_half"][:], ALU.pow).then_inc(rstd_ok, 1)
                if o_bias:
                    pool.wait_ge(xn_ok, w + 1)
                    x = x_res[:, w * PAIR:(w + 1) * PAIR, :] if isinstance(w, int) else x_res[:, bass.ds(w * PAIR, PAIR), :]
                    pool.tensor_tensor(x, x, row_o[:], ALU.add).then_inc(biased, 1)
            window(0)
            with pool.Fori(1, NG) as w:
                window(w)

        @block.scalar
        def _(act):
            act.wait_ge(*((w_fold, 1) if rope else (w_in, 16 * n_loads)))
            act.activation(w_hi[:], w_raw[:], ACT.Copy).then_inc(hi_ok, 1)
            if cross:
                act.wait_ge(setup_pe, 1)
                act.activation(add_maskT[:], FA[:, 0:P], ACT.Copy).then_inc(setup, 1)
                act.wait_ge(setup_pe, 2)
                for b in range(PAIR):
                    last = act.activation(q_mul[:, b * P:(b + 1) * P], FB[:, 0:P], ACT.Copy)
                last.then_inc(setup, 1)

            def exp_step(G, t, parity):
                T = G * STEPS + t
                act.wait_ge(s2_full, T + 1)
                at_least(act, av_full, T - 3)
                act.activation(probs[:, t % 4, :], S2[t % 2][:], ACT.Exp, scale=DH ** -0.5).then_inc(exp_ok, 1)

            def out_high(B, G, b):
                act.wait_ge(o32_ok, B + 1)
                at_least(act, out_full, G)
                act.activation(o_hi[:, b], o32[:], ACT.Copy).then_inc(ohi_ok, 1)

            def group(G, parity):
                w, wp = G + 1, 1 - parity
                for t in range(STEPS):
                    if has_step(G, t - 2):
                        exp_step(G, t - 2, parity)
                    if has_window(G) and t == 1:
                        act.wait_ge(pt_full, w + 1)
                        at_least(act, v_full, w)
                        act.activation(xT_hi[:], FA[:].rearrange("p (c t) -> p c t", c=KC),
                                       ACT.Copy).then_inc(pt_hi, 1)
                        if cross:
                            act.wait_ge(ctx_full, w + 1)
                            act.activation(cT_hi[:], FB[:].rearrange("p (c t) -> p c t", c=KC),
                                           ACT.Copy).then_inc(ctx_hi, 1)
                    if has_window(G) and t == 4:
                        if not dve_q:
                            act.wait_ge(q_full, w + 1)
                            at_least(act, qm_ok, w)
                            act.activation(q32[:], FB[:].rearrange("p (c t) -> p c t", c=KC),
                                           ACT.Copy).then_inc(q_free, 1)
                        act.wait_ge(q_free, w + 1)
                        at_least(act, s1_full, (w - 1) * STEPS)
                        act.activation(q_hi[wp][:], q32[:], ACT.Copy).then_inc(qhi_ok, 1)
                        at_least(act, s2_full, (w - 1) * STEPS)
                        for v in range(QH):
                            last = act.activation(qm_hi[wp][:, :, :, v, :],
                                                  q32[:].rearrange("p c (b t) -> p c b t", b=PAIR),
                                                  ACT.Copy, scale=head_mask[:, v:v + 1])
                        last.then_inc(qmhi_ok, 1)
                    if has_window(G) and t == 5:
                        if not dve_k:
                            act.wait_ge(k_full, w + 1)
                            at_least(act, klo_ok, w)
                            for c in range(KC):
                                if not k_bias:
                                    last = act.activation(k32[:, c], FA[:, c * TOK:(c + 1) * TOK], ACT.Copy)
                                else:
                                    last = act.activation(k32[:, c], FA[:, c * TOK:(c + 1) * TOK], ACT.Identity,
                                                          bias=bias_cols[:, KC + c:KC + c + 1])
                            last.then_inc(k_free, 1)
                        act.wait_ge(k_free, w + 1)
                        at_least(act, s2_full, (w - 1) * STEPS)
                        act.activation(k_hi[wp][:], k32[:], ACT.Copy).then_inc(khi_ok, 1)
                        for v in range(QH):
                            last = act.activation(km_hi[wp][:, :, :, v, :],
                                                  k32[:].rearrange("p c (b t) -> p c b t", b=PAIR),
                                                  ACT.Copy, scale=head_mask[:, v:v + 1])
                        last.then_inc(km_ok, 1)
                    if has_window(G) and t == 6 and not v_bias:
                        act.wait_ge(v_full, w + 1)
                        at_least(act, av_full, (w - 1) * STEPS)
                        if isinstance(w, int):
                            at_least(act, zeroed, 2)
                        v_out = v_pad[wp][:].rearrange("p b h e -> p (b h e)")
                        act.activation(v_places(v_out, 0), v_cols(FB, 0), ACT.Copy)
                        act.activation(v_places(v_out, 1), v_cols(FB, 1), ACT.Copy).then_inc(v_free, 1)
                    if t == 3 and whole(G - 1):
                        out_high(G * PAIR - 1, G - 1, 1)
                    if t == 7 and whole(G):
                        out_high(G * PAIR, G, 0)
            schedule(act, group)

        @block.vector
        def _(dve):
            dve.wait_ge(w_in, 16 * n_loads)
            if rope:
                new = w_raw[:, :, 0:2 * D].rearrange("p k (h e) -> p k h e", e=DH)
                turned = w_turned[:].rearrange("p k (h e) -> p k h e", e=DH)
                for k in range(KC):
                    dve.tensor_tensor(new[:, k, :, 0:DH // 2], new[:, k, :, 0:DH // 2],
                                      turned[:, k, :, 0:DH // 2], ALU.subtract)
                    dve.tensor_tensor(new[:, k, :, DH // 2:], new[:, k, :, DH // 2:],
                                      turned[:, k, :, DH // 2:], ALU.add)
                dve.scalar_tensor_tensor(bias_cols[:], bias_turned[:], consts["turn_sign"][:], bias_cols[:],
                                         op0=ALU.mult, op1=ALU.add).then_inc(w_fold, 1)
            dve.wait_ge(hi_ok, 1)
            dve.tensor_tensor(w_lo[:], w_raw[:], f32(w_hi[:]), ALU.subtract).then_inc(w_ok, 1)
            if cross:
                dve.tensor_copy(keep[:], mask_u8[:]).then_inc(mask_link, 1)
                dve.wait_ge(mask_link, 1)
                dve.tensor_reduce(any_kept[:], keep[:], AXX, ALU.max).then_inc(mask_link, 1)
                dve.tensor_scalar(add_mask32[:], keep[:], -1.0, -MASKED, ALU.add, ALU.mult).then_inc(mask_link, 1)
                dve.wait_ge(mask_link, 3)
                dve.tensor_scalar(add_mask32[:], add_mask32[:], any_kept[:], None, ALU.mult).then_inc(mask_link, 1)
                dve.wait_ge(mask_link, 4)
                dve.tensor_copy(add_mask[:], add_mask32[:]).then_inc(mask_link, 1)

            def x_seq(w, b):
                return x_res[:, w * PAIR + b, :] if isinstance(w, int) else \
                    x_res[:, bass.ds(w * PAIR + b, 1), :].rearrange("p b d -> p (b d)")

            def moments_of(w):
                if x_dram is not None and isinstance(w, int):
                    dve.wait_ge(x_in, 64)
                for b in range(PAIR):
                    dve.bn_stats(stats[:, b, :], x_seq(w, b)).then_inc(ln_link, 1)
                wait_apart(dve, ln_link, w * LN_LINKS + PAIR, ln_mark)
                for b in range(PAIR):
                    dve.bn_aggr(moments[:, b, :], stats[:, b, :]).then_inc(ln_link, 1)

            def layer_norm(w):
                dve.wait_ge(rstd_ok, w + 1)
                at_least(dve, pt_full, w)
                for b in range(PAIR):
                    last = dve.tensor_scalar(xn[:, b, :], x_seq(w, b), moments[:, b, 0:1], rstd[:, b:b + 1],
                                             ALU.subtract, ALU.mult)
                last.then_inc(xn_ok, 1)

            def max_step(G, t):
                T = G * STEPS + t
                dve.wait_ge(s1_full, T + 1)
                at_least(dve, s2_full, T - 3)
                dve.tensor_reduce(row_max[:, t % 4, :], S1[t % 2][:].rearrange("p (h k) -> p h k", h=QH),
                                  AXX, ALU.max).then_inc(max_ok, 1)

            def normalise(B, b):
                dve.wait_ge(av_full, B * NQ + NQ)
                dve.reciprocal(inv_den[:], AV[b][:, D:2 * D]).then_inc(inv_ok, 1)
                at_least(dve, ohi_ok, B)
                dve.wait_ge(inv_ok, B + 1)
                dve.tensor_tensor(o32[:].rearrange("p c t -> p (c t)"), AV[b][:, 0:D], inv_den[:],
                                  ALU.mult).then_inc(o32_ok, 1)

            def out_low(B, b):
                dve.wait_ge(ohi_ok, B + 1)
                dve.tensor_tensor(o_lo[:, b], o32[:], f32(o_hi[:, b]), ALU.subtract).then_inc(olo_ok, 1)

            def group(G, parity):
                w, wp = G + 1, 1 - parity
                for t in range(STEPS):
                    if has_step(G, t):
                        max_step(G, t)
                    if t == 0 and whole(G - 1):
                        out_low(G * PAIR - PAIR, 0)
                    if t == 4 and whole(G - 1):
                        out_low(G * PAIR - 1, 1)
                    if t == 0 and isinstance(G, int) and G < 0:
                        moments_of(0)
                        layer_norm(0)
                    if has_norm(G) and t == 2:
                        moments_of(w + 1)
                    if has_norm(G) and t == 3:
                        layer_norm(w + 1)
                    if has_window(G) and t == 2:
                        dve.wait_ge(pt_hi, w + 1)
                        dve.tensor_tensor(xT_lo[:], FA[:].rearrange("p (c t) -> p c t", c=KC), f32(xT_hi[:]),
                                          ALU.subtract).then_inc(pt_lo, 1)
                        if cross:
                            dve.wait_ge(ctx_hi, w + 1)
                            dve.tensor_tensor(cT_lo[:], FB[:].rearrange("p (c t) -> p c t", c=KC), f32(cT_hi[:]),
                                              ALU.subtract).then_inc(ctx_lo, 1)
                    if t == 3 and whole(G - 1):
                        normalise(G * PAIR - 1, 1)
                    if has_window(G) and t == 4 and dve_q:
                        dve.wait_ge(q_full, w + 1)
                        at_least(dve, qmhi_ok, w)
                        for c in range(KC):
                            last = dve.scalar_tensor_tensor(q32[:, c], FB[:, c * TOK:(c + 1) * TOK],
                                                            bias_cols[:, c:c + 1], q_mul[:], op0=ALU.add, op1=ALU.mult)
                        last.then_inc(q_free, 1)
                    if has_window(G) and t == 5:
                        if dve_k:
                            dve.wait_ge(k_full, w + 1)
                            at_least(dve, km_ok, w)
                            for c in range(KC):
                                last = dve.scalar_tensor_tensor(k32[:, c], FA[:, c * TOK:(c + 1) * TOK],
                                                                bias_cols[:, KC + c:KC + c + 1], q_mul[:],
                                                                op0=ALU.add, op1=ALU.mult)
                            last.then_inc(k_free, 1)
                        dve.wait_ge(qhi_ok, w + 1)
                        dve.tensor_tensor(q_lo[:], q32[:], f32(q_hi[wp][:]), ALU.subtract).then_inc(qlo_ok, 1)
                        at_least(dve, s2_full, (w - 1) * STEPS)
                    if has_window(G) and t == 6:
                        dve.wait_ge(qlo_ok, w + 1)
                        for v in range(QH):
                            last = dve.tensor_scalar(qm_lo[wp][:, :, :, v, :],
                                                     q_lo[:].rearrange("p c (b t) -> p c b t", b=PAIR),
                                                     head_mask[:, v:v + 1], None, ALU.mult)
                        last.then_inc(qm_ok, 1)
                        dve.wait_ge(khi_ok, w + 1)
                        dve.tensor_tensor(k_lo[wp][:], k32[:], f32(k_hi[wp][:]), ALU.subtract).then_inc(klo_ok, 1)
                        if v_bias:
                            dve.wait_ge(v_full, w + 1)
                            at_least(dve, av_full, (w - 1) * STEPS)
                            if isinstance(w, int):
                                dve.wait_ge(zeroed, 2)
                            flat = v_pad[wp][:].rearrange("p b h e -> p (b h e)")
                            for u in range(2):
                                last = dve.tensor_tensor(v_places(flat, u), v_cols(FB, u), v_cols(row_v_flat, u), ALU.add)
                            last.then_inc(v_free, 1)
                    if t == 7 and whole(G - 1):
                        dve.wait_ge(out_full, G)
                        if o_bias:
                            dve.wait_ge(biased, G)
                        x = x_res[:, (G - 1) * PAIR:G * PAIR, :] if isinstance(G, int) else \
                            x_res[:, bass.ds((G - 1) * PAIR, PAIR), :]
                        dve.tensor_tensor(x, x, FA[:].rearrange("p (b d) -> p b d", b=PAIR), ALU.add).then_inc(out_free, 1)
                    if t == 7 and whole(G):
                        normalise(G * PAIR, 0)
            schedule(dve, group)

        @block.tensor
        def _(pe):
            if cross:
                pe.wait_ge(mask_link, 5)
                pe.transpose(FA[:, 0:P], add_mask32[:], ident[:]).then_inc(setup_pe, 1)
                pe.matmul(FB[:, 0:P], any_kept[:].to_broadcast([P, P]), ident[:], start=True, stop=True).then_inc(setup_pe, 1)
                pe.wait_ge(setup, 2)
            pe.wait_ge(hi_ok, 1)
            pe.wait_ge(w_ok, 1)

            def s1_step(G, t, parity):
                T = G * STEPS + t
                b, c, u, _ = place(t)
                rows64 = slice(64 * u, 64 * u + 64)
                if t == 0:
                    pe.wait_ge(qhi_ok, G + 1)
                    pe.wait_ge(km_ok, G + 1)
                at_least(pe, max_ok, T - 1)
                last = pe.matmul(S1[t % 2][:], q_hi[parity][rows64, c, b * P:(b + 1) * P],
                                 km_hi[parity][rows64, c, b].rearrange("p h t -> p (h t)"), start=True, stop=not cross)
                if cross:
                    for v in range(QH):
                        last = pe.matmul(S1[t % 2][:, v * P:(v + 1) * P], ident_b[:], add_mask[:],
                                         start=False, stop=v == QH - 1)
                last.then_inc(s1_full, 1)

            def s2_step(G, t, parity):
                T = G * STEPS + t
                b, c, u, before = place(t)
                par = 1 - parity if before else parity
                rows64 = slice(64 * u, 64 * u + 64)
                tok = slice(b * P, (b + 1) * P)
                if t == 0:
                    pe.wait_ge(qmhi_ok, G + 1)
                    pe.wait_ge(qm_ok, G + 1)
                    pe.wait_ge(klo_ok, G + 1)
                at_least(pe, exp_ok, T - 1)
                bank = S2[t % 2]
                q_high = qm_hi[par][rows64, c, b].rearrange("p h t -> p (h t)")
                q_low = qm_lo[par][rows64, c, b].rearrange("p h t -> p (h t)")
                pe.matmul(bank[:], k_hi[par][rows64, c, tok], q_high, start=True, stop=False)
                pe.matmul(bank[:], k_hi[par][rows64, c, tok], q_low, start=False, stop=False)
                pe.matmul(bank[:], k_lo[par][rows64, c, tok], q_high, start=False, stop=False)
                pe.wait_ge(max_ok, T + 1)
                for v in range(QH):
                    part = bank[:, v * P:(v + 1) * P]
                    if cross:
                        pe.matmul(part, ident_b[:], add_maskT[:], start=False, stop=False)
                    last = pe.matmul(part, row_max[:, t % 4, v:v + 1].to_broadcast([P, P]), neg_ident_b[:],
                                     start=False, stop=v == QH - 1)
                last.then_inc(s2_full, 1)

            def av_step(G, t, parity):
                T = G * STEPS + t
                b, c, u, before = place(t)
                par = 1 - parity if before else parity
                if t == 0:
                    pe.wait_ge(v_free, G + 1)
                if t % NQ == 0:
                    at_least(pe, o32_ok, G * PAIR + t // NQ - 1)
                pe.wait_ge(exp_ok, T + 1)
                for v in range(QH):
                    pe.matmul(AV[b][32 * v:32 * v + 32, c * P:(c + 1) * P], v_pad[par][:, b, c * 8 + u * QH + v, :],
                              probs[:, t % 4, v * P:(v + 1) * P], start=(t % NQ == 0), stop=False)
                for v in range(QH):
                    last = pe.matmul(AV[b][32 * v:32 * v + 32, D + c * P:D + (c + 1) * P], consts["half_ones"][:, u, :],
                                     probs[:, t % 4, v * P:(v + 1) * P], start=False, stop=(t % NQ == NQ - 1))
                last.then_inc(av_full, 1)

            def project(bank, cols, hi, lo):
                for m in range(KC):
                    wcol = slice(cols.start + m * P, cols.start + (m + 1) * P)
                    last = three_pass(pe, bank[:, m * TOK:(m + 1) * TOK], lambda k: w_hi[:, k, wcol],
                                      lambda k: w_lo[:, k, wcol], lambda k: hi[:, k, :], lambda k: lo[:, k, :], KC)
                return last

            def group(G, parity):
                w = G + 1
                for t in range(STEPS):
                    if has_step(G, t):
                        s1_step(G, t, parity)
                    if has_step(G, t - 2):
                        s2_step(G, t - 2, parity)
                    if has_step(G, t - 4):
                        av_step(G, t - 4, parity)
                    if has_window(G) and t == 1:
                        pe.wait_ge(xn_ok, w + 1)
                        at_least(pe, out_free, w - 2)
                        at_least(pe, k_free, w)
                        for c in range(KC):
                            for b in range(PAIR):
                                last = pe.transpose(FA[:, c * TOK + b * P:c * TOK + (b + 1) * P],
                                                    xn[:, b, c * P:(c + 1) * P], ident[:])
                        last.then_inc(pt_full, 1)
                        at_least(pe, v_free, w)
                        if cross:
                            pe.wait_ge(cx_in[1 - parity], 16 * ((w // 2) + 1) if isinstance(w, int) else cx_count(w, 1 - parity))
                            for c in range(KC):
                                for b in range(PAIR):
                                    last = pe.transpose(FB[:, c * TOK + b * P:c * TOK + (b + 1) * P],
                                                        cx[1 - parity][:, b, c * P:(c + 1) * P], ident[:])
                            last.then_inc(ctx_full, 1)
                    if has_window(G) and t == 3:
                        pe.wait_ge(pt_lo, w + 1)
                        if cross:
                            pe.wait_ge(ctx_lo, w + 1)
                        project(FB, WQ, xT_hi, xT_lo).then_inc(q_full, 1)
                    if has_window(G) and t == 4:
                        project(FA, WK, kvT_hi, kvT_lo).then_inc(k_full, 1)
                    if has_window(G) and t == 5:
                        pe.wait_ge(q_free, w + 1)
                        for b in range(PAIR):
                            tok = slice(b * P, (b + 1) * P)
                            last = three_pass(pe, FB[:, b * D:(b + 1) * D], lambda k: kvT_hi[:, k, tok],
                                              lambda k: kvT_lo[:, k, tok], lambda k: w_hi[:, k, WV],
                                              lambda k: w_lo[:, k, WV], KC)
                        last.then_inc(v_full, 1)
                    if t == 6 and whole(G - 1):
                        pe.wait_ge(olo_ok, G * PAIR)
                        if has_window(G):
                            pe.wait_ge(k_free, w + 1)
                        else:
                            pe.wait_ge(k_free, NG)
                            pe.wait_ge(out_free, G - 1)
                        for b in range(PAIR):
                            last = three_pass(pe, FA[:, b * D:(b + 1) * D], lambda k: o_hi[:, b, k, :],
                                              lambda k: o_lo[:, b, k, :], lambda k: w_hi[:, k, WO],
                                              lambda k: w_lo[:, k, WO], KC)
                        last.then_inc(out_full, 1)
            schedule(pe, group)
    nm.clear_semaphores()
    nm_ctx.close()


class Normed:

    def __init__(self, nm, consts, x_res, bank, x_in=None, n_x=0):
        self.x_res, self.ident, self.minus_half, self.eps, self.bank = x_res, consts["ident"], consts["minus_half"], consts["ln_eps"], bank
        self.mark = nm.sb("ln_mark", [P, 1])
        self.x_in, self.n_x = x_in, n_x
        self.stats, self.moments = nm.sb("stats", [P, PAIR, 6]), nm.sb("moments", [P, PAIR, 2])
        self.var_eps, self.rstd = nm.sb("var_eps", [P, PAIR]), nm.sb("rstd", [P, PAIR])
        self.xn = nm.sb("xn", [P, PAIR, D])
        self.hi = [nm.sb(f"xT_hi{i}", [P, KC, TOK], F32R) for i in range(2)]
        self.lo = [nm.sb(f"xT_lo{i}", [P, KC, TOK], F32R) for i in range(2)]
        self.ln_link, self.var_ok, self.rstd_ok, self.xn_ok = (nm.sem(n) for n in ("ln_link", "var_ok", "rstd_ok", "xn_ok"))
        self.full, self.hi_ok, self.lo_ok = (nm.sem(n) for n in ("pt_full", "pt_hi", "pt_lo"))

    def x(self, w, b):
        return self.x_res[:, w * PAIR + b, :] if isinstance(w, int) else \
            self.x_res[:, bass.ds(w * PAIR + b, 1), :].rearrange("p b d -> p (b d)")

    def x_group(self, w):
        return self.x_res[:, w * PAIR:(w + 1) * PAIR, :] if isinstance(w, int) else \
            self.x_res[:, bass.ds(w * PAIR, PAIR), :]

    def dve_moments(self, dve, w):
        if self.x_in is not None and isinstance(w, int):
            dve.wait_ge(self.x_in, self.n_x)
        for b in range(PAIR):
            dve.bn_stats(self.stats[:, b, :], self.x(w, b)).then_inc(self.ln_link, 1)
        wait_apart(dve, self.ln_link, w * LN_LINKS + PAIR, self.mark)
        for b in range(PAIR):
            dve.bn_aggr(self.moments[:, b, :], self.stats[:, b, :]).then_inc(self.ln_link, 1)

    def dve_normalise(self, dve, w):
        dve.wait_ge(self.rstd_ok, w + 1)
        at_least(dve, self.full, w)
        for b in range(PAIR):
            last = dve.tensor_scalar(self.xn[:, b, :], self.x(w, b), self.moments[:, b, 0:1], self.rstd[:, b:b + 1],
                                     ALU.subtract, ALU.mult)
        last.then_inc(self.xn_ok, 1)

    def pool_rstd(self, pool, w):
        pool.wait_ge(self.ln_link, (w + 1) * LN_LINKS)
        at_least(pool, self.xn_ok, w)
        pool.tensor_tensor(self.var_eps[:], self.moments[:, :, 1], self.eps[:], ALU.add).then_inc(self.var_ok, 1)
        pool.wait_ge(self.var_ok, w + 1)
        pool.tensor_tensor(self.rstd[:], self.var_eps[:], self.minus_half[:], ALU.pow).then_inc(self.rstd_ok, 1)

    def pe_transpose(self, pe, w):
        pe.wait_ge(self.xn_ok, w + 1)
        at_least(pe, self.lo_ok, w)
        for c in range(KC):
            for b in range(PAIR):
                last = pe.transpose(self.bank[:, c * TOK + b * P:c * TOK + (b + 1) * P],
                                    self.xn[:, b, c * P:(c + 1) * P], self.ident[:])
        last.then_inc(self.full, 1)

    def act_high(self, act, w, parity, used, per_group=1):
        act.wait_ge(self.full, w + 1)
        at_least(act, used, (w - 1) * per_group)
        act.activation(self.hi[parity][:], chunked(self.bank), ACT.Copy).then_inc(self.hi_ok, 1)

    def dve_low(self, dve, w, parity):
        dve.wait_ge(self.hi_ok, w + 1)
        dve.tensor_tensor(self.lo[parity][:], chunked(self.bank), f32(self.hi[parity][:]),
                          ALU.subtract).then_inc(self.lo_ok, 1)


def chunked(bank):
    return bank[:].rearrange("p (c t) -> p c t", c=KC)


def windows(eng, window, last=NG):
    for w in range(-2, 3):
        window(w, w % 2)
    with eng.Fori(1, (NG - 4) // 2) as i:
        window(i * 2 + 1, 1)
        window(i * 2 + 2, 0)
    for w in range(NG - 3, last + 1):
        window(w, w % 2)


def in_stage(w):
    return not isinstance(w, int) or 0 <= w < NG


def entangled_stage(nc, name, x_res, consts, a, x_dram=None):
    with ExitStack() as ctx:
        nm = Names(nc, ctx, name)
        sb, sem = nm.sb, nm.sem
        PT, PC, ENT, VT, VTOK, SC, PP, OUT = (nm.ps(n) for n in ("PT", "PC", "ENT", "VT", "VTOK", "SC", "PP", "OUT"))
        x_in = sem("x_in")
        ln = Normed(nm, consts, x_res, PT, x_in if x_dram is not None else None, 16)
        w_raw = sb("w_raw", [P, KC, 5 * D])
        fold = sb("fold", [P, KC, 3 * D])
        w_hi, w_lo = sb("w_hi", [P, KC, 3 * D], F32R), sb("w_lo", [P, KC, 3 * D], F32R)
        bias_in = sb("bias_in", [P, 4 * KC])
        bias_e = sb("bias_e", [P, KC])
        cx = [sb(f"cx{i}", [P, PAIR, D]) for i in range(2)]
        cT_hi = [sb(f"cT_hi{i}", [P, KC, TOK], F32R) for i in range(2)]
        cT_lo = [sb(f"cT_lo{i}", [P, KC, TOK], F32R) for i in range(2)]
        ent, vT = sb("ent", [P, KC, TOK]), sb("vT", [P, KC, TOK])
        v_tok = sb("v_tok", [P, PAIR, D])
        top, shift = sb("top", [P, PAIR]), sb("shift", [P, PAIR])
        probs, probsT = sb("probs", [P, PAIR, P]), sb("probsT", [P, PAIR, P])
        total, inv_total = sb("total", [P, PAIR]), sb("inv_total", [P, PAIR])
        w_in, folded, fold_ok, hi_ok, w_ok = (sem(n) for n in ("w_in", "folded", "fold_ok", "hi_ok", "w_ok"))
        cx_in = [sem(f"cx_in{i}") for i in range(2)]
        pc_full, pc_hi, pc_lo = sem("pc_full"), sem("pc_hi"), sem("pc_lo")
        ent_full, ent_ok, vt_full, vt_ok = sem("ent_full"), sem("ent_ok"), sem("vt_full"), sem("vt_ok")
        vtok_full, vtok_ok, sc_full, top_ok, shift_ok = (sem(n) for n in ("vtok_full", "vtok_ok", "sc_full", "top_ok", "shift_ok"))
        exp_ok, inv_ok, pp_full, pp_ok, out_full, out_ok = (sem(n) for n in ("exp_ok", "inv_ok", "pp_full", "pp_ok", "out_full", "out_ok"))

        with nc.Block() as block:

            @block.sync
            def _(sp):
                if x_dram is not None:
                    sp.dma_start(x_res[:], x_dram).then_inc(x_in, 16)
                for n, k in enumerate(("L0_xattn_Wq", "L0_xattn_Wk", "L0_xattn_Weq", "L0_xattn_Wek", "L0_xattn_Wv")):
                    sp.dma_start(w_raw[:, :, n * D:(n + 1) * D], a[k]).then_inc(w_in, 16)
                sp.dma_start(bias_in[:], a["L0_xattn_b"]).then_inc(w_in, 16)

                def load_ctx(w, parity):
                    at_least(sp, pc_full, w - 1)
                    src = a["ctx"][:, w * PAIR:(w + 1) * PAIR, :] if isinstance(w, int) else \
                        a["ctx"][:, bass.ds(w * PAIR, PAIR), :]
                    sp.dma_start(cx[parity][:], src).then_inc(cx_in[parity], 16)
                load_ctx(0, 0)
                load_ctx(1, 1)
                with sp.Fori(1, NG // 2) as i:
                    load_ctx(i * 2, 0)
                    load_ctx(i * 2 + 1, 1)

            @block.gpsimd
            def _(pool):
                ln.pool_rstd(pool, 0)
                with pool.Fori(1, NG) as w:
                    ln.pool_rstd(pool, w)

            @block.scalar
            def _(act):
                act.wait_ge(folded, 1)
                for n, bank in enumerate((ENT, VT)):
                    act.activation(fold[:, :, n * D:(n + 1) * D], chunked(bank), ACT.Copy)
                act.wait_ge(w_in, 16 * 6)
                act.activation(fold[:, :, 2 * D:], w_raw[:, :, 4 * D:], ACT.Copy).then_inc(fold_ok, 1)
                act.wait_ge(fold_ok, 2)
                act.activation(w_hi[:], fold[:], ACT.Copy).then_inc(hi_ok, 1)

                def window(w, parity):
                    if in_stage(w - 1):
                        for b in range(PAIR):
                            act.wait_ge(shift_ok, w)
                            if b == 0:
                                at_least(act, pp_full, w - 1)
                            last = act.activation(probs[:, b, :], SC[:, b * P:(b + 1) * P], ACT.Exp, bias=shift[:, b:b + 1],
                                                  scale=D ** -0.5, accum_out=total[:, b:b + 1])
                        last.then_inc(exp_ok, 1)
                    if in_stage(w + 1):
                        ln.act_high(act, w + 1, 1 - parity, vt_full)
                        act.wait_ge(pc_full, w + 2)
                        act.activation(cT_hi[1 - parity][:], chunked(PC), ACT.Copy).then_inc(pc_hi, 1)
                    if in_stage(w):
                        act.wait_ge(ent_full, w + 1)
                        at_least(act, sc_full, w)
                        for m in range(KC):
                            last = act.activation(ent[:, m, :], ENT[:, m * TOK:(m + 1) * TOK], ACT.Tanh, bias=bias_e[:, m:m + 1])
                        last.then_inc(ent_ok, 1)
                        act.wait_ge(vt_full, w + 1)
                        for m in range(KC):
                            last = act.activation(vT[:, m, :], VT[:, m * TOK:(m + 1) * TOK], ACT.Identity,
                                                  bias=bias_in[:, 3 * KC + m:3 * KC + m + 1])
                        last.then_inc(vt_ok, 1)
                    if in_stage(w - 1):
                        act.wait_ge(pp_full, w)
                        at_least(act, out_full, w - 1)
                        act.activation(probsT[:].rearrange("p b t -> p (b t)"), PP[:, 0:TOK], ACT.Copy).then_inc(pp_ok, 1)
                    if in_stage(w):
                        act.wait_ge(vtok_full, w + 1)
                        at_least(act, out_full, w)
                        act.activation(v_tok[:].rearrange("p b d -> p (b d)"), VTOK[:], ACT.Copy).then_inc(vtok_ok, 1)
                windows(act, window)

            @block.vector
            def _(dve):
                dve.wait_ge(folded, 1)
                dve.wait_ge(w_in, 16 * 6)
                dve.tensor_tensor(bias_e[:], bias_in[:, 2 * KC:3 * KC], OUT[:, 0:KC], ALU.add).then_inc(fold_ok, 1)
                dve.wait_ge(hi_ok, 1)
                dve.tensor_tensor(w_lo[:], fold[:], f32(w_hi[:]), ALU.subtract).then_inc(w_ok, 1)

                def window(w, parity):
                    if in_stage(w - 1):
                        dve.wait_ge(sc_full, w)
                        at_least(dve, exp_ok, w - 1)
                        dve.tensor_reduce(top[:], SC[:, 0:TOK].rearrange("p (b t) -> p b t", b=PAIR), AXX, ALU.max).then_inc(top_ok, 1)
                        dve.wait_ge(top_ok, w)
                        dve.tensor_scalar(shift[:], top[:], -(D ** -0.5), None, ALU.mult).then_inc(shift_ok, 1)
                    if in_stage(w + 2):
                        ln.dve_moments(dve, w + 2)
                    if in_stage(w + 1):
                        ln.dve_low(dve, w + 1, 1 - parity)
                        dve.wait_ge(pc_hi, w + 2)
                        dve.tensor_tensor(cT_lo[1 - parity][:], chunked(PC), f32(cT_hi[1 - parity][:]), ALU.subtract).then_inc(pc_lo, 1)
                    if in_stage(w + 2):
                        ln.dve_normalise(dve, w + 2)
                    if in_stage(w - 1):
                        dve.wait_ge(exp_ok, w)
                        dve.reciprocal(inv_total[:], total[:]).then_inc(inv_ok, 1)
                        dve.wait_ge(inv_ok, w)
                        dve.wait_ge(out_full, w)
                        for b in range(PAIR):
                            last = dve.scalar_tensor_tensor(ln.x(w - 1, b), OUT[:, b * D:(b + 1) * D], inv_total[:, b:b + 1],
                                                            ln.x(w - 1, b), op0=ALU.mult, op1=ALU.add)
                        last.then_inc(out_ok, 1)
                windows(dve, window)

            @block.tensor
            def _(pe):
                pe.wait_ge(w_in, 16 * 6)
                for n, bank in enumerate((ENT, VT)):
                    for m in range(KC):
                        for k in range(KC):
                            pe.matmul(bank[:, m * D:(m + 1) * D], w_raw[:, k, n * D + m * P:n * D + (m + 1) * P],
                                      w_raw[:, k, (2 + n) * D:(3 + n) * D], start=(k == 0), stop=(k == KC - 1))
                for m in range(KC):
                    for j in range(2 * KC):
                        n, k = j // KC, j % KC
                        last = pe.matmul(OUT[:, m:m + 1], w_raw[:, k, (2 + n) * D + m * P:(2 + n) * D + (m + 1) * P],
                                         bias_in[:, n * KC + k:n * KC + k + 1], start=(j == 0), stop=(j == 2 * KC - 1))
                last.then_inc(folded, 1)
                pe.wait_ge(w_ok, 1)

                def window(w, parity):
                    if in_stage(w - 1):
                        pe.wait_ge(vt_ok, w)
                        at_least(pe, exp_ok, w - 1)
                        for b in range(PAIR):
                            for k in range(KC):
                                last = pe.matmul(SC[:, b * P:(b + 1) * P], ent[:, k, b * P:(b + 1) * P],
                                                 vT[:, k, b * P:(b + 1) * P], start=(k == 0), stop=(k == KC - 1))
                        last.then_inc(sc_full, 1)
                    if in_stage(w + 1):
                        ln.pe_transpose(pe, w + 1)
                        pe.wait_ge(cx_in[1 - parity], 16 * ((w + 1) // 2 + 1) if isinstance(w, int) else cx_count(w + 1, 1 - parity))
                        at_least(pe, pc_lo, w + 1)
                        for c in range(KC):
                            for b in range(PAIR):
                                last = pe.transpose(PC[:, c * TOK + b * P:c * TOK + (b + 1) * P],
                                                    cx[1 - parity][:, b, c * P:(c + 1) * P], consts["ident"][:])
                        last.then_inc(pc_full, 1)
                    if in_stage(w):
                        hi, lo, chi, clo = ln.hi[parity], ln.lo[parity], cT_hi[parity], cT_lo[parity]
                        pe.wait_ge(ln.lo_ok, w + 1)
                        pe.wait_ge(pc_lo, w + 1)
                        at_least(pe, ent_ok, w)
                        for m in range(KC):
                            eq, ek = slice(m * P, (m + 1) * P), slice(D + m * P, D + (m + 1) * P)
                            last = three_pass(pe, ENT[:, m * TOK:(m + 1) * TOK],
                                              lambda k: w_hi[:, k, eq] if k < KC else w_hi[:, k - KC, ek],
                                              lambda k: w_lo[:, k, eq] if k < KC else w_lo[:, k - KC, ek],
                                              lambda k: hi[:, k, :] if k < KC else chi[:, k - KC, :],
                                              lambda k: lo[:, k, :] if k < KC else clo[:, k - KC, :], 2 * KC)
                        last.then_inc(ent_full, 1)
                        at_least(pe, vt_ok, w)
                        for m in range(KC):
                            ev = slice(2 * D + m * P, 2 * D + (m + 1) * P)
                            last = three_pass(pe, VT[:, m * TOK:(m + 1) * TOK], lambda k: w_hi[:, k, ev], lambda k: w_lo[:, k, ev],
                                              lambda k: chi[:, k, :], lambda k: clo[:, k, :], KC)
                        last.then_inc(vt_full, 1)
                    if in_stage(w - 1):
                        pe.wait_ge(exp_ok, w)
                        at_least(pe, pp_ok, w - 1)
                        for b in range(PAIR):
                            last = pe.transpose(PP[:, b * P:(b + 1) * P], probs[:, b, :], consts["ident"][:])
                        last.then_inc(pp_full, 1)
                    if in_stage(w - 1):
                        pe.wait_ge(pp_ok, w)
                        pe.wait_ge(vtok_ok, w)
                        at_least(pe, out_ok, w - 1)
                        for b in range(PAIR):
                            last = pe.matmul(OUT[:, b * D:(b + 1) * D], probsT[:, b, :], v_tok[:, b, :], start=True, stop=True)
                        last.then_inc(out_full, 1)
                    if in_stage(w):
                        pe.wait_ge(vt_ok, w + 1)
                        at_least(pe, vtok_ok, w)
                        for b in range(PAIR):
                            for c in range(KC):
                                last = pe.transpose(VTOK[:, b * D + c * P:b * D + (c + 1) * P],
                                                    vT[:, c, b * P:(b + 1) * P], consts["ident"][:])
                        last.then_inc(vtok_full, 1)
                windows(pe, window)
        nm.clear_semaphores()


def routed_stage(nc, name, x_res, consts, a, x_dram=None):
    FC = F // P
    ER = E * R
    GA = E + ER
    with ExitStack() as ctx:
        nm = Names(nc, ctx, name)
        sb, sem = nm.sb, nm.sem
        PT, RT, LT, OUT = (nm.ps(n) for n in ("PT", "RT", "LT", "OUT"))
        HB = [nm.ps(f"HB{i}") for i in range(2)]
        x_in = sem("x_in")
        ln = Normed(nm, consts, x_res, PT, x_in if x_dram is not None else None, 16)
        wi_raw, wo_raw = sb("wi_raw", [P, KC, F + GA]), sb("wo_raw", [P, FC, D])
        wi_hi, wi_lo = sb("wi_hi", [P, KC, F + GA], F32R), sb("wi_lo", [P, KC, F + GA], F32R)
        wo_hi, wo_lo = sb("wo_hi", [P, FC, D], F32R), sb("wo_lo", [P, FC, D], F32R)
        b_raw = sb("b_raw", [3 * ER, F])
        b_parts = sb("b_parts", [3 * ER, F], F32R)
        gate_row, bias_i, row_o = sb("gate_row", [P, PAIR, E]), sb("bias_i", [P, FC]), sb("row_o", [P, PAIR, D])
        expert_of = sb("expert_of", [P, ER])
        route_mark = sb("route_mark", [P, 1])
        logits, top8 = sb("logits", [P, PAIR, E]), sb("top8", [P, PAIR, 8])
        top_at, top1 = sb("top_at", [P, PAIR, 8], U32), sb("top1", [P, PAIR])
        low32, low_hi = sb("low32", [P, PAIR, ER]), sb("low_hi", [P, PAIR, ER], F32R)
        low_parts = sb("low_parts", [P, PAIR, 3 * ER])
        lowT = [sb(f"lowT{i}", [3 * ER, TOK], F32R) for i in range(2)]
        h32 = [sb(f"h32_{i}", [P, 2 * TOK]) for i in range(2)]
        h_hi = [sb(f"h_hi{i}", [P, FC // 2, 2 * TOK], F32R) for i in range(2)]
        h_lo = [sb(f"h_lo{i}", [P, FC // 2, 2 * TOK], F32R) for i in range(2)]
        w_in, hi_ok, w_ok, biased = sem("w_in"), sem("hi_ok"), sem("w_ok"), sem("biased")
        rt_full, link, low_ok, lt_full, lt_ok = (sem(n) for n in ("rt_full", "link", "low_ok", "lt_full", "lt_ok"))
        hb_full, relu_ok, hhi_ok, hlo_ok, out_full, out_ok = (sem(n) for n in ("hb_full", "relu_ok", "hhi_ok", "hlo_ok", "out_full", "out_ok"))
        N_IN = 8
        HALVES = FC // 2
        LINKS = 11

        with nc.Block() as block:

            @block.sync
            def _(sp):
                if x_dram is not None:
                    sp.dma_start(x_res[:], x_dram).then_inc(x_in, 16)
                for dst, k in ((wi_raw[:, :, 0:F], "L0_ffn_wi_W"), (wi_raw[:, :, F:], "L0_ffn_gA"), (wo_raw[:], "L0_ffn_wo_W"),
                               (b_raw[:], "L0_ffn_B"), (gate_row[:], "L0_ffn_gate_b"), (bias_i[:], "L0_ffn_wi_b"),
                               (row_o[:], "L0_ffn_wo_b"), (expert_of[:], "expert_of")):
                    sp.dma_start(dst, a[k]).then_inc(w_in, 16)

            @block.gpsimd
            def _(pool):
                pool.wait_ge(w_in, 16 * N_IN)

                def window(w):
                    ln.pool_rstd(pool, w)
                    pool.wait_ge(ln.xn_ok, w + 1)
                    pool.tensor_tensor(ln.x_group(w), ln.x_group(w), row_o[:], ALU.add).then_inc(biased, 1)
                window(0)
                with pool.Fori(1, NG) as w:
                    window(w)

            @block.scalar
            def _(act):
                act.wait_ge(w_in, 16 * N_IN)
                act.activation(b_parts[:], b_raw[:], ACT.Copy).then_inc(hi_ok, 1)
                act.activation(wi_hi[:], wi_raw[:], ACT.Copy).then_inc(hi_ok, 1)
                act.activation(wo_hi[:], wo_raw[:], ACT.Copy).then_inc(hi_ok, 1)

                def window(w, parity):
                    if in_stage(w + 1):
                        ln.act_high(act, w + 1, 1 - parity, hb_full, HALVES)
                    for n in range(HALVES):
                        if in_stage(w):
                            T = w * HALVES + n
                            act.wait_ge(hb_full, T + 1)
                            at_least(act, hlo_ok, T - 1)
                            for m in range(2):
                                f = 2 * n + m
                                last = act.activation(h32[n % 2][:, m * TOK:(m + 1) * TOK], HB[n % 2][:, m * TOK:(m + 1) * TOK],
                                                      ACT.Relu, bias=bias_i[:, f:f + 1])
                            last.then_inc(relu_ok, 1)
                            if n == 0:
                                at_least(act, out_full, w - 1)
                            act.wait_ge(relu_ok, T + 1)
                            act.activation(h_hi[parity][:, n, :], h32[n % 2][:], ACT.Copy).then_inc(hhi_ok, 1)
                    if in_stage(w + 1):
                        act.wait_ge(lt_full, w + 2)
                        at_least(act, hb_full, w * HALVES)
                        act.activation(lowT[1 - parity][:], LT[0:3 * ER, 0:TOK], ACT.Copy).then_inc(lt_ok, 1)
                windows(act, window)

            @block.vector
            def _(dve):
                dve.wait_ge(hi_ok, 3)
                dve.tensor_tensor(b_parts[ER:2 * ER, :], b_raw[ER:2 * ER, :], f32(b_parts[ER:2 * ER, :]), ALU.subtract)
                dve.tensor_tensor(wi_lo[:], wi_raw[:], f32(wi_hi[:]), ALU.subtract)
                dve.tensor_tensor(wo_lo[:], wo_raw[:], f32(wo_hi[:]), ALU.subtract).then_inc(w_ok, 1)

                def route(w):
                    done = [0]

                    def step(*instructions, apart=False):
                        for ins in instructions:
                            done[0] += 1
                            ins.then_inc(link, 1)
                        if apart:
                            wait_apart(dve, link, w * LINKS + done[0], route_mark)
                            done[0] += 1
                        else:
                            dve.wait_ge(link, w * LINKS + done[0])
                    dve.wait_ge(rt_full, w + 1)
                    rt = RT[:, 0:PAIR * GA].rearrange("p (b n) -> p b n", b=PAIR)
                    at_least(dve, lt_full, w)
                    step(dve.tensor_tensor(logits[:], rt[:, :, 0:E], gate_row[:], ALU.add), apart=True)
                    step(*(dve.max(top8[:, b, :], logits[:, b, :]) for b in range(PAIR)), apart=True)
                    step(*(dve.max_index(top_at[:, b, :], top8[:, b, :], logits[:, b, :]) for b in range(PAIR)))
                    step(dve.tensor_copy(top1[:], top_at[:, :, 0]))
                    step(*(dve.scalar_tensor_tensor(low32[:, b, :], expert_of[:], top1[:, b:b + 1], rt[:, b, E:],
                                                    op0=ALU.is_equal, op1=ALU.mult) for b in range(PAIR)))
                    step(dve.tensor_copy(low_hi[:], low32[:]))
                    dve.tensor_tensor(low_parts[:, :, 2 * ER:], low32[:], f32(low_hi[:]), ALU.subtract)
                    dve.tensor_copy(low_parts[:, :, 0:ER], f32(low_hi[:]))
                    dve.tensor_copy(low_parts[:, :, ER:2 * ER], f32(low_hi[:])).then_inc(low_ok, 1)

                def window(w, parity):
                    if in_stage(w + 1):
                        ln.dve_low(dve, w + 1, 1 - parity)
                    for n in range(HALVES):
                        if in_stage(w):
                            T = w * HALVES + n
                            dve.wait_ge(hhi_ok, T + 1)
                            dve.tensor_tensor(h_lo[parity][:, n, :], h32[n % 2][:], f32(h_hi[parity][:, n, :]),
                                              ALU.subtract).then_inc(hlo_ok, 1)
                        if n == 0 and in_stage(w + 2):
                            ln.dve_moments(dve, w + 2)
                        if n == 1 and in_stage(w + 2):
                            ln.dve_normalise(dve, w + 2)
                        if n == 2 and in_stage(w + 1):
                            route(w + 1)
                    if in_stage(w - 1):
                        dve.wait_ge(out_full, w)
                        dve.wait_ge(biased, w)
                        dve.tensor_tensor(ln.x_group(w - 1), ln.x_group(w - 1),
                                          OUT[:].rearrange("p (b d) -> p b d", b=PAIR), ALU.add).then_inc(out_ok, 1)
                windows(dve, window)

            @block.tensor
            def _(pe):
                pe.wait_ge(w_ok, 1)

                def window(w, parity):
                    if in_stage(w + 1):
                        ln.pe_transpose(pe, w + 1)
                    if in_stage(w):
                        hi, lo = ln.hi[parity], ln.lo[parity]
                        for n in range(HALVES):
                            T = w * HALVES + n
                            at_least(pe, relu_ok, T - 1)
                            if n == 0:
                                pe.wait_ge(ln.lo_ok, w + 1)
                                pe.wait_ge(lt_ok, w + 1)
                            for m in range(2):
                                out = HB[n % 2][:, m * TOK:(m + 1) * TOK]
                                fs = slice((2 * n + m) * P, (2 * n + m + 1) * P)
                                for k in range(KC):
                                    pe.matmul(out, wi_hi[:, k, fs], hi[:, k, :], start=(k == 0), stop=False)
                                    pe.matmul(out, wi_lo[:, k, fs], hi[:, k, :], start=False, stop=False)
                                    pe.matmul(out, wi_hi[:, k, fs], lo[:, k, :], start=False, stop=False)
                                last = pe.matmul(out, b_parts[:, fs], lowT[parity][:], start=False, stop=True)
                            last.then_inc(hb_full, 1)
                    if in_stage(w + 1):
                        hi, lo = ln.hi[1 - parity], ln.lo[1 - parity]
                        pe.wait_ge(ln.lo_ok, w + 2)
                        at_least(pe, low_ok, w + 1)
                        for b in range(PAIR):
                            tok = slice(b * P, (b + 1) * P)
                            last = three_pass(pe, RT[:, b * GA:(b + 1) * GA], lambda k: hi[:, k, tok], lambda k: lo[:, k, tok],
                                              lambda k: wi_hi[:, k, F:], lambda k: wi_lo[:, k, F:], KC)
                        last.then_inc(rt_full, 1)
                    if in_stage(w - 1):
                        pe.wait_ge(hlo_ok, w * HALVES)
                        at_least(pe, out_ok, w - 1)
                        h, l = h_hi[1 - parity], h_lo[1 - parity]
                        for b in range(PAIR):
                            def chunk(t, k, b=b):
                                return t[:, k // 2, (k % 2) * TOK + b * P:(k % 2) * TOK + (b + 1) * P]
                            last = three_pass(pe, OUT[:, b * D:(b + 1) * D], lambda k: chunk(h, k), lambda k: chunk(l, k),
                                              lambda k: wo_hi[:, k, :], lambda k: wo_lo[:, k, :], FC)
                        last.then_inc(out_full, 1)
                    if in_stage(w + 1):
                        pe.wait_ge(low_ok, w + 2)
                        at_least(pe, lt_ok, w + 1)
                        for b in range(PAIR):
                            last = pe.transpose(LT[0:3 * ER, b * P:(b + 1) * P], low_parts[:, b, :], consts["ident"][:])
                        last.then_inc(lt_full, 1)
                windows(pe, window)
        nm.clear_semaphores()


def ternary_stage(nc, name, x_res, consts, a, x_dram=None, out_dram=None):
    FC = F // P
    HB_COLS = 512
    HALVES = F // HB_COLS
    with ExitStack() as ctx:
        nm = Names(nc, ctx, name)
        sb, sem = nm.sb, nm.sem
        PT, OUT = nm.ps("PT"), nm.ps("OUT")
        HB = [nm.ps(f"HB{i}") for i in range(2)]
        ZT = [nm.ps(f"ZT{i}") for i in range(4)]
        x_in = sem("x_in")
        ln = Normed(nm, consts, x_res, PT, x_in if x_dram is not None else None, 16)
        raw = [sb("fc_raw", [P, KC * F]), sb("proj_raw", [P, FC * D])]
        quant = [sb("fc_q", [P, KC, F], F32R), sb("proj_q", [P, FC, D], F32R)]
        below = sb("below", [P, KC * F])
        sums, level = sb("sums", [P, 2]), sb("level", [P, 2, 2])
        gain, offset = sb("gain", [P, FC]), sb("offset", [P, FC])
        hid = [[sb(f"hid{i}{b}", [P, F]) for b in range(PAIR)] for i in range(2)]
        z = [sb(f"z{b}", [P, F]) for b in range(PAIR)]
        h_stats, h_moments = sb("h_stats", [P, PAIR, HALVES, 6]), sb("h_moments", [P, PAIR, 2])
        h_var, h_rstd = sb("h_var", [P, PAIR]), sb("h_rstd", [P, PAIR])
        y32 = [sb(f"y32_{i}", [P, 2 * TOK]) for i in range(FC // 2)]
        y_hi, y_lo = sb("y_hi", [P, FC // 2, 2 * TOK], F32R), sb("y_lo", [P, FC // 2, 2 * TOK], F32R)
        hs_mark = sb("hs_mark", [P, 1])
        w_in, sums_ok, total_ok, level_ok, below_ok, quant_ok = (
            sem(n) for n in ("w_in", "sums_ok", "total_ok", "level_ok", "below_ok", "quant_ok"))
        hb_full, gelu_ok, hs_link, hvar_ok, hrstd_ok, z_ok = (
            sem(n) for n in ("hb_full", "gelu_ok", "hs_link", "hvar_ok", "hrstd_ok", "z_ok"))
        zt_full, y_ok, yhi_ok, out_full, out_ok, stored = (sem(n) for n in ("zt_full", "y_ok", "yhi_ok", "out_full", "out_ok", "stored"))
        ylo_ok = [sem("ylo_first_ok"), sem("ylo_last_ok")]
        N_IN = 4
        PARTS = FC // 2
        FILLS = PAIR * HALVES
        LINKS = FILLS + 1 + PAIR

        def low_part(eng, w, n):
            eng.wait_ge(yhi_ok, w * PARTS + n + 1)
            eng.tensor_tensor(y_lo[:, n, :], y32[n][:], f32(y_hi[:, n, :]), ALU.subtract).then_inc(ylo_ok[n // 2], 1)

        with nc.Block() as block:

            @block.sync
            def _(sp):
                if x_dram is not None:
                    sp.dma_start(x_res[:], x_dram).then_inc(x_in, 16)
                for dst, k in ((raw[0], "L1_ffn_W_fc"), (raw[1], "L1_ffn_W_proj"), (gain, "L1_ffn_ln_w"), (offset, "L1_ffn_ln_b")):
                    sp.dma_start(dst[:], a[k]).then_inc(w_in, 16)

                def store(w):
                    sp.wait_ge(out_ok, w + 1)
                    dst = out_dram[:, w * PAIR:(w + 1) * PAIR, :] if isinstance(w, int) else \
                        out_dram[:, bass.ds(w * PAIR, PAIR), :]
                    sp.dma_start(dst, ln.x_group(w)).then_inc(stored, 16)
                with sp.Fori(0, NG) as w:
                    store(w)
                sp.wait_ge(stored, 16 * NG)

            @block.gpsimd
            def _(pool):
                def window(w, parity):
                    if in_stage(w + 2):
                        ln.pool_rstd(pool, w + 2)
                    if in_stage(w - 1):
                        low_part(pool, w - 1, 0)
                    if in_stage(w - 1):
                        low_part(pool, w - 1, 1)
                    if in_stage(w):
                        pool.wait_ge(hs_link, w * LINKS + LINKS)
                        at_least(pool, z_ok, w * PAIR)
                        pool.tensor_tensor(h_var[:], h_moments[:, :, 1], consts["ln_eps"][:], ALU.add).then_inc(hvar_ok, 1)
                        pool.wait_ge(hvar_ok, w + 1)
                        pool.tensor_tensor(h_rstd[:], h_var[:], consts["minus_half"][:], ALU.pow).then_inc(hrstd_ok, 1)
                windows(pool, window)

            @block.scalar
            def _(act):
                act.wait_ge(w_in, 16 * N_IN)
                for n in range(2):
                    last = act.activation(quant[n][:].rearrange("p k n -> p (k n)"), raw[n][:], ACT.Abs, accum_out=sums[:, n:n + 1])
                last.then_inc(sums_ok, 1)

                def activate(w, n, parity):
                    at_least(act, z_ok, (w - 1) * PAIR)
                    act.wait_ge(hb_full, w * FILLS + n + 1)
                    act.activation(hid[parity][n // HALVES][:, (n % HALVES) * HB_COLS:(n % HALVES + 1) * HB_COLS],
                                   HB[n % 2][:], ACT.Gelu).then_inc(gelu_ok, 1)

                def rescale(w, n):
                    T = w * PARTS + n
                    act.wait_ge(zt_full, T + 1)
                    at_least(act, ylo_ok[n // 2], (w - 1) * 2 + n % 2 + 1)
                    for m in range(2):
                        f = 2 * n + m
                        last = act.activation(y32[n][:, m * TOK:(m + 1) * TOK], ZT[n][:, m * TOK:(m + 1) * TOK],
                                              ACT.Identity, bias=offset[:, f:f + 1], scale=gain[:, f:f + 1])
                    last.then_inc(y_ok, 1)
                    if n == 0:
                        at_least(act, out_full, w)
                    act.wait_ge(y_ok, T + 1)
                    act.activation(y_hi[:, n, :], y32[n][:], ACT.Copy).then_inc(yhi_ok, 1)

                def window(w, parity):
                    if in_stage(w + 1):
                        ln.act_high(act, w + 1, 1 - parity, hb_full, FILLS)
                    if in_stage(w):
                        activate(w, 0, parity)
                    for n in range(PARTS):
                        if in_stage(w) and n + 1 < FILLS:
                            activate(w, n + 1, parity)
                        if in_stage(w - 1):
                            rescale(w - 1, n)
                windows(act, window)

            @block.vector
            def _(dve):
                dve.wait_ge(total_ok, 1)
                for n in range(2):
                    dve.tensor_scalar(level[:, n, 0:1], OUT[:, n:n + 1], 1.0 / (F * D), ABSMEAN_EPS, ALU.mult, ALU.add).then_inc(level_ok, 1)
                for n in range(2):
                    dve.wait_ge(level_ok, 2 + 2 * n)
                    dve.tensor_scalar(level[:, n, 1:2], level[:, n, 0:1], -0.5, None, ALU.mult).then_inc(level_ok, 1)
                    dve.wait_ge(level_ok, 3 + 2 * n)
                    dve.tensor_scalar(level[:, n, 0:1], level[:, n, 0:1], 0.5, None, ALU.mult).then_inc(level_ok, 1)
                dve.wait_ge(level_ok, 6)
                for n in range(2):
                    at_least(dve, quant_ok, n)
                    dve.tensor_scalar(below[:], raw[n][:], level[:, n, 1:2], None, ALU.is_lt).then_inc(below_ok, 1)
                    dve.wait_ge(below_ok, n + 1)
                    dve.scalar_tensor_tensor(quant[n][:].rearrange("p k n -> p (k n)"), raw[n][:], level[:, n, 0:1], below[:],
                                             op0=ALU.is_gt, op1=ALU.subtract).then_inc(quant_ok, 1)

                def spread(w, n, parity):
                    dve.wait_ge(gelu_ok, w * FILLS + n + 1)
                    b, half = n // HALVES, n % HALVES
                    dve.bn_stats(h_stats[:, b, half, :], hid[parity][b][:, half * HB_COLS:(half + 1) * HB_COLS]).then_inc(hs_link, 1)

                def window(w, parity):
                    if in_stage(w - 1):
                        dve.wait_ge(hrstd_ok, w)
                        at_least(dve, zt_full, (w - 1) * PARTS)
                        for b in range(PAIR):
                            dve.tensor_scalar(z[b][:], hid[1 - parity][b][:], h_moments[:, b, 0:1], h_rstd[:, b:b + 1],
                                              ALU.subtract, ALU.mult).then_inc(z_ok, 1)
                    if in_stage(w + 1):
                        ln.dve_low(dve, w + 1, 1 - parity)
                    if in_stage(w):
                        spread(w, 0, parity)
                        spread(w, 1, parity)
                    if in_stage(w + 2):
                        ln.dve_moments(dve, w + 2)
                    if in_stage(w - 2):
                        dve.wait_ge(out_full, w - 1)
                        dve.tensor_tensor(ln.x_group(w - 2), ln.x_group(w - 2),
                                          OUT[:].rearrange("p (b d) -> p b d", b=PAIR), ALU.add).then_inc(out_ok, 1)
                    if in_stage(w + 2):
                        ln.dve_normalise(dve, w + 2)
                    if in_stage(w):
                        spread(w, 2, parity)
                        spread(w, 3, parity)
                        wait_apart(dve, hs_link, w * LINKS + FILLS, hs_mark)
                        for b in range(PAIR):
                            dve.bn_aggr(h_moments[:, b, :], h_stats[:, b].rearrange("p h s -> p (h s)")).then_inc(hs_link, 1)
                    if in_stage(w - 1):
                        low_part(dve, w - 1, 2)
                    if in_stage(w - 1):
                        low_part(dve, w - 1, 3)
                windows(dve, window, NG + 1)

            @block.tensor
            def _(pe):
                pe.wait_ge(sums_ok, 1)
                pe.matmul(OUT[:, 0:2], consts["ones"][:], sums[:], start=True, stop=True).then_inc(total_ok, 1)
                pe.wait_ge(quant_ok, 2)

                def expand(w, n, parity):
                    at_least(pe, gelu_ok, w * FILLS + n - 1)
                    tok = slice((n // HALVES) * P, (n // HALVES + 1) * P)
                    cols = slice((n % HALVES) * HB_COLS, (n % HALVES + 1) * HB_COLS)
                    for k in range(KC):
                        pe.matmul(HB[n % 2][:], ln.hi[parity][:, k, tok], quant[0][:, k, cols], start=(k == 0), stop=False)
                        last = pe.matmul(HB[n % 2][:], ln.lo[parity][:, k, tok], quant[0][:, k, cols], start=False, stop=(k == KC - 1))
                    last.then_inc(hb_full, 1)

                def turn(w, n):
                    at_least(pe, y_ok, (w - 1) * PARTS + n + 1)
                    for m in range(2):
                        for b in range(PAIR):
                            f = 2 * n + m
                            last = pe.transpose(ZT[n][:, m * TOK + b * P:m * TOK + (b + 1) * P], z[b][:, f * P:(f + 1) * P],
                                                consts["ident"][:])
                    last.then_inc(zt_full, 1)

                def window(w, parity):
                    if in_stage(w + 1):
                        ln.pe_transpose(pe, w + 1)
                    if in_stage(w):
                        pe.wait_ge(ln.lo_ok, w + 1)
                        expand(w, 0, parity)
                        expand(w, 1, parity)
                    if in_stage(w - 2):
                        at_least(pe, out_ok, w - 2)
                        for k in range(FC):
                            part = k // 2
                            if k % 2 == 0:
                                pe.wait_ge(yhi_ok, (w - 2) * PARTS + part + 1)
                                pe.wait_ge(ylo_ok[part // 2], (w - 2) * 2 + part % 2 + 1)
                            for b in range(PAIR):
                                cols = slice((k % 2) * TOK + b * P, (k % 2) * TOK + (b + 1) * P)
                                for y in (y_hi, y_lo):
                                    last = pe.matmul(OUT[:, b * D:(b + 1) * D], y[:, part, cols], quant[1][:, k, :],
                                                     start=(k == 0 and b == 0 and y is y_hi), stop=(k == FC - 1 and b == PAIR - 1 and y is y_lo))
                        last.then_inc(out_full, 1)
                    if in_stage(w - 1):
                        pe.wait_ge(z_ok, w * PAIR)
                    for n in range(PARTS):
                        if in_stage(w) and 0 < n < FILLS - 1:
                            expand(w, n + 1, parity)
                        if in_stage(w - 1):
                            turn(w - 1, n)
                windows(pe, window, NG + 1)
        nm.clear_semaphores()


def decoder(nc, a, out, stages=6, only=None):
    def wanted(n):
        return (n in only if isinstance(only, tuple) else n == only) if only is not None else n <= stages

    def x_of(n):
        return a["x"] if n == (only[0] if isinstance(only, tuple) else only or 1) else None

    with ExitStack() as ctx:
        nm = Names(nc, ctx, "all")
        x_res = nm.sb("x_res", [P, NB, D])
        consts = {
            "ident": nm.sb("ident", [P, P]), "head_mask": nm.sb("head_mask", [P, QH]),
            "half_ones": nm.sb("half_ones", [P, 2, 2 * DH]), "turn_sign": nm.sb("turn_sign", [P, 1]),
            "ones": nm.sb("ones", [P, P]), "minus_half": nm.sb("minus_half", [P, PAIR]),
            "ln_eps": nm.sb("ln_eps", [P, PAIR]),
            "ident_b": nm.sb("ident_b", [P, P], BF16), "neg_ident_b": nm.sb("neg_ident_b", [P, P], BF16),
        }
        consts_in = nm.sem("consts_in")
        with nc.Block() as block:

            @block.sync
            def _(sp):
                for k in ("ident", "head_mask", "half_ones", "turn_sign"):
                    sp.dma_start(consts[k][:], a[k]).then_inc(consts_in, 16)

            @block.vector
            def _(dve):
                dve.memset(consts["minus_half"][:], -0.5)
                dve.memset(consts["ln_eps"][:], LN_EPS)
                dve.memset(consts["ones"][:], 1.0)
                dve.wait_ge(consts_in, 64)
                dve.tensor_copy(consts["ident_b"][:], consts["ident"][:])
                dve.tensor_scalar(consts["neg_ident_b"][:], consts["ident"][:], -1.0, None, ALU.mult)

        if wanted(1):
            attention_stage(nc, "a0", x_res, consts,
                            w_dram=[(0, a["L0_attn_Wqkv"]), (3, a["L0_attn_Wout"])],
                            rows=[("bias_cols", a["L0_attn_bqk"]), ("row_v", a["L0_attn_bv"]), ("row_o", a["L0_attn_bout"]),
                                  ("q_mul", a["emb"]), ("w_turned", a["L0_attn_Wturned"]), ("bias_turned", a["L0_attn_bturned"])],
                            rope=True, v_bias=True, o_bias=True, x_dram=x_of(1))
        if wanted(2):
            entangled_stage(nc, "b0", x_res, consts, a, x_dram=x_of(2))
        if wanted(3):
            routed_stage(nc, "c0", x_res, consts, a, x_dram=x_of(3))
        if wanted(4):
            attention_stage(nc, "a1", x_res, consts,
                            w_dram=[(0, a["L1_attn_W_query"]), (1, a["L1_attn_W_key"]), (2, a["L1_attn_W_val"]),
                                    (3, a["L1_attn_W_out"])], rows=[], x_dram=x_of(4))
        if wanted(5):
            attention_stage(nc, "a2", x_res, consts,
                            w_dram=[(0, a["L1_xattn_wq"]), (1, a["L1_xattn_wk"]), (2, a["L1_xattn_wv"]), (3, a["L1_xattn_wo"])],
                            rows=[("bias_cols", a["L1_xattn_bqk"]), ("row_v", a["L1_xattn_bv"]),
                                  ("row_o", a["L1_xattn_bo"]), ("mask", a["mask"])],
                            ctx_dram=a["ctx"], k_bias=True, v_bias=True, o_bias=True, x_dram=x_of(5))
        if wanted(6):
            ternary_stage(nc, "d1", x_res, consts, a, x_dram=x_of(6), out_dram=out)
            return
        stored = nm.sem("stored")
        with nc.Block() as block:

            @block.sync
            def _(sp):
                for n in range(4):
                    part = slice(n * NB // 4, (n + 1) * NB // 4)
                    sp.dma_start(out[:, part, :], x_res[:, part, :]).then_inc(stored, 16)
                sp.wait_ge(stored, 64)


def layout(inputs):
    g = {k: np.asarray(v) for k, v in inputs.items()}

    def chunks(w):
        return w.reshape(-1, P, w.shape[1]).transpose(1, 0, 2)

    def cols(*bs):
        return np.concatenate([b.reshape(-1, P).T for b in bs], axis=1)

    def row(b, n=PAIR):
        return np.broadcast_to(b, (P, n, b.shape[0]))

    def out_rows(w):
        return w.reshape(KC, 2, QH, DH, D).transpose(0, 2, 1, 3, 4).reshape(D, D)

    turned = np.array([h * DH + (2 * j + 1 if j < DH // 2 else 2 * (j - DH // 2)) for h in range(2 * H) for j in range(DH)])
    theta = np.float32(10000.0) ** (-np.arange(0, DH, 2, dtype=np.float32) / np.float32(DH))
    freqs = np.arange(P, dtype=np.float32)[:, None] * theta[None, :]
    emb = np.concatenate([np.sin(freqs), np.cos(freqs)], axis=-1).astype(np.float32)
    p = np.arange(P)
    half_ones = np.zeros((P, 2, 2 * DH), np.float32)
    half_ones[:, 0, :DH] = 1
    half_ones[:, 1, DH:] = 1
    a = {
        "x": g["x"].transpose(1, 0, 2), "ctx": g["ctx_1024"].transpose(1, 0, 2), "mask": g["mask_SxS2_bk0"],
        "ident": np.eye(P, dtype=np.float32), "half_ones": half_ones,
        "head_mask": ((p[:, None] // DH) % QH == np.arange(QH)[None, :]).astype(np.float32),
        "turn_sign": np.where(p % DH < DH // 2, -1, 1).astype(np.float32)[:, None],
        "emb": np.tile(emb.T, (P // DH, PAIR)),
        "L0_attn_Wqkv": chunks(g["L0_attn_Wqkv"]), "L0_attn_Wturned": chunks(g["L0_attn_Wqkv"][:, turned]),
        "L0_attn_bqk": cols(g["L0_attn_bqkv"][:2 * D]), "L0_attn_bturned": cols(g["L0_attn_bqkv"][turned]),
        "L0_attn_bv": row(g["L0_attn_bqkv"][2 * D:]), "L0_attn_Wout": chunks(out_rows(g["L0_attn_Wout"])),
        "L0_attn_bout": row(g["L0_attn_bout"]),
        "L1_xattn_bqk": cols(g["L1_xattn_bq"], g["L1_xattn_bk"]), "L1_xattn_bv": row(g["L1_xattn_bv"]),
        "L1_xattn_bo": row(g["L1_xattn_bo"]), "L1_xattn_wo": chunks(out_rows(g["L1_xattn_wo"].T)),
        "L1_attn_W_out": chunks(out_rows(g["L1_attn_W_out"].reshape(D, D))),
    }
    a.update({
        "L0_xattn_Wq": chunks(g["L0_xattn_Wq"]), "L0_xattn_Wk": chunks(g["L0_xattn_Wk"]),
        "L0_xattn_Weq": chunks(g["L0_xattn_We"][:, :D].T), "L0_xattn_Wek": chunks(g["L0_xattn_We"][:, D:].T),
        "L0_xattn_Wv": chunks(g["L0_xattn_Wv"].T),
        "L0_xattn_b": cols(*(g[f"L0_xattn_b{n}"] for n in "qkev")),
        "L0_ffn_wi_W": chunks(g["L0_ffn_wi_W"].T), "L0_ffn_wo_W": chunks(g["L0_ffn_wo_W"].T),
        "L0_ffn_gA": chunks(np.concatenate([g["L0_ffn_gate_W"], g["L0_ffn_lora_A"].reshape(E * R, D)]).T),
        "L0_ffn_B": np.tile(g["L0_ffn_lora_B"].transpose(0, 2, 1).reshape(E * R, F), (3, 1)),
        "L0_ffn_gate_b": row(g["L0_ffn_gate_b"]), "L0_ffn_wi_b": cols(g["L0_ffn_wi_b"]), "L0_ffn_wo_b": row(g["L0_ffn_wo_b"]),
        "L1_ffn_W_fc": chunks(g["L1_ffn_W_fc"].T).reshape(P, -1), "L1_ffn_W_proj": chunks(g["L1_ffn_W_proj"].T).reshape(P, -1),
        "L1_ffn_ln_w": cols(g["L1_ffn_ln_w"]), "L1_ffn_ln_b": cols(g["L1_ffn_ln_b"]),
        "expert_of": np.broadcast_to((np.arange(E * R) // R).astype(np.float32), (P, E * R)),
    })
    for k in ("L1_attn_W_query", "L1_attn_W_key", "L1_attn_W_val"):
        a[k] = chunks(g[k].transpose(1, 0, 2).reshape(D, D))
    for k in ("L1_xattn_wq", "L1_xattn_wk", "L1_xattn_wv"):
        a[k] = chunks(g[k].T)
    return {k: np.ascontiguousarray(v) for k, v in a.items()}


def kernel(**inputs):
    import numpy as _np
    import concourse.bacc as _bacc
    from concourse import mybir as _mybir
    from concourse.bass_utils import run_bass_kernel_spmd as _run

    nc = _bacc.Bacc("TRN2", target_bir_lowering=False, num_devices=1)
    arrays, args = {}, {}
    for name, value in layout(inputs).items():
        arrays[f"in_{name}"] = value
        args[name] = nc.dram_tensor(f"in_{name}", value.shape, _mybir.dt.from_np(value.dtype), kind="ExternalInput").ap()
    out = nc.dram_tensor("out_x", (P, NB, D), FP32, kind="ExternalOutput").ap()
    decoder(nc, args, out)
    r = _run(nc, [arrays], core_ids=[0])
    return _np.ascontiguousarray(_np.asarray(r.results[0]["out_x"]).transpose(1, 0, 2))
```

```python
import numpy as np
import concourse.bass as bass
from concourse import mybir
from contextlib import ExitStack

FP32 = mybir.dt.float32
F32R = mybir.dt.float32r
BF16 = mybir.dt.bfloat16
U8 = mybir.dt.uint8
U32 = mybir.dt.uint32
ALU = mybir.AluOpType
ACT = mybir.ActivationFunctionType
AXX = mybir.AxisListType.X

P = 128
NB = 32
D = 256
KC = D // P
PAIR = 2
NG = NB // PAIR
TOK = PAIR * P
H, DH = 16, 16
QH = 4
NQ = H // QH
STEPS = PAIR * NQ
F = 1024
E, R = 8, 4
GATED = F + E + E * R
LN_EPS = 1e-5
LN_LINKS = 2 * PAIR + 1
ABSMEAN_EPS = 1e-6
X_SEQS = 4
X_LOADS = NB // X_SEQS
MASKED = -4.0e9


def at_least(eng, sem, value):
    if not isinstance(value, int) or value > 0:
        eng.wait_ge(sem, value)


def wait_apart(dve, link, value, mark):
    dve.wait_ge(link, value)
    dve.memset(mark[:], 0.0).then_inc(link, 1)


def cx_count(w, parity):
    return (w - parity) * 8 + 16


def f32(ap):
    return ap.bitcast(FP32)


class Names:

    def __init__(self, nc, ctx, stage):
        self.nc, self.ctx, self.stage, self.sems = nc, ctx, stage, []

    def sb(self, name, shape, dt=FP32):
        return self.ctx.enter_context(self.nc.sbuf_tensor(f"{self.stage}_{name}", shape, dt))

    def ps(self, name):
        return self.ctx.enter_context(self.nc.psum_tensor(f"{self.stage}_{name}", [P, 512], FP32))

    def sem(self, name):
        handle = self.ctx.enter_context(self.nc.semaphore(f"{self.stage}_{name}"))
        self.sems.append(handle)
        return handle

    def clear_semaphores(self):
        with self.nc.Block() as block:

            @block.gpsimd
            def _(pool):
                for handle in self.sems:
                    pool.sem_clear(handle)


def three_pass(pe, out, w_hi, w_lo, m_hi, m_lo, chunks):
    last = None
    for k in range(chunks):
        for n, (w, m) in enumerate(((w_hi, m_hi), (w_lo, m_hi), (w_hi, m_lo))):
            last = pe.matmul(out, w(k), m(k), start=(k == 0 and n == 0), stop=(k == chunks - 1 and n == 2))
    return last


class Arena:

    def __init__(self, *tensors, used=(0, 0)):
        self.tensors, self.used = tensors, list(used)

    def sb(self, shape, dt=FP32):
        kind, n = int(dt == F32R), int(np.prod(shape[1:]))
        tile = self.tensors[kind][0:shape[0], self.used[kind]:self.used[kind] + n]
        self.used[kind] += n
        if len(shape) == 3:
            return tile.rearrange("p (k n) -> p k n", k=shape[1])
        return tile.rearrange("p (b k n) -> p b k n", b=shape[1], k=shape[2]) if len(shape) == 4 else tile


class SplitWeights:

    def __init__(self, sems, stage):
        self.w_in, self.hi_ok, self.w_ok = (sems.sem(f"{stage}_{n}") for n in ("w_in", "w_hi_ok", "w_ok"))
        self.of, self.loads, self.pieces, self.prepared = stage, [], [], False

    def load(self, sp):
        for dst, src in self.loads:
            sp.dma_start(dst, src).then_inc(self.w_in, 16)

    def wait_in(self, eng):
        eng.wait_ge(self.w_in, 16 * len(self.loads))

    def act_piece(self, act, i):
        if i == 0:
            self.wait_in(act)
        raw, hi, _ = self.pieces[i]
        act.activation(hi, raw, ACT.Copy).then_inc(self.hi_ok, 1)

    def dve_piece(self, dve, i):
        raw, hi, lo = self.pieces[i]
        dve.wait_ge(self.hi_ok, i + 1)
        dve.tensor_tensor(lo, raw, f32(hi), ALU.subtract).then_inc(self.w_ok, 1)

    def prepare_act(self, act):
        for i in range(len(self.pieces)):
            self.act_piece(act, i)

    def prepare_dve(self, dve):
        for i in range(len(self.pieces)):
            self.dve_piece(dve, i)

    def wait_split(self, pe):
        pe.wait_ge(self.hi_ok, len(self.pieces))
        pe.wait_ge(self.w_ok, len(self.pieces))


class AttentionWeights(SplitWeights):

    def __init__(self, sems, stage, arena, w_dram, rows, rope=False):
        super().__init__(sems, stage)
        self.w_dram, self.rows, self.rope = w_dram, rows, rope
        self.hi, self.lo = arena.sb([P, KC, 4 * D], F32R), arena.sb([P, KC, 4 * D], F32R)
        self.bias_cols = self.row_v = self.row_o = self.q_mul = None
        if rows:
            self.bias_cols, self.row_v, self.row_o = arena.sb([P, 4]), arena.sb([P, PAIR, D]), arena.sb([P, PAIR, D])
            self.q_mul = arena.sb([P, TOK])
        if rope:
            self.w_fold = sems.sem(f"{stage}_w_fold")

    def stage(self, nm):
        self.raw = nm.sb(f"{self.of}_raw", [P, KC, 4 * D])
        self.loads = [(self.raw[:, :, n * D:n * D + src.shape[2]], src) for n, src in self.w_dram]
        into = {"bias_cols": self.bias_cols, "row_v": self.row_v, "row_o": self.row_o, "q_mul": self.q_mul}
        if self.rope:
            self.turned, self.bias_turned = nm.sb("w_turned", [P, KC, 2 * D]), nm.sb("bias_turned", [P, 4])
            into.update({"w_turned": self.turned, "bias_turned": self.bias_turned})
        self.loads += [(into[k][:], src) for k, src in self.rows]
        halves = [(k, slice(n * 2 * D, (n + 1) * 2 * D)) for n in range(2) for k in range(KC)]
        self.pieces = [(self.raw[:, k, cols], self.hi[:, k, cols], self.lo[:, k, cols]) for k, cols in halves]

    def fold(self, dve, turn_sign):
        self.wait_in(dve)
        new = self.raw[:, :, 0:2 * D].rearrange("p k (h e) -> p k h e", e=DH)
        turned = self.turned[:].rearrange("p k (h e) -> p k h e", e=DH)
        for k in range(KC):
            dve.tensor_tensor(new[:, k, :, 0:DH // 2], new[:, k, :, 0:DH // 2], turned[:, k, :, 0:DH // 2], ALU.subtract)
            dve.tensor_tensor(new[:, k, :, DH // 2:], new[:, k, :, DH // 2:], turned[:, k, :, DH // 2:], ALU.add)
        dve.scalar_tensor_tensor(self.bias_cols[:], self.bias_turned[:], turn_sign, self.bias_cols[:],
                                 op0=ALU.mult, op1=ALU.add).then_inc(self.w_fold, 1)

    def act_piece(self, act, i):
        if i == 0 and self.rope:
            act.wait_ge(self.w_fold, 1)
        super().act_piece(act, i)


class RoutedWeights(SplitWeights):

    def __init__(self, sems, stage, arena, a):
        super().__init__(sems, stage)
        self.a = a
        self.wi_hi, self.wi_lo = arena.sb([P, KC, GATED], F32R), arena.sb([P, KC, GATED], F32R)
        self.wo_hi, self.wo_lo = arena.sb([P, F // P, D], F32R), arena.sb([P, F // P, D], F32R)
        self.b_parts = arena.sb([3 * E * R, F], F32R)
        self.gate_row, self.bias_i, self.row_o = arena.sb([P, PAIR, E]), arena.sb([P, F // P]), arena.sb([P, PAIR, D])
        self.expert_of = arena.sb([P, E * R])

    def stage(self, nm):
        ER = E * R
        wi, wo = nm.sb("routed_wi", [P, KC, GATED]), nm.sb("routed_wo", [P, F // P, D])
        b = nm.sb("routed_b", [3 * ER, F])
        self.loads = [(wi[:, :, 0:F], self.a["L0_ffn_wi_W"]), (wi[:, :, F:], self.a["L0_ffn_gA"]), (wo[:], self.a["L0_ffn_wo_W"]),
                      (b[:], self.a["L0_ffn_B"]), (self.gate_row[:], self.a["L0_ffn_gate_b"]),
                      (self.bias_i[:], self.a["L0_ffn_wi_b"]), (self.row_o[:], self.a["L0_ffn_wo_b"]),
                      (self.expert_of[:], self.a["expert_of"])]
        self.b = b
        half = F // P // 2
        self.pieces = [(wi[:, k, :], self.wi_hi[:, k, :], self.wi_lo[:, k, :]) for k in range(KC)]
        self.pieces += [(wo[:, n * half:(n + 1) * half, :], self.wo_hi[:, n * half:(n + 1) * half, :],
                         self.wo_lo[:, n * half:(n + 1) * half, :]) for n in range(2)]
        self.pieces.append((b[:], self.b_parts[:], None))

    def dve_piece(self, dve, i):
        if self.pieces[i][2] is not None:
            super().dve_piece(dve, i)
            return
        low = slice(E * R, 2 * E * R)
        dve.wait_ge(self.hi_ok, i + 1)
        dve.tensor_tensor(self.b_parts[low, :], self.b[low, :], f32(self.b_parts[low, :]), ALU.subtract).then_inc(self.w_ok, 1)


class EntangledWeights(SplitWeights):

    def __init__(self, sems, stage, arena, a):
        super().__init__(sems, stage)
        self.raw, self.bias_in = arena.sb([P, KC, 5 * D]), arena.sb([P, 4 * KC])
        self.loads = [(self.raw[:, :, n * D:(n + 1) * D], a[f"L0_xattn_{k}"]) for n, k in enumerate(("Wq", "Wk", "Weq", "Wek", "Wv"))]
        self.loads.append((self.bias_in[:], a["L0_xattn_b"]))

    def stage(self, nm):
        pass


class TernaryWeights(SplitWeights):

    def __init__(self, sems, stage, arena, a):
        super().__init__(sems, stage)
        self.raw = [arena.sb([P, KC * F]), arena.sb([P, F // P * D])]
        self.gain, self.offset, self.sums = arena.sb([P, F // P]), arena.sb([P, F // P]), arena.sb([P, 4])
        self.loads = [(self.raw[0][:], a["L1_ffn_W_fc"]), (self.raw[1][:], a["L1_ffn_W_proj"]),
                      (self.gain[:], a["L1_ffn_ln_w"]), (self.offset[:], a["L1_ffn_ln_b"])]

    def stage(self, nm):
        half = KC * F // 2
        self.magnitudes = nm.sb("magnitudes", [P, half], BF16)
        self.pieces = [(self.raw[n // 2][:, n % 2 * half:(n % 2 + 1) * half], None, None) for n in range(4)]

    def act_piece(self, act, i):
        if i == 0:
            self.wait_in(act)
        else:
            act.wait_ge(self.hi_ok, i)
        act.activation(self.magnitudes[:], self.pieces[i][0], ACT.Abs, accum_out=self.sums[:, i:i + 1]).then_inc(self.hi_ok, 1)

    def dve_piece(self, dve, i):
        pass


def attention_stage(nc, name, x_res, consts, wt, following, spare, ctx_dram=None, mask_dram=None, rope=False,
                    k_bias=False, v_bias=False, o_bias=False, x_dram=None):
    nm_ctx = ExitStack()
    nm = Names(nc, nm_ctx, name)
    sb, sem = nm.sb, nm.sem
    ident, ident_b, neg_ident_b, head_mask = (consts[k] for k in ("ident", "ident_b", "neg_ident_b", "head_mask"))

    if not wt.prepared:
        wt.stage(nm)
    following.stage(nm)
    w_hi, w_lo, bias_cols, row_v, row_o, q_mul = wt.hi, wt.lo, wt.bias_cols, wt.row_v, wt.row_o, wt.q_mul
    WQ, WK, WV, WO = (slice(n * D, (n + 1) * D) for n in range(4))

    stats = sb("stats", [P, PAIR, 6])
    moments = sb("moments", [P, PAIR, 2])
    var_eps = sb("var_eps", [P, PAIR])
    ln_mark = sb("ln_mark", [P, 1])
    rstd = sb("rstd", [P, PAIR])
    xn = sb("xn", [P, PAIR, D])
    xT_hi = spare.sb([P, KC, TOK], F32R)
    xT_lo = spare.sb([P, KC, TOK], F32R)
    q32 = sb("q32", [P, KC, TOK])
    k32 = sb("k32", [P, KC, TOK])
    q_lo = sb("q_lo", [P, KC, TOK])
    q_hi = [spare.sb([P, KC, TOK], F32R) for i in range(2)]
    k_hi = [spare.sb([P, KC, TOK], F32R) for i in range(2)]
    k_lo = [spare.sb([P, KC, TOK], F32R) for i in range(2)]
    qm_hi = [sb(f"qm_hi{i}", [P, KC, PAIR, QH, P], F32R) for i in range(2)]
    qm_lo = [sb(f"qm_lo{i}", [P, KC, PAIR, QH, P], F32R) for i in range(2)]
    km_hi = [sb(f"km_hi{i}", [P, KC, PAIR, QH, P], F32R) for i in range(2)]
    v_pad = [sb(f"v_pad{i}", [P, PAIR, H, 2 * DH]) for i in range(2)]
    row_max = sb("row_max", [P, 4, QH], BF16)
    probs = sb("probs", [P, 4, QH * P])
    inv_den = sb("inv_den", [P, D])
    o32 = sb("o32", [P, KC, P])
    o_hi = spare.sb([P, PAIR, KC, P], F32R)
    o_lo = spare.sb([P, PAIR, KC, P], F32R)

    S1 = [nm.ps(f"S1_{i}") for i in range(2)]
    S2 = [nm.ps(f"S2_{i}") for i in range(2)]
    AV = [nm.ps(f"AV_{i}") for i in range(2)]
    FA, FB = nm.ps("FA"), nm.ps("FB")


    cross = ctx_dram is not None
    if cross:
        mask_link = sem("mask_link")
        cx = [sb(f"cx{i}", [P, PAIR, D]) for i in range(2)]
        cT_hi = sb("cT_hi", [P, KC, TOK], F32R)
        cT_lo = sb("cT_lo", [P, KC, TOK], F32R)
        mask_u8 = sb("mask_u8", [P, P], U8)
        keep = sb("keep", [P, P])
        any_kept = sb("any_kept", [P, 1])
        add_mask32 = sb("add_mask32", [P, P])
        add_mask = sb("add_mask", [P, P], BF16)
        add_maskT = sb("add_maskT", [P, P], BF16)
        cx_in = [sem(f"cx_in{i}") for i in range(2)]
        ctx_full, ctx_hi, ctx_lo = sem("ctx_full"), sem("ctx_hi"), sem("ctx_lo")
    kvT_hi, kvT_lo = (cT_hi, cT_lo) if cross else (xT_hi, xT_lo)

    x_first, x_rest, mask_in = sem("x_first"), sem("x_rest"), sem("mask_in")
    zeroed, setup, setup_pe = sem("zeroed"), sem("setup"), sem("setup_pe")
    ln_link, var_ok, rstd_ok, xn_ok, biased = sem("ln_link"), sem("var_ok"), sem("rstd_ok"), sem("xn_ok"), sem("biased")
    pt_full, pt_hi, pt_lo = sem("pt_full"), sem("pt_hi"), sem("pt_lo")
    q_full, q_free, qhi_ok, qlo_ok, qmhi_ok, qm_ok = (sem(n) for n in ("q_full", "q_free", "qhi_ok", "qlo_ok", "qmhi_ok", "qm_ok"))
    k_full, k_free, khi_ok, klo_ok, km_ok = (sem(n) for n in ("k_full", "k_free", "khi_ok", "klo_ok", "km_ok"))
    v_full, v_free, out_full, out_free = sem("v_full"), sem("v_free"), sem("out_full"), sem("out_free")
    s1_full, max_ok, s2_full, exp_ok, av_full = (sem(n) for n in ("s1_full", "max_ok", "s2_full", "exp_ok", "av_full"))
    inv_ok, o32_ok, ohi_ok, olo_ok = sem("inv_ok"), sem("o32_ok"), sem("ohi_ok"), sem("olo_ok")

    dve_q = rope or cross
    dve_k = rope

    def schedule(eng, group):
        for G in range(-1, 3):
            group(G, G % 2)
        with eng.Fori(1, (NG - 4) // 2) as i:
            group(i * 2 + 1, 1)
            group(i * 2 + 2, 0)
        for G in range(NG - 3, NG + 1):
            group(G, G % 2)

    def has_norm(G):
        return not isinstance(G, int) or G + 2 < NG

    def has_window(G):
        return not isinstance(G, int) or G + 1 < NG

    def has_step(G, t):
        return not isinstance(G, int) or 0 <= STEPS * G + t < STEPS * NG

    def whole(G):
        return not isinstance(G, int) or 0 <= G < NG

    def place(t):
        tt = t % STEPS
        return tt // NQ, (tt % NQ) // 2, tt % 2, t < 0

    def v_places(flat, u):
        v = flat.rearrange("p (b c u v e) -> p (b c) u v e", c=KC, u=2, v=QH, e=2 * DH, b=PAIR)
        return v[:, :, u, :, u * DH:(u + 1) * DH]

    def v_cols(bank, u):
        return bank[:].rearrange("p (b c u v e) -> p (b c) u v e", c=KC, u=2, v=QH, e=DH, b=PAIR)[:, :, u]

    with nc.Block() as block:

        @block.sync
        def _(sp):
            def load_x(n):
                part = slice(n * X_SEQS, (n + 1) * X_SEQS)
                sp.dma_start(x_res[:, part, :], x_dram[:, part, :]).then_inc(x_first if n == 0 else x_rest, 16)
            if x_dram is not None:
                load_x(0)
            if not wt.prepared:
                wt.load(sp)
            if cross:
                sp.dma_start(mask_u8[:], mask_dram).then_inc(mask_in, 16)
            if x_dram is not None:
                for n in range(1, X_LOADS):
                    load_x(n)
            if cross:
                def load_ctx(w, parity):
                    at_least(sp, ctx_full, w - 1)
                    src = ctx_dram[:, w * PAIR:(w + 1) * PAIR, :] if isinstance(w, int) else \
                        ctx_dram[:, bass.ds(w * PAIR, PAIR), :]
                    sp.dma_start(cx[parity][:], src).then_inc(cx_in[parity], 16)
                load_ctx(0, 0)
                load_ctx(1, 1)
                following.load(sp)
                with sp.Fori(1, NG // 2) as i:
                    load_ctx(i * 2, 0)
                    load_ctx(i * 2 + 1, 1)
            else:
                following.load(sp)

        @block.gpsimd
        def _(pool):
            for i in range(2):
                pool.memset(v_pad[i][:], 0.0).then_inc(zeroed, 1)
            if o_bias:
                wt.wait_in(pool)

            def window(w):
                pool.wait_ge(ln_link, (w + 1) * LN_LINKS)
                at_least(pool, xn_ok, w)
                pool.tensor_tensor(var_eps[:], moments[:, :, 1], consts["ln_eps"][:], ALU.add).then_inc(var_ok, 1)
                pool.wait_ge(var_ok, w + 1)
                pool.tensor_tensor(rstd[:], var_eps[:], consts["minus_half"][:], ALU.pow).then_inc(rstd_ok, 1)
                if o_bias:
                    pool.wait_ge(xn_ok, w + 1)
                    x = x_res[:, w * PAIR:(w + 1) * PAIR, :] if isinstance(w, int) else x_res[:, bass.ds(w * PAIR, PAIR), :]
                    pool.tensor_tensor(x, x, row_o[:], ALU.add).then_inc(biased, 1)
            window(0)
            with pool.Fori(1, NG) as w:
                window(w)

        @block.scalar
        def _(act):
            if not wt.prepared:
                wt.prepare_act(act)
            wt.wait_in(act)
            def exp_step(G, t, parity):
                T = G * STEPS + t
                act.wait_ge(s2_full, T + 1)
                at_least(act, av_full, T - 3)
                act.activation(probs[:, t % 4, :], S2[t % 2][:], ACT.Exp, scale=DH ** -0.5).then_inc(exp_ok, 1)

            def out_high(B, G, b):
                act.wait_ge(o32_ok, B + 1)
                at_least(act, out_full, G)
                act.activation(o_hi[:, b], o32[:], ACT.Copy).then_inc(ohi_ok, 1)

            def group(G, parity):
                w, wp = G + 1, 1 - parity
                for t in range(STEPS):
                    if has_step(G, t - 2):
                        exp_step(G, t - 2, parity)
                    if has_window(G) and t == 1:
                        act.wait_ge(pt_full, w + 1)
                        at_least(act, v_full, w)
                        act.activation(xT_hi[:], FA[:].rearrange("p (c t) -> p c t", c=KC),
                                       ACT.Copy).then_inc(pt_hi, 1)
                        if cross:
                            act.wait_ge(ctx_full, w + 1)
                            act.activation(cT_hi[:], FB[:].rearrange("p (c t) -> p c t", c=KC),
                                           ACT.Copy).then_inc(ctx_hi, 1)
                            if isinstance(G, int) and G < 0:
                                act.wait_ge(setup_pe, 1)
                                act.activation(add_maskT[:], S1[0][:, 0:P], ACT.Copy).then_inc(setup, 1)
                                act.wait_ge(setup_pe, 2)
                                for b in range(PAIR):
                                    last = act.activation(q_mul[:, b * P:(b + 1) * P], S1[1][:, 0:P], ACT.Copy)
                                last.then_inc(setup, 1)
                    if has_window(G) and t == 4:
                        if not dve_q:
                            act.wait_ge(q_full, w + 1)
                            at_least(act, qm_ok, w)
                            act.activation(q32[:], FB[:].rearrange("p (c t) -> p c t", c=KC),
                                           ACT.Copy).then_inc(q_free, 1)
                        act.wait_ge(q_free, w + 1)
                        at_least(act, s1_full, (w - 1) * STEPS)
                        act.activation(q_hi[wp][:], q32[:], ACT.Copy).then_inc(qhi_ok, 1)
                        at_least(act, s2_full, (w - 1) * STEPS)
                        for v in range(QH):
                            last = act.activation(qm_hi[wp][:, :, :, v, :],
                                                  q32[:].rearrange("p c (b t) -> p c b t", b=PAIR),
                                                  ACT.Copy, scale=head_mask[:, v:v + 1])
                        last.then_inc(qmhi_ok, 1)
                    if has_window(G) and t == 5:
                        if not dve_k:
                            act.wait_ge(k_full, w + 1)
                            at_least(act, klo_ok, w)
                            for c in range(KC):
                                if not k_bias:
                                    last = act.activation(k32[:, c], FA[:, c * TOK:(c + 1) * TOK], ACT.Copy)
                                else:
                                    last = act.activation(k32[:, c], FA[:, c * TOK:(c + 1) * TOK], ACT.Identity,
                                                          bias=bias_cols[:, KC + c:KC + c + 1])
                            last.then_inc(k_free, 1)
                        act.wait_ge(k_free, w + 1)
                        at_least(act, s2_full, (w - 1) * STEPS)
                        act.activation(k_hi[wp][:], k32[:], ACT.Copy).then_inc(khi_ok, 1)
                        for v in range(QH):
                            last = act.activation(km_hi[wp][:, :, :, v, :],
                                                  k32[:].rearrange("p c (b t) -> p c b t", b=PAIR),
                                                  ACT.Copy, scale=head_mask[:, v:v + 1])
                        last.then_inc(km_ok, 1)
                    if has_window(G) and t == 6 and not v_bias:
                        act.wait_ge(v_full, w + 1)
                        at_least(act, av_full, (w - 1) * STEPS)
                        if isinstance(w, int):
                            at_least(act, zeroed, 2)
                        v_out = v_pad[wp][:].rearrange("p b h e -> p (b h e)")
                        act.activation(v_places(v_out, 0), v_cols(FB, 0), ACT.Copy)
                        act.activation(v_places(v_out, 1), v_cols(FB, 1), ACT.Copy).then_inc(v_free, 1)
                    if t == 3 and whole(G - 1):
                        out_high(G * PAIR - 1, G - 1, 1)
                    if t == 7 and whole(G):
                        out_high(G * PAIR, G, 0)
                    if isinstance(G, int) and G == NG - 1 and t < len(following.pieces):
                        following.act_piece(act, t)
            schedule(act, group)

        @block.vector
        def _(dve):
            def x_seq(w, b):
                return x_res[:, w * PAIR + b, :] if isinstance(w, int) else \
                    x_res[:, bass.ds(w * PAIR + b, 1), :].rearrange("p b d -> p (b d)")

            def moments_of(w):
                if x_dram is not None and isinstance(w, int) and w * PAIR < X_SEQS:
                    dve.wait_ge(x_first, 16)
                elif x_dram is not None and isinstance(w, int):
                    dve.wait_ge(x_rest, 16 * (X_LOADS - 1))
                for b in range(PAIR):
                    dve.bn_stats(stats[:, b, :], x_seq(w, b)).then_inc(ln_link, 1)
                wait_apart(dve, ln_link, w * LN_LINKS + PAIR, ln_mark)
                for b in range(PAIR):
                    dve.bn_aggr(moments[:, b, :], stats[:, b, :]).then_inc(ln_link, 1)

            if not wt.prepared:
                if x_dram is not None:
                    moments_of(0)
                if rope:
                    wt.fold(dve, consts["turn_sign"][:])
                wt.prepare_dve(dve)
            wt.wait_in(dve)
            def masks():
                dve.wait_ge(mask_in, 16)
                dve.tensor_copy(keep[:], mask_u8[:]).then_inc(mask_link, 1)
                dve.wait_ge(mask_link, 1)
                dve.tensor_reduce(any_kept[:], keep[:], AXX, ALU.max).then_inc(mask_link, 1)
                dve.tensor_scalar(add_mask32[:], keep[:], -1.0, -MASKED, ALU.add, ALU.mult).then_inc(mask_link, 1)
                dve.wait_ge(mask_link, 3)
                dve.tensor_scalar(add_mask32[:], add_mask32[:], any_kept[:], None, ALU.mult).then_inc(mask_link, 1)
                dve.wait_ge(mask_link, 4)
                dve.tensor_copy(add_mask[:], add_mask32[:]).then_inc(mask_link, 1)

            def layer_norm(w):
                dve.wait_ge(rstd_ok, w + 1)
                at_least(dve, pt_full, w)
                for b in range(PAIR):
                    last = dve.tensor_scalar(xn[:, b, :], x_seq(w, b), moments[:, b, 0:1], rstd[:, b:b + 1],
                                             ALU.subtract, ALU.mult)
                last.then_inc(xn_ok, 1)

            def max_step(G, t):
                T = G * STEPS + t
                dve.wait_ge(s1_full, T + 1)
                at_least(dve, s2_full, T - 3)
                dve.tensor_reduce(row_max[:, t % 4, :], S1[t % 2][:].rearrange("p (h k) -> p h k", h=QH),
                                  AXX, ALU.max).then_inc(max_ok, 1)

            def normalise(B, b):
                dve.wait_ge(av_full, B * NQ + NQ)
                dve.reciprocal(inv_den[:], AV[b][:, D:2 * D]).then_inc(inv_ok, 1)
                at_least(dve, ohi_ok, B)
                dve.wait_ge(inv_ok, B + 1)
                dve.tensor_tensor(o32[:].rearrange("p c t -> p (c t)"), AV[b][:, 0:D], inv_den[:],
                                  ALU.mult).then_inc(o32_ok, 1)

            def out_low(B, b):
                dve.wait_ge(ohi_ok, B + 1)
                dve.tensor_tensor(o_lo[:, b], o32[:], f32(o_hi[:, b]), ALU.subtract).then_inc(olo_ok, 1)

            def group(G, parity):
                w, wp = G + 1, 1 - parity
                for t in range(STEPS):
                    if has_step(G, t):
                        max_step(G, t)
                    if t == 0 and whole(G - 1):
                        out_low(G * PAIR - PAIR, 0)
                    if t == 4 and whole(G - 1):
                        out_low(G * PAIR - 1, 1)
                    if t == 0 and isinstance(G, int) and G < 0:
                        if wt.prepared or x_dram is None:
                            moments_of(0)
                        layer_norm(0)
                        if cross:
                            masks()
                    if has_norm(G) and t == 2:
                        moments_of(w + 1)
                    if has_norm(G) and t == 3:
                        layer_norm(w + 1)
                    if has_window(G) and t == 2:
                        dve.wait_ge(pt_hi, w + 1)
                        dve.tensor_tensor(xT_lo[:], FA[:].rearrange("p (c t) -> p c t", c=KC), f32(xT_hi[:]),
                                          ALU.subtract).then_inc(pt_lo, 1)
                        if cross:
                            dve.wait_ge(ctx_hi, w + 1)
                            dve.tensor_tensor(cT_lo[:], FB[:].rearrange("p (c t) -> p c t", c=KC), f32(cT_hi[:]),
                                              ALU.subtract).then_inc(ctx_lo, 1)
                    if t == 3 and whole(G - 1):
                        normalise(G * PAIR - 1, 1)
                    if has_window(G) and t == 4 and dve_q:
                        dve.wait_ge(q_full, w + 1)
                        if cross and isinstance(w, int) and w == 0:
                            dve.wait_ge(setup, 2)
                        at_least(dve, qmhi_ok, w)
                        for c in range(KC):
                            last = dve.scalar_tensor_tensor(q32[:, c], FB[:, c * TOK:(c + 1) * TOK],
                                                            bias_cols[:, c:c + 1], q_mul[:], op0=ALU.add, op1=ALU.mult)
                        last.then_inc(q_free, 1)
                    if has_window(G) and t == 5:
                        if dve_k:
                            dve.wait_ge(k_full, w + 1)
                            at_least(dve, km_ok, w)
                            for c in range(KC):
                                last = dve.scalar_tensor_tensor(k32[:, c], FA[:, c * TOK:(c + 1) * TOK],
                                                                bias_cols[:, KC + c:KC + c + 1], q_mul[:],
                                                                op0=ALU.add, op1=ALU.mult)
                            last.then_inc(k_free, 1)
                        dve.wait_ge(qhi_ok, w + 1)
                        dve.tensor_tensor(q_lo[:], q32[:], f32(q_hi[wp][:]), ALU.subtract).then_inc(qlo_ok, 1)
                        at_least(dve, s2_full, (w - 1) * STEPS)
                    if has_window(G) and t == 6:
                        dve.wait_ge(qlo_ok, w + 1)
                        for v in range(QH):
                            last = dve.tensor_scalar(qm_lo[wp][:, :, :, v, :],
                                                     q_lo[:].rearrange("p c (b t) -> p c b t", b=PAIR),
                                                     head_mask[:, v:v + 1], None, ALU.mult)
                        last.then_inc(qm_ok, 1)
                        dve.wait_ge(khi_ok, w + 1)
                        dve.tensor_tensor(k_lo[wp][:], k32[:], f32(k_hi[wp][:]), ALU.subtract).then_inc(klo_ok, 1)
                        if v_bias:
                            dve.wait_ge(v_full, w + 1)
                            at_least(dve, av_full, (w - 1) * STEPS)
                            if isinstance(w, int):
                                dve.wait_ge(zeroed, 2)
                            flat = v_pad[wp][:].rearrange("p b h e -> p (b h e)")
                            for u in range(2):
                                last = dve.tensor_tensor(v_places(flat, u), v_cols(FB, u), v_cols(row_v[:].rearrange("p b d -> p (b d)"), u), ALU.add)
                            last.then_inc(v_free, 1)
                    if t == 7 and whole(G - 1):
                        dve.wait_ge(out_full, G)
                        if o_bias:
                            dve.wait_ge(biased, G)
                        x = x_res[:, (G - 1) * PAIR:G * PAIR, :] if isinstance(G, int) else \
                            x_res[:, bass.ds((G - 1) * PAIR, PAIR), :]
                        dve.tensor_tensor(x, x, FA[:].rearrange("p (b d) -> p b d", b=PAIR), ALU.add).then_inc(out_free, 1)
                    if t == 7 and whole(G):
                        normalise(G * PAIR, 0)
                    if isinstance(G, int) and G == NG - 1 and 1 <= t <= len(following.pieces):
                        following.dve_piece(dve, t - 1)
            schedule(dve, group)

        @block.tensor
        def _(pe):
            def s1_step(G, t, parity):
                T = G * STEPS + t
                b, c, u, _ = place(t)
                rows64 = slice(64 * u, 64 * u + 64)
                if cross and isinstance(G, int) and G == 0 and t == 0:
                    pe.wait_ge(setup, 2)
                if t == 0:
                    pe.wait_ge(qhi_ok, G + 1)
                    pe.wait_ge(km_ok, G + 1)
                at_least(pe, max_ok, T - 1)
                last = pe.matmul(S1[t % 2][:], q_hi[parity][rows64, c, b * P:(b + 1) * P],
                                 km_hi[parity][rows64, c, b].rearrange("p h t -> p (h t)"), start=True, stop=not cross)
                if cross:
                    for v in range(QH):
                        last = pe.matmul(S1[t % 2][:, v * P:(v + 1) * P], ident_b[:], add_mask[:],
                                         start=False, stop=v == QH - 1)
                last.then_inc(s1_full, 1)

            def s2_step(G, t, parity):
                T = G * STEPS + t
                b, c, u, before = place(t)
                par = 1 - parity if before else parity
                rows64 = slice(64 * u, 64 * u + 64)
                tok = slice(b * P, (b + 1) * P)
                if t == 0:
                    pe.wait_ge(qmhi_ok, G + 1)
                    pe.wait_ge(qm_ok, G + 1)
                    pe.wait_ge(klo_ok, G + 1)
                at_least(pe, exp_ok, T - 1)
                bank = S2[t % 2]
                q_high = qm_hi[par][rows64, c, b].rearrange("p h t -> p (h t)")
                q_low = qm_lo[par][rows64, c, b].rearrange("p h t -> p (h t)")
                pe.matmul(bank[:], k_hi[par][rows64, c, tok], q_high, start=True, stop=False)
                pe.matmul(bank[:], k_hi[par][rows64, c, tok], q_low, start=False, stop=False)
                pe.matmul(bank[:], k_lo[par][rows64, c, tok], q_high, start=False, stop=False)
                pe.wait_ge(max_ok, T + 1)
                for v in range(QH):
                    part = bank[:, v * P:(v + 1) * P]
                    if cross:
                        pe.matmul(part, ident_b[:], add_maskT[:], start=False, stop=False)
                    last = pe.matmul(part, row_max[:, t % 4, v:v + 1].to_broadcast([P, P]), neg_ident_b[:],
                                     start=False, stop=v == QH - 1)
                last.then_inc(s2_full, 1)

            def av_step(G, t, parity):
                T = G * STEPS + t
                b, c, u, before = place(t)
                par = 1 - parity if before else parity
                if t == 0:
                    pe.wait_ge(v_free, G + 1)
                if t % NQ == 0:
                    at_least(pe, o32_ok, G * PAIR + t // NQ - 1)
                pe.wait_ge(exp_ok, T + 1)
                for v in range(QH):
                    pe.matmul(AV[b][32 * v:32 * v + 32, c * P:(c + 1) * P], v_pad[par][:, b, c * 8 + u * QH + v, :],
                              probs[:, t % 4, v * P:(v + 1) * P], start=(t % NQ == 0), stop=False)
                for v in range(QH):
                    last = pe.matmul(AV[b][32 * v:32 * v + 32, D + c * P:D + (c + 1) * P], consts["half_ones"][:, u, :],
                                     probs[:, t % 4, v * P:(v + 1) * P], start=False, stop=(t % NQ == NQ - 1))
                last.then_inc(av_full, 1)

            def project(bank, cols, hi, lo):
                for m in range(KC):
                    wcol = slice(cols.start + m * P, cols.start + (m + 1) * P)
                    last = three_pass(pe, bank[:, m * TOK:(m + 1) * TOK], lambda k: w_hi[:, k, wcol],
                                      lambda k: w_lo[:, k, wcol], lambda k: hi[:, k, :], lambda k: lo[:, k, :], KC)
                return last

            def group(G, parity):
                w = G + 1
                for t in range(STEPS):
                    if has_step(G, t):
                        s1_step(G, t, parity)
                    if has_step(G, t - 2):
                        s2_step(G, t - 2, parity)
                    if has_step(G, t - 4):
                        av_step(G, t - 4, parity)
                    if has_window(G) and t == 1:
                        pe.wait_ge(xn_ok, w + 1)
                        at_least(pe, out_free, w - 2)
                        at_least(pe, k_free, w)
                        for c in range(KC):
                            for b in range(PAIR):
                                last = pe.transpose(FA[:, c * TOK + b * P:c * TOK + (b + 1) * P],
                                                    xn[:, b, c * P:(c + 1) * P], ident[:])
                        last.then_inc(pt_full, 1)
                        at_least(pe, v_free, w)
                        if cross:
                            pe.wait_ge(cx_in[1 - parity], 16 * ((w // 2) + 1) if isinstance(w, int) else cx_count(w, 1 - parity))
                            for c in range(KC):
                                for b in range(PAIR):
                                    last = pe.transpose(FB[:, c * TOK + b * P:c * TOK + (b + 1) * P],
                                                        cx[1 - parity][:, b, c * P:(c + 1) * P], ident[:])
                            last.then_inc(ctx_full, 1)
                            if isinstance(G, int) and G < 0:
                                pe.wait_ge(mask_link, 5)
                                pe.transpose(S1[0][:, 0:P], add_mask32[:], ident[:]).then_inc(setup_pe, 1)
                                pe.matmul(S1[1][:, 0:P], any_kept[:].to_broadcast([P, P]), ident[:], start=True,
                                          stop=True).then_inc(setup_pe, 1)
                    if has_window(G) and t == 3:
                        pe.wait_ge(pt_lo, w + 1)
                        if cross:
                            pe.wait_ge(ctx_lo, w + 1)
                        if isinstance(w, int) and w == 0:
                            wt.wait_split(pe)
                        project(FB, WQ, xT_hi, xT_lo).then_inc(q_full, 1)
                    if has_window(G) and t == 4:
                        project(FA, WK, kvT_hi, kvT_lo).then_inc(k_full, 1)
                    if has_window(G) and t == 5:
                        pe.wait_ge(q_free, w + 1)
                        for b in range(PAIR):
                            tok = slice(b * P, (b + 1) * P)
                            last = three_pass(pe, FB[:, b * D:(b + 1) * D], lambda k: kvT_hi[:, k, tok],
                                              lambda k: kvT_lo[:, k, tok], lambda k: w_hi[:, k, WV],
                                              lambda k: w_lo[:, k, WV], KC)
                        last.then_inc(v_full, 1)
                    if t == 6 and whole(G - 1):
                        pe.wait_ge(olo_ok, G * PAIR)
                        if has_window(G):
                            pe.wait_ge(k_free, w + 1)
                        else:
                            pe.wait_ge(k_free, NG)
                            pe.wait_ge(out_free, G - 1)
                        for b in range(PAIR):
                            last = three_pass(pe, FA[:, b * D:(b + 1) * D], lambda k: o_hi[:, b, k, :],
                                              lambda k: o_lo[:, b, k, :], lambda k: w_hi[:, k, WO],
                                              lambda k: w_lo[:, k, WO], KC)
                        last.then_inc(out_full, 1)
            schedule(pe, group)
    nm.clear_semaphores()
    nm_ctx.close()


class Normed:

    def __init__(self, nm, consts, x_res, bank, x_in=None, n_x=0):
        self.x_res, self.ident, self.minus_half, self.eps, self.bank = x_res, consts["ident"], consts["minus_half"], consts["ln_eps"], bank
        self.mark = nm.sb("ln_mark", [P, 1])
        self.x_in, self.n_x = x_in, n_x
        self.stats, self.moments = nm.sb("stats", [P, PAIR, 6]), nm.sb("moments", [P, PAIR, 2])
        self.var_eps, self.rstd = nm.sb("var_eps", [P, PAIR]), nm.sb("rstd", [P, PAIR])
        self.xn = nm.sb("xn", [P, PAIR, D])
        self.hi = [nm.sb(f"xT_hi{i}", [P, KC, TOK], F32R) for i in range(2)]
        self.lo = [nm.sb(f"xT_lo{i}", [P, KC, TOK], F32R) for i in range(2)]
        self.ln_link, self.var_ok, self.rstd_ok, self.xn_ok = (nm.sem(n) for n in ("ln_link", "var_ok", "rstd_ok", "xn_ok"))
        self.full, self.hi_ok, self.lo_ok = (nm.sem(n) for n in ("pt_full", "pt_hi", "pt_lo"))

    def x(self, w, b):
        return self.x_res[:, w * PAIR + b, :] if isinstance(w, int) else \
            self.x_res[:, bass.ds(w * PAIR + b, 1), :].rearrange("p b d -> p (b d)")

    def x_group(self, w):
        return self.x_res[:, w * PAIR:(w + 1) * PAIR, :] if isinstance(w, int) else \
            self.x_res[:, bass.ds(w * PAIR, PAIR), :]

    def dve_moments(self, dve, w):
        if self.x_in is not None and isinstance(w, int):
            dve.wait_ge(self.x_in, self.n_x)
        for b in range(PAIR):
            dve.bn_stats(self.stats[:, b, :], self.x(w, b)).then_inc(self.ln_link, 1)
        wait_apart(dve, self.ln_link, w * LN_LINKS + PAIR, self.mark)
        for b in range(PAIR):
            dve.bn_aggr(self.moments[:, b, :], self.stats[:, b, :]).then_inc(self.ln_link, 1)

    def dve_normalise(self, dve, w):
        dve.wait_ge(self.rstd_ok, w + 1)
        at_least(dve, self.full, w)
        for b in range(PAIR):
            last = dve.tensor_scalar(self.xn[:, b, :], self.x(w, b), self.moments[:, b, 0:1], self.rstd[:, b:b + 1],
                                     ALU.subtract, ALU.mult)
        last.then_inc(self.xn_ok, 1)

    def pool_rstd(self, pool, w):
        pool.wait_ge(self.ln_link, (w + 1) * LN_LINKS)
        at_least(pool, self.xn_ok, w)
        pool.tensor_tensor(self.var_eps[:], self.moments[:, :, 1], self.eps[:], ALU.add).then_inc(self.var_ok, 1)
        pool.wait_ge(self.var_ok, w + 1)
        pool.tensor_tensor(self.rstd[:], self.var_eps[:], self.minus_half[:], ALU.pow).then_inc(self.rstd_ok, 1)

    def pe_transpose(self, pe, w):
        pe.wait_ge(self.xn_ok, w + 1)
        at_least(pe, self.lo_ok, w)
        for c in range(KC):
            for b in range(PAIR):
                last = pe.transpose(self.bank[:, c * TOK + b * P:c * TOK + (b + 1) * P],
                                    self.xn[:, b, c * P:(c + 1) * P], self.ident[:])
        last.then_inc(self.full, 1)

    def act_high(self, act, w, parity, used, per_group=1):
        act.wait_ge(self.full, w + 1)
        at_least(act, used, (w - 1) * per_group)
        act.activation(self.hi[parity][:], chunked(self.bank), ACT.Copy).then_inc(self.hi_ok, 1)

    def dve_low(self, dve, w, parity):
        dve.wait_ge(self.hi_ok, w + 1)
        dve.tensor_tensor(self.lo[parity][:], chunked(self.bank), f32(self.hi[parity][:]),
                          ALU.subtract).then_inc(self.lo_ok, 1)


def chunked(bank):
    return bank[:].rearrange("p (c t) -> p c t", c=KC)


def windows(eng, window, last=NG):
    for w in range(-2, 3):
        window(w, w % 2)
    with eng.Fori(1, (NG - 4) // 2) as i:
        window(i * 2 + 1, 1)
        window(i * 2 + 2, 0)
    for w in range(NG - 3, last + 1):
        window(w, w % 2)


def next_pieces(w, following):
    if not isinstance(w, int) or following is None or w < NG - 3:
        return range(0)
    return range(min(2 * (w - NG + 3), len(following.pieces)), min(2 * (w - NG + 4), len(following.pieces)))


def in_stage(w):
    return not isinstance(w, int) or 0 <= w < NG


def entangled_stage(nc, name, x_res, consts, a, wt, following, x_dram=None):
    with ExitStack() as ctx:
        nm = Names(nc, ctx, name)
        sb, sem = nm.sb, nm.sem
        PT, PC, ENT, VT, VTOK, SC, PP, OUT = (nm.ps(n) for n in ("PT", "PC", "ENT", "VT", "VTOK", "SC", "PP", "OUT"))
        x_in = sem("x_in")
        ln = Normed(nm, consts, x_res, PT, x_in if x_dram is not None else None, 16)
        following.stage(nm)
        w_raw, bias_in = wt.raw, wt.bias_in
        fold = sb("fold", [P, KC, 3 * D])
        w_hi, w_lo = sb("w_hi", [P, KC, 3 * D], F32R), sb("w_lo", [P, KC, 3 * D], F32R)
        bias_e = sb("bias_e", [P, KC])
        cx = [sb(f"cx{i}", [P, PAIR, D]) for i in range(2)]
        cT_hi = [sb(f"cT_hi{i}", [P, KC, TOK], F32R) for i in range(2)]
        cT_lo = [sb(f"cT_lo{i}", [P, KC, TOK], F32R) for i in range(2)]
        ent, vT = sb("ent", [P, KC, TOK]), sb("vT", [P, KC, TOK])
        v_tok = sb("v_tok", [P, PAIR, D])
        top, shift = sb("top", [P, PAIR]), sb("shift", [P, PAIR])
        probs, probsT = sb("probs", [P, PAIR, P]), sb("probsT", [P, PAIR, P])
        total, inv_total = sb("total", [P, PAIR]), sb("inv_total", [P, PAIR])
        folded, fold_ok, hi_ok, w_ok = (sem(n) for n in ("folded", "fold_ok", "hi_ok", "w_ok"))
        cx_in = [sem(f"cx_in{i}") for i in range(2)]
        pc_full, pc_hi, pc_lo = sem("pc_full"), sem("pc_hi"), sem("pc_lo")
        ent_full, ent_ok, vt_full, vt_ok = sem("ent_full"), sem("ent_ok"), sem("vt_full"), sem("vt_ok")
        vtok_full, vtok_ok, sc_full, top_ok, shift_ok = (sem(n) for n in ("vtok_full", "vtok_ok", "sc_full", "top_ok", "shift_ok"))
        exp_ok, inv_ok, pp_full, pp_ok, out_full, out_ok = (sem(n) for n in ("exp_ok", "inv_ok", "pp_full", "pp_ok", "out_full", "out_ok"))

        with nc.Block() as block:

            @block.sync
            def _(sp):
                if x_dram is not None:
                    sp.dma_start(x_res[:], x_dram).then_inc(x_in, 16)
                if not wt.prepared:
                    wt.load(sp)

                def load_ctx(w, parity):
                    at_least(sp, pc_full, w - 1)
                    src = a["ctx"][:, w * PAIR:(w + 1) * PAIR, :] if isinstance(w, int) else \
                        a["ctx"][:, bass.ds(w * PAIR, PAIR), :]
                    sp.dma_start(cx[parity][:], src).then_inc(cx_in[parity], 16)
                load_ctx(0, 0)
                load_ctx(1, 1)
                following.load(sp)
                with sp.Fori(1, NG // 2) as i:
                    load_ctx(i * 2, 0)
                    load_ctx(i * 2 + 1, 1)

            @block.gpsimd
            def _(pool):
                ln.pool_rstd(pool, 0)
                with pool.Fori(1, NG) as w:
                    ln.pool_rstd(pool, w)

            @block.scalar
            def _(act):
                act.wait_ge(folded, 1)
                for n, bank in enumerate((ENT, VT)):
                    act.activation(fold[:, :, n * D:(n + 1) * D], chunked(bank), ACT.Copy)
                wt.wait_in(act)
                act.activation(fold[:, :, 2 * D:], w_raw[:, :, 4 * D:], ACT.Copy).then_inc(fold_ok, 1)
                act.wait_ge(fold_ok, 2)
                act.activation(w_hi[:], fold[:], ACT.Copy).then_inc(hi_ok, 1)

                def window(w, parity):
                    if in_stage(w - 1):
                        for b in range(PAIR):
                            act.wait_ge(shift_ok, w)
                            if b == 0:
                                at_least(act, pp_full, w - 1)
                            last = act.activation(probs[:, b, :], SC[:, b * P:(b + 1) * P], ACT.Exp, bias=shift[:, b:b + 1],
                                                  scale=D ** -0.5, accum_out=total[:, b:b + 1])
                        last.then_inc(exp_ok, 1)
                    if in_stage(w + 1):
                        ln.act_high(act, w + 1, 1 - parity, vt_full)
                        act.wait_ge(pc_full, w + 2)
                        act.activation(cT_hi[1 - parity][:], chunked(PC), ACT.Copy).then_inc(pc_hi, 1)
                    if in_stage(w - 1):
                        act.wait_ge(pp_full, w)
                        at_least(act, out_full, w - 1)
                        act.activation(probsT[:].rearrange("p b t -> p (b t)"), PP[:, 0:TOK], ACT.Copy).then_inc(pp_ok, 1)
                    if in_stage(w):
                        act.wait_ge(ent_full, w + 1)
                        at_least(act, sc_full, w)
                        for m in range(KC):
                            last = act.activation(ent[:, m, :], ENT[:, m * TOK:(m + 1) * TOK], ACT.Tanh, bias=bias_e[:, m:m + 1])
                        last.then_inc(ent_ok, 1)
                        act.wait_ge(vt_full, w + 1)
                        for m in range(KC):
                            last = act.activation(vT[:, m, :], VT[:, m * TOK:(m + 1) * TOK], ACT.Identity,
                                                  bias=bias_in[:, 3 * KC + m:3 * KC + m + 1])
                        last.then_inc(vt_ok, 1)
                    if in_stage(w):
                        act.wait_ge(vtok_full, w + 1)
                        at_least(act, out_full, w)
                        act.activation(v_tok[:].rearrange("p b d -> p (b d)"), VTOK[:], ACT.Copy).then_inc(vtok_ok, 1)
                    for i in next_pieces(w, following):
                        following.act_piece(act, i)
                windows(act, window)

            @block.vector
            def _(dve):
                dve.wait_ge(folded, 1)
                wt.wait_in(dve)
                dve.tensor_tensor(bias_e[:], bias_in[:, 2 * KC:3 * KC], OUT[:, 0:KC], ALU.add).then_inc(fold_ok, 1)
                dve.wait_ge(hi_ok, 1)
                dve.tensor_tensor(w_lo[:], fold[:], f32(w_hi[:]), ALU.subtract).then_inc(w_ok, 1)

                def window(w, parity):
                    if in_stage(w - 1):
                        dve.wait_ge(sc_full, w)
                        at_least(dve, exp_ok, w - 1)
                        dve.tensor_reduce(top[:], SC[:, 0:TOK].rearrange("p (b t) -> p b t", b=PAIR), AXX, ALU.max).then_inc(top_ok, 1)
                        dve.wait_ge(top_ok, w)
                        dve.tensor_scalar(shift[:], top[:], -(D ** -0.5), None, ALU.mult).then_inc(shift_ok, 1)
                    if in_stage(w + 2):
                        ln.dve_moments(dve, w + 2)
                    if in_stage(w + 1):
                        ln.dve_low(dve, w + 1, 1 - parity)
                        dve.wait_ge(pc_hi, w + 2)
                        dve.tensor_tensor(cT_lo[1 - parity][:], chunked(PC), f32(cT_hi[1 - parity][:]), ALU.subtract).then_inc(pc_lo, 1)
                    if in_stage(w + 2):
                        ln.dve_normalise(dve, w + 2)
                    if in_stage(w - 1):
                        dve.wait_ge(exp_ok, w)
                        dve.reciprocal(inv_total[:], total[:]).then_inc(inv_ok, 1)
                        dve.wait_ge(inv_ok, w)
                        dve.wait_ge(out_full, w)
                        for b in range(PAIR):
                            last = dve.scalar_tensor_tensor(ln.x(w - 1, b), OUT[:, b * D:(b + 1) * D], inv_total[:, b:b + 1],
                                                            ln.x(w - 1, b), op0=ALU.mult, op1=ALU.add)
                        last.then_inc(out_ok, 1)
                    for i in next_pieces(w, following):
                        following.dve_piece(dve, i)
                windows(dve, window)

            @block.tensor
            def _(pe):
                wt.wait_in(pe)
                for n, bank in enumerate((ENT, VT)):
                    for m in range(KC):
                        for k in range(KC):
                            pe.matmul(bank[:, m * D:(m + 1) * D], w_raw[:, k, n * D + m * P:n * D + (m + 1) * P],
                                      w_raw[:, k, (2 + n) * D:(3 + n) * D], start=(k == 0), stop=(k == KC - 1))
                for m in range(KC):
                    for j in range(2 * KC):
                        n, k = j // KC, j % KC
                        last = pe.matmul(OUT[:, m:m + 1], w_raw[:, k, (2 + n) * D + m * P:(2 + n) * D + (m + 1) * P],
                                         bias_in[:, n * KC + k:n * KC + k + 1], start=(j == 0), stop=(j == 2 * KC - 1))
                last.then_inc(folded, 1)

                def window(w, parity):
                    if in_stage(w - 1):
                        pe.wait_ge(vt_ok, w)
                        at_least(pe, exp_ok, w - 1)
                        for b in range(PAIR):
                            for k in range(KC):
                                last = pe.matmul(SC[:, b * P:(b + 1) * P], ent[:, k, b * P:(b + 1) * P],
                                                 vT[:, k, b * P:(b + 1) * P], start=(k == 0), stop=(k == KC - 1))
                        last.then_inc(sc_full, 1)
                    if in_stage(w + 1):
                        ln.pe_transpose(pe, w + 1)
                        pe.wait_ge(cx_in[1 - parity], 16 * ((w + 1) // 2 + 1) if isinstance(w, int) else cx_count(w + 1, 1 - parity))
                        at_least(pe, pc_lo, w + 1)
                        for c in range(KC):
                            for b in range(PAIR):
                                last = pe.transpose(PC[:, c * TOK + b * P:c * TOK + (b + 1) * P],
                                                    cx[1 - parity][:, b, c * P:(c + 1) * P], consts["ident"][:])
                        last.then_inc(pc_full, 1)
                    if in_stage(w):
                        hi, lo, chi, clo = ln.hi[parity], ln.lo[parity], cT_hi[parity], cT_lo[parity]
                        if isinstance(w, int) and w == 0:
                            pe.wait_ge(w_ok, 1)
                        pe.wait_ge(ln.lo_ok, w + 1)
                        pe.wait_ge(pc_lo, w + 1)
                        at_least(pe, ent_ok, w)
                        for m in range(KC):
                            eq, ek = slice(m * P, (m + 1) * P), slice(D + m * P, D + (m + 1) * P)
                            last = three_pass(pe, ENT[:, m * TOK:(m + 1) * TOK],
                                              lambda k: w_hi[:, k, eq] if k < KC else w_hi[:, k - KC, ek],
                                              lambda k: w_lo[:, k, eq] if k < KC else w_lo[:, k - KC, ek],
                                              lambda k: hi[:, k, :] if k < KC else chi[:, k - KC, :],
                                              lambda k: lo[:, k, :] if k < KC else clo[:, k - KC, :], 2 * KC)
                        last.then_inc(ent_full, 1)
                    if in_stage(w - 1):
                        pe.wait_ge(exp_ok, w)
                        at_least(pe, pp_ok, w - 1)
                        for b in range(PAIR):
                            last = pe.transpose(PP[:, b * P:(b + 1) * P], probs[:, b, :], consts["ident"][:])
                        last.then_inc(pp_full, 1)
                    if in_stage(w):
                        at_least(pe, vt_ok, w)
                        for m in range(KC):
                            ev = slice(2 * D + m * P, 2 * D + (m + 1) * P)
                            last = three_pass(pe, VT[:, m * TOK:(m + 1) * TOK], lambda k: w_hi[:, k, ev], lambda k: w_lo[:, k, ev],
                                              lambda k: chi[:, k, :], lambda k: clo[:, k, :], KC)
                        last.then_inc(vt_full, 1)
                    if in_stage(w - 1):
                        pe.wait_ge(pp_ok, w)
                        pe.wait_ge(vtok_ok, w)
                        at_least(pe, out_ok, w - 1)
                        for b in range(PAIR):
                            last = pe.matmul(OUT[:, b * D:(b + 1) * D], probsT[:, b, :], v_tok[:, b, :], start=True, stop=True)
                        last.then_inc(out_full, 1)
                    if in_stage(w):
                        pe.wait_ge(vt_ok, w + 1)
                        at_least(pe, vtok_ok, w)
                        for b in range(PAIR):
                            for c in range(KC):
                                last = pe.transpose(VTOK[:, b * D + c * P:b * D + (c + 1) * P],
                                                    vT[:, c, b * P:(b + 1) * P], consts["ident"][:])
                        last.then_inc(vtok_full, 1)
                windows(pe, window)
        nm.clear_semaphores()


def routed_stage(nc, name, x_res, consts, a, wt, following, x_dram=None):
    FC = F // P
    ER = E * R
    GA = E + ER
    with ExitStack() as ctx:
        nm = Names(nc, ctx, name)
        sb, sem = nm.sb, nm.sem
        PT, RT, LT, OUT = (nm.ps(n) for n in ("PT", "RT", "LT", "OUT"))
        HB = [nm.ps(f"HB{i}") for i in range(2)]
        x_in = sem("x_in")
        ln = Normed(nm, consts, x_res, PT, x_in if x_dram is not None else None, 16)
        if not wt.prepared:
            wt.stage(nm)
        following.stage(nm)
        wi_hi, wi_lo, wo_hi, wo_lo, b_parts = wt.wi_hi, wt.wi_lo, wt.wo_hi, wt.wo_lo, wt.b_parts
        gate_row, bias_i, row_o, expert_of = wt.gate_row, wt.bias_i, wt.row_o, wt.expert_of
        route_mark = sb("route_mark", [P, 1])
        logits, top8 = sb("logits", [P, PAIR, E]), sb("top8", [P, PAIR, 8])
        top_at, top1 = sb("top_at", [P, PAIR, 8], U32), sb("top1", [P, PAIR])
        low32, low_hi = sb("low32", [P, PAIR, ER]), sb("low_hi", [P, PAIR, ER], F32R)
        low_parts = sb("low_parts", [P, PAIR, 3 * ER])
        lowT = [sb(f"lowT{i}", [3 * ER, TOK], F32R) for i in range(2)]
        h32 = [sb(f"h32_{i}", [P, 2 * TOK]) for i in range(2)]
        h_hi = [sb(f"h_hi{i}", [P, FC // 2, 2 * TOK], F32R) for i in range(2)]
        h_lo = [sb(f"h_lo{i}", [P, FC // 2, 2 * TOK], F32R) for i in range(2)]
        biased = sem("biased")
        rt_full, link, low_ok, lt_full, lt_ok = (sem(n) for n in ("rt_full", "link", "low_ok", "lt_full", "lt_ok"))
        hb_full, relu_ok, hhi_ok, hlo_ok, out_full, out_ok = (sem(n) for n in ("hb_full", "relu_ok", "hhi_ok", "hlo_ok", "out_full", "out_ok"))
        HALVES = FC // 2
        LINKS = 11

        with nc.Block() as block:

            @block.sync
            def _(sp):
                if x_dram is not None:
                    sp.dma_start(x_res[:], x_dram).then_inc(x_in, 16)
                if not wt.prepared:
                    wt.load(sp)
                following.load(sp)

            @block.gpsimd
            def _(pool):
                wt.wait_in(pool)

                def window(w):
                    ln.pool_rstd(pool, w)
                    pool.wait_ge(ln.xn_ok, w + 1)
                    pool.tensor_tensor(ln.x_group(w), ln.x_group(w), row_o[:], ALU.add).then_inc(biased, 1)
                window(0)
                with pool.Fori(1, NG) as w:
                    window(w)

            @block.scalar
            def _(act):
                if not wt.prepared:
                    wt.prepare_act(act)
                wt.wait_in(act)

                def window(w, parity):
                    if in_stage(w + 1):
                        ln.act_high(act, w + 1, 1 - parity, hb_full, HALVES)
                    for n in range(HALVES):
                        if in_stage(w):
                            T = w * HALVES + n
                            act.wait_ge(hb_full, T + 1)
                            at_least(act, hlo_ok, T - 1)
                            for m in range(2):
                                f = 2 * n + m
                                last = act.activation(h32[n % 2][:, m * TOK:(m + 1) * TOK], HB[n % 2][:, m * TOK:(m + 1) * TOK],
                                                      ACT.Relu, bias=bias_i[:, f:f + 1])
                            last.then_inc(relu_ok, 1)
                            if n == 0:
                                at_least(act, out_full, w - 1)
                            act.wait_ge(relu_ok, T + 1)
                            act.activation(h_hi[parity][:, n, :], h32[n % 2][:], ACT.Copy).then_inc(hhi_ok, 1)
                    if in_stage(w + 1):
                        act.wait_ge(lt_full, w + 2)
                        at_least(act, hb_full, w * HALVES)
                        act.activation(lowT[1 - parity][:], LT[0:3 * ER, 0:TOK], ACT.Copy).then_inc(lt_ok, 1)
                    for i in next_pieces(w, following):
                        following.act_piece(act, i)
                windows(act, window)

            @block.vector
            def _(dve):
                if not wt.prepared:
                    wt.prepare_dve(dve)
                wt.wait_in(dve)

                def route(w):
                    done = [0]

                    def step(*instructions, apart=False):
                        for ins in instructions:
                            done[0] += 1
                            ins.then_inc(link, 1)
                        if apart:
                            wait_apart(dve, link, w * LINKS + done[0], route_mark)
                            done[0] += 1
                        else:
                            dve.wait_ge(link, w * LINKS + done[0])
                    dve.wait_ge(rt_full, w + 1)
                    rt = RT[:, 0:PAIR * GA].rearrange("p (b n) -> p b n", b=PAIR)
                    at_least(dve, lt_full, w)
                    step(dve.tensor_tensor(logits[:], rt[:, :, 0:E], gate_row[:], ALU.add), apart=True)
                    step(*(dve.max(top8[:, b, :], logits[:, b, :]) for b in range(PAIR)), apart=True)
                    step(*(dve.max_index(top_at[:, b, :], top8[:, b, :], logits[:, b, :]) for b in range(PAIR)))
                    step(dve.tensor_copy(top1[:], top_at[:, :, 0]))
                    step(*(dve.scalar_tensor_tensor(low32[:, b, :], expert_of[:], top1[:, b:b + 1], rt[:, b, E:],
                                                    op0=ALU.is_equal, op1=ALU.mult) for b in range(PAIR)))
                    step(dve.tensor_copy(low_hi[:], low32[:]))
                    dve.tensor_tensor(low_parts[:, :, 2 * ER:], low32[:], f32(low_hi[:]), ALU.subtract)
                    dve.tensor_copy(low_parts[:, :, 0:ER], f32(low_hi[:]))
                    dve.tensor_copy(low_parts[:, :, ER:2 * ER], f32(low_hi[:])).then_inc(low_ok, 1)

                def window(w, parity):
                    if in_stage(w + 1):
                        ln.dve_low(dve, w + 1, 1 - parity)
                    for n in range(HALVES):
                        if in_stage(w):
                            T = w * HALVES + n
                            dve.wait_ge(hhi_ok, T + 1)
                            dve.tensor_tensor(h_lo[parity][:, n, :], h32[n % 2][:], f32(h_hi[parity][:, n, :]),
                                              ALU.subtract).then_inc(hlo_ok, 1)
                        if n == 0 and in_stage(w + 2):
                            ln.dve_moments(dve, w + 2)
                        if n == 1 and in_stage(w + 2):
                            ln.dve_normalise(dve, w + 2)
                        if n == 2 and in_stage(w + 1):
                            route(w + 1)
                    if in_stage(w - 1):
                        dve.wait_ge(out_full, w)
                        dve.wait_ge(biased, w)
                        dve.tensor_tensor(ln.x_group(w - 1), ln.x_group(w - 1),
                                          OUT[:].rearrange("p (b d) -> p b d", b=PAIR), ALU.add).then_inc(out_ok, 1)
                    for i in next_pieces(w, following):
                        following.dve_piece(dve, i)
                windows(dve, window)

            @block.tensor
            def _(pe):
                wt.wait_split(pe)

                def window(w, parity):
                    if in_stage(w + 1):
                        ln.pe_transpose(pe, w + 1)
                    if in_stage(w):
                        hi, lo = ln.hi[parity], ln.lo[parity]
                        for n in range(HALVES):
                            T = w * HALVES + n
                            at_least(pe, relu_ok, T - 1)
                            if n == 0:
                                pe.wait_ge(ln.lo_ok, w + 1)
                                pe.wait_ge(lt_ok, w + 1)
                            for m in range(2):
                                out = HB[n % 2][:, m * TOK:(m + 1) * TOK]
                                fs = slice((2 * n + m) * P, (2 * n + m + 1) * P)
                                for k in range(KC):
                                    pe.matmul(out, wi_hi[:, k, fs], hi[:, k, :], start=(k == 0), stop=False)
                                    pe.matmul(out, wi_lo[:, k, fs], hi[:, k, :], start=False, stop=False)
                                    pe.matmul(out, wi_hi[:, k, fs], lo[:, k, :], start=False, stop=False)
                                last = pe.matmul(out, b_parts[:, fs], lowT[parity][:], start=False, stop=True)
                            last.then_inc(hb_full, 1)
                    if in_stage(w + 1):
                        hi, lo = ln.hi[1 - parity], ln.lo[1 - parity]
                        pe.wait_ge(ln.lo_ok, w + 2)
                        at_least(pe, low_ok, w + 1)
                        for b in range(PAIR):
                            tok = slice(b * P, (b + 1) * P)
                            last = three_pass(pe, RT[:, b * GA:(b + 1) * GA], lambda k: hi[:, k, tok], lambda k: lo[:, k, tok],
                                              lambda k: wi_hi[:, k, F:], lambda k: wi_lo[:, k, F:], KC)
                        last.then_inc(rt_full, 1)
                    if in_stage(w - 1):
                        pe.wait_ge(hlo_ok, w * HALVES)
                        at_least(pe, out_ok, w - 1)
                        h, l = h_hi[1 - parity], h_lo[1 - parity]
                        for b in range(PAIR):
                            def chunk(t, k, b=b):
                                return t[:, k // 2, (k % 2) * TOK + b * P:(k % 2) * TOK + (b + 1) * P]
                            last = three_pass(pe, OUT[:, b * D:(b + 1) * D], lambda k: chunk(h, k), lambda k: chunk(l, k),
                                              lambda k: wo_hi[:, k, :], lambda k: wo_lo[:, k, :], FC)
                        last.then_inc(out_full, 1)
                    if in_stage(w + 1):
                        pe.wait_ge(low_ok, w + 2)
                        at_least(pe, lt_ok, w + 1)
                        for b in range(PAIR):
                            last = pe.transpose(LT[0:3 * ER, b * P:(b + 1) * P], low_parts[:, b, :], consts["ident"][:])
                        last.then_inc(lt_full, 1)
                windows(pe, window)
        nm.clear_semaphores()


def ternary_stage(nc, name, x_res, consts, wt, x_dram=None, out_dram=None):
    FC = F // P
    HB_COLS = 512
    HALVES = F // HB_COLS
    with ExitStack() as ctx:
        nm = Names(nc, ctx, name)
        sb, sem = nm.sb, nm.sem
        PT, OUT = nm.ps("PT"), nm.ps("OUT")
        HB = [nm.ps(f"HB{i}") for i in range(2)]
        ZT = [nm.ps(f"ZT{i}") for i in range(4)]
        x_in = sem("x_in")
        ln = Normed(nm, consts, x_res, PT, x_in if x_dram is not None else None, 16)
        if not wt.prepared:
            wt.stage(nm)
        raw, sums, gain, offset = wt.raw, wt.sums, wt.gain, wt.offset
        quant = [sb("fc_q", [P, KC, F], F32R), sb("proj_q", [P, FC, D], F32R)]
        below = sb("below", [P, KC * F])
        total, level = sb("total", [P, 2]), sb("level", [P, 2, 2])
        hid = [[sb(f"hid{i}{b}", [P, F]) for b in range(PAIR)] for i in range(2)]
        z = [sb(f"z{b}", [P, F]) for b in range(PAIR)]
        h_stats, h_moments = sb("h_stats", [P, PAIR, HALVES, 6]), sb("h_moments", [P, PAIR, 2])
        h_var, h_rstd = sb("h_var", [P, PAIR]), sb("h_rstd", [P, PAIR])
        y32 = [sb(f"y32_{i}", [P, 2 * TOK]) for i in range(FC // 2)]
        y_hi, y_lo = sb("y_hi", [P, FC // 2, 2 * TOK], F32R), sb("y_lo", [P, FC // 2, 2 * TOK], F32R)
        hs_mark = sb("hs_mark", [P, 1])
        total_ok, level_ok, below_ok, quant_ok = (sem(n) for n in ("total_ok", "level_ok", "below_ok", "quant_ok"))
        hb_full, gelu_ok, hs_link, hvar_ok, hrstd_ok, z_ok = (
            sem(n) for n in ("hb_full", "gelu_ok", "hs_link", "hvar_ok", "hrstd_ok", "z_ok"))
        zt_full, y_ok, yhi_ok, out_full, out_ok, stored = (sem(n) for n in ("zt_full", "y_ok", "yhi_ok", "out_full", "out_ok", "stored"))
        ylo_ok = [sem("ylo_first_ok"), sem("ylo_last_ok")]
        PARTS = FC // 2
        FILLS = PAIR * HALVES
        LINKS = FILLS + 1 + PAIR

        def low_part(eng, w, n):
            eng.wait_ge(yhi_ok, w * PARTS + n + 1)
            eng.tensor_tensor(y_lo[:, n, :], y32[n][:], f32(y_hi[:, n, :]), ALU.subtract).then_inc(ylo_ok[n // 2], 1)

        with nc.Block() as block:

            @block.sync
            def _(sp):
                if x_dram is not None:
                    sp.dma_start(x_res[:], x_dram).then_inc(x_in, 16)
                if not wt.prepared:
                    wt.load(sp)

                def store(w):
                    sp.wait_ge(out_ok, w + 1)
                    dst = out_dram[:, w * PAIR:(w + 1) * PAIR, :] if isinstance(w, int) else \
                        out_dram[:, bass.ds(w * PAIR, PAIR), :]
                    sp.dma_start(dst, ln.x_group(w)).then_inc(stored, 16)
                with sp.Fori(0, NG) as w:
                    store(w)
                sp.wait_ge(stored, 16 * NG)

            @block.gpsimd
            def _(pool):
                def window(w, parity):
                    if in_stage(w + 2):
                        ln.pool_rstd(pool, w + 2)
                    if in_stage(w - 1):
                        low_part(pool, w - 1, 0)
                    if in_stage(w - 1):
                        low_part(pool, w - 1, 1)
                    if in_stage(w):
                        pool.wait_ge(hs_link, w * LINKS + LINKS)
                        at_least(pool, z_ok, w * PAIR)
                        pool.tensor_tensor(h_var[:], h_moments[:, :, 1], consts["ln_eps"][:], ALU.add).then_inc(hvar_ok, 1)
                        pool.wait_ge(hvar_ok, w + 1)
                        pool.tensor_tensor(h_rstd[:], h_var[:], consts["minus_half"][:], ALU.pow).then_inc(hrstd_ok, 1)
                windows(pool, window)

            @block.scalar
            def _(act):
                if not wt.prepared:
                    wt.prepare_act(act)
                wt.wait_in(act)

                def activate(w, n, parity):
                    at_least(act, z_ok, (w - 1) * PAIR)
                    act.wait_ge(hb_full, w * FILLS + n + 1)
                    act.activation(hid[parity][n // HALVES][:, (n % HALVES) * HB_COLS:(n % HALVES + 1) * HB_COLS],
                                   HB[n % 2][:], ACT.Gelu).then_inc(gelu_ok, 1)

                def rescale(w, n):
                    T = w * PARTS + n
                    act.wait_ge(zt_full, T + 1)
                    at_least(act, ylo_ok[n // 2], (w - 1) * 2 + n % 2 + 1)
                    for m in range(2):
                        f = 2 * n + m
                        last = act.activation(y32[n][:, m * TOK:(m + 1) * TOK], ZT[n][:, m * TOK:(m + 1) * TOK],
                                              ACT.Identity, bias=offset[:, f:f + 1], scale=gain[:, f:f + 1])
                    last.then_inc(y_ok, 1)
                    if n == 0:
                        at_least(act, out_full, w)
                    act.wait_ge(y_ok, T + 1)
                    act.activation(y_hi[:, n, :], y32[n][:], ACT.Copy).then_inc(yhi_ok, 1)

                def window(w, parity):
                    if in_stage(w + 1):
                        ln.act_high(act, w + 1, 1 - parity, hb_full, FILLS)
                    if in_stage(w):
                        activate(w, 0, parity)
                    for n in range(PARTS):
                        if in_stage(w) and n + 1 < FILLS:
                            activate(w, n + 1, parity)
                        if in_stage(w - 1):
                            rescale(w - 1, n)
                windows(act, window)

            @block.vector
            def _(dve):
                wt.wait_in(dve)
                def levels():
                    dve.wait_ge(total_ok, 1)
                    dve.tensor_reduce(total[:], OUT[:, 0:4].rearrange("p (n h) -> p n h", n=2), AXX, ALU.add).then_inc(level_ok, 1)
                    dve.wait_ge(level_ok, 1)
                    dve.tensor_scalar(level[:, :, 0], total[:], 1.0 / (F * D), ABSMEAN_EPS, ALU.mult, ALU.add).then_inc(level_ok, 1)
                    dve.wait_ge(level_ok, 2)
                    dve.tensor_scalar(level[:, :, 1], level[:, :, 0], -0.5, None, ALU.mult).then_inc(level_ok, 1)
                    dve.wait_ge(level_ok, 3)
                    dve.tensor_scalar(level[:, :, 0], level[:, :, 0], 0.5, None, ALU.mult).then_inc(level_ok, 1)
                    dve.wait_ge(level_ok, 4)

                def quantise(n):
                    at_least(dve, quant_ok, n)
                    dve.tensor_scalar(below[:], raw[n][:], level[:, n, 1:2], None, ALU.is_lt).then_inc(below_ok, 1)
                    dve.wait_ge(below_ok, n + 1)
                    dve.scalar_tensor_tensor(quant[n][:].rearrange("p k n -> p (k n)"), raw[n][:], level[:, n, 0:1], below[:],
                                             op0=ALU.is_gt, op1=ALU.subtract).then_inc(quant_ok, 1)

                def spread(w, n, parity):
                    dve.wait_ge(gelu_ok, w * FILLS + n + 1)
                    b, half = n // HALVES, n % HALVES
                    dve.bn_stats(h_stats[:, b, half, :], hid[parity][b][:, half * HB_COLS:(half + 1) * HB_COLS]).then_inc(hs_link, 1)

                def window(w, parity):
                    if in_stage(w - 1):
                        dve.wait_ge(hrstd_ok, w)
                        at_least(dve, zt_full, (w - 1) * PARTS)
                        for b in range(PAIR):
                            dve.tensor_scalar(z[b][:], hid[1 - parity][b][:], h_moments[:, b, 0:1], h_rstd[:, b:b + 1],
                                              ALU.subtract, ALU.mult).then_inc(z_ok, 1)
                    if in_stage(w + 1):
                        ln.dve_low(dve, w + 1, 1 - parity)
                    if in_stage(w):
                        spread(w, 0, parity)
                        spread(w, 1, parity)
                    if in_stage(w + 2):
                        ln.dve_moments(dve, w + 2)
                    if in_stage(w - 2):
                        dve.wait_ge(out_full, w - 1)
                        dve.tensor_tensor(ln.x_group(w - 2), ln.x_group(w - 2),
                                          OUT[:].rearrange("p (b d) -> p b d", b=PAIR), ALU.add).then_inc(out_ok, 1)
                    if in_stage(w + 2):
                        ln.dve_normalise(dve, w + 2)
                    if in_stage(w):
                        spread(w, 2, parity)
                        spread(w, 3, parity)
                        wait_apart(dve, hs_link, w * LINKS + FILLS, hs_mark)
                        for b in range(PAIR):
                            dve.bn_aggr(h_moments[:, b, :], h_stats[:, b].rearrange("p h s -> p (h s)")).then_inc(hs_link, 1)
                    if in_stage(w - 1):
                        low_part(dve, w - 1, 2)
                    if in_stage(w - 1):
                        low_part(dve, w - 1, 3)
                    if isinstance(w, int) and w == -2:
                        levels()
                        quantise(0)
                    if isinstance(w, int) and w == 0:
                        quantise(1)
                windows(dve, window, NG + 1)

            @block.tensor
            def _(pe):
                pe.wait_ge(wt.hi_ok, len(wt.pieces))
                pe.matmul(OUT[:, 0:4], consts["ones"][:], sums[:], start=True, stop=True).then_inc(total_ok, 1)

                def expand(w, n, parity):
                    at_least(pe, gelu_ok, w * FILLS + n - 1)
                    tok = slice((n // HALVES) * P, (n // HALVES + 1) * P)
                    cols = slice((n % HALVES) * HB_COLS, (n % HALVES + 1) * HB_COLS)
                    for k in range(KC):
                        pe.matmul(HB[n % 2][:], ln.hi[parity][:, k, tok], quant[0][:, k, cols], start=(k == 0), stop=False)
                        last = pe.matmul(HB[n % 2][:], ln.lo[parity][:, k, tok], quant[0][:, k, cols], start=False, stop=(k == KC - 1))
                    last.then_inc(hb_full, 1)

                def turn(w, n):
                    at_least(pe, y_ok, (w - 1) * PARTS + n + 1)
                    for m in range(2):
                        for b in range(PAIR):
                            f = 2 * n + m
                            last = pe.transpose(ZT[n][:, m * TOK + b * P:m * TOK + (b + 1) * P], z[b][:, f * P:(f + 1) * P],
                                                consts["ident"][:])
                    last.then_inc(zt_full, 1)

                def window(w, parity):
                    if in_stage(w + 1):
                        ln.pe_transpose(pe, w + 1)
                    if in_stage(w):
                        pe.wait_ge(ln.lo_ok, w + 1)
                        if isinstance(w, int) and w == 0:
                            pe.wait_ge(quant_ok, 1)
                        expand(w, 0, parity)
                        expand(w, 1, parity)
                    if in_stage(w - 2):
                        at_least(pe, out_ok, w - 2)
                        if isinstance(w, int) and w == 2:
                            pe.wait_ge(quant_ok, 2)
                        for k in range(FC):
                            part = k // 2
                            if k % 2 == 0:
                                pe.wait_ge(yhi_ok, (w - 2) * PARTS + part + 1)
                                pe.wait_ge(ylo_ok[part // 2], (w - 2) * 2 + part % 2 + 1)
                            for b in range(PAIR):
                                cols = slice((k % 2) * TOK + b * P, (k % 2) * TOK + (b + 1) * P)
                                for y in (y_hi, y_lo):
                                    last = pe.matmul(OUT[:, b * D:(b + 1) * D], y[:, part, cols], quant[1][:, k, :],
                                                     start=(k == 0 and b == 0 and y is y_hi), stop=(k == FC - 1 and b == PAIR - 1 and y is y_lo))
                        last.then_inc(out_full, 1)
                    if in_stage(w - 1):
                        pe.wait_ge(z_ok, w * PAIR)
                    for n in range(PARTS):
                        if in_stage(w) and 0 < n < FILLS - 1:
                            expand(w, n + 1, parity)
                        if in_stage(w - 1):
                            turn(w - 1, n)
                windows(pe, window, NG + 1)
        nm.clear_semaphores()


def decoder(nc, a, out, stages=6, only=None):
    def wanted(n):
        return (n in only if isinstance(only, tuple) else n == only) if only is not None else n <= stages

    def x_of(n):
        return a["x"] if n == (only[0] if isinstance(only, tuple) else only or 1) else None

    with ExitStack() as ctx:
        nm = Names(nc, ctx, "all")
        x_res = nm.sb("x_res", [P, NB, D])
        consts = {
            "ident": nm.sb("ident", [P, P]), "head_mask": nm.sb("head_mask", [P, QH]),
            "half_ones": nm.sb("half_ones", [P, 2, 2 * DH]), "turn_sign": nm.sb("turn_sign", [P, 1]),
            "ones": nm.sb("ones", [P, P]), "minus_half": nm.sb("minus_half", [P, PAIR]),
            "ln_eps": nm.sb("ln_eps", [P, PAIR]),
            "ident_b": nm.sb("ident_b", [P, P], BF16), "neg_ident_b": nm.sb("neg_ident_b", [P, P], BF16),
        }
        consts_in = nm.sem("consts_in")
        with nc.Block() as block:

            @block.sync
            def _(sp):
                for k in ("ident", "head_mask", "half_ones", "turn_sign"):
                    sp.dma_start(consts[k][:], a[k]).then_inc(consts_in, 16)

            @block.vector
            def _(dve):
                dve.memset(consts["minus_half"][:], -0.5)
                dve.memset(consts["ln_eps"][:], LN_EPS)
                dve.memset(consts["ones"][:], 1.0)
                dve.wait_ge(consts_in, 64)
                dve.tensor_copy(consts["ident_b"][:], consts["ident"][:])
                dve.tensor_scalar(consts["neg_ident_b"][:], consts["ident"][:], -1.0, None, ALU.mult)

        odd = nm.sb("odd_weights", [P, 4 + 2 * PAIR * D + TOK]), nm.sb("odd_split", [P, 2 * KC * GATED + 2 * F * D // P + F], F32R)
        even = nm.sb("even_weights", [P, 2 * F * D // P + 2 * F // P + 4]), nm.sb("even_split", [P, 2 * KC * 4 * D], F32R)

        def spare():
            return Arena(*odd, used=(odd[0].shape[1], 2 * KC * 4 * D))
        L0_attn = AttentionWeights(nm, "a0", Arena(*odd), [(0, a["L0_attn_Wqkv"]), (3, a["L0_attn_Wout"])],
                                   [("bias_cols", a["L0_attn_bqk"]), ("row_v", a["L0_attn_bv"]), ("row_o", a["L0_attn_bout"]),
                                    ("q_mul", a["emb"]), ("w_turned", a["L0_attn_Wturned"]), ("bias_turned", a["L0_attn_bturned"])],
                                   rope=True)
        L0_xattn = EntangledWeights(nm, "b0", Arena(*even), a)
        L0_ffn = RoutedWeights(nm, "c0", Arena(*odd), a)
        L1_attn = AttentionWeights(nm, "a1", Arena(*even), [(0, a["L1_attn_W_query"]), (1, a["L1_attn_W_key"]),
                                                                (2, a["L1_attn_W_val"]), (3, a["L1_attn_W_out"])], [])
        L1_xattn = AttentionWeights(nm, "a2", Arena(*odd), [(0, a["L1_xattn_wq"]), (1, a["L1_xattn_wk"]),
                                                                 (2, a["L1_xattn_wv"]), (3, a["L1_xattn_wo"])],
                                    [("bias_cols", a["L1_xattn_bqk"]), ("row_v", a["L1_xattn_bv"]), ("row_o", a["L1_xattn_bo"])])
        L1_ffn = TernaryWeights(nm, "d1", Arena(*even), a)
        weights = [L0_attn, L0_xattn, L0_ffn, L1_attn, L1_xattn, L1_ffn]
        for n in range(2, 7):
            weights[n - 1].prepared = wanted(n - 1) and wanted(n)
        if wanted(1):
            attention_stage(nc, "a0", x_res, consts, L0_attn, L0_xattn, spare(), rope=True, v_bias=True, o_bias=True, x_dram=x_of(1))
        if wanted(2):
            entangled_stage(nc, "b0", x_res, consts, a, L0_xattn, L0_ffn, x_dram=x_of(2))
        if wanted(3):
            routed_stage(nc, "c0", x_res, consts, a, L0_ffn, L1_attn, x_dram=x_of(3))
        if wanted(4):
            attention_stage(nc, "a1", x_res, consts, L1_attn, L1_xattn, spare(), x_dram=x_of(4))
        if wanted(5):
            attention_stage(nc, "a2", x_res, consts, L1_xattn, L1_ffn, spare(), ctx_dram=a["ctx"], mask_dram=a["mask"],
                            k_bias=True, v_bias=True, o_bias=True, x_dram=x_of(5))
        if wanted(6):
            ternary_stage(nc, "d1", x_res, consts, L1_ffn, x_dram=x_of(6), out_dram=out)
            return
        stored = nm.sem("stored")
        with nc.Block() as block:

            @block.sync
            def _(sp):
                for n in range(4):
                    part = slice(n * NB // 4, (n + 1) * NB // 4)
                    sp.dma_start(out[:, part, :], x_res[:, part, :]).then_inc(stored, 16)
                sp.wait_ge(stored, 64)


def layout(inputs):
    g = {k: np.asarray(v) for k, v in inputs.items()}

    def chunks(w):
        return w.reshape(-1, P, w.shape[1]).transpose(1, 0, 2)

    def cols(*bs):
        return np.concatenate([b.reshape(-1, P).T for b in bs], axis=1)

    def row(b, n=PAIR):
        return np.broadcast_to(b, (P, n, b.shape[0]))

    def out_rows(w):
        return w.reshape(KC, 2, QH, DH, D).transpose(0, 2, 1, 3, 4).reshape(D, D)

    turned = np.array([h * DH + (2 * j + 1 if j < DH // 2 else 2 * (j - DH // 2)) for h in range(2 * H) for j in range(DH)])
    theta = np.float32(10000.0) ** (-np.arange(0, DH, 2, dtype=np.float32) / np.float32(DH))
    freqs = np.arange(P, dtype=np.float32)[:, None] * theta[None, :]
    emb = np.concatenate([np.sin(freqs), np.cos(freqs)], axis=-1).astype(np.float32)
    p = np.arange(P)
    half_ones = np.zeros((P, 2, 2 * DH), np.float32)
    half_ones[:, 0, :DH] = 1
    half_ones[:, 1, DH:] = 1
    a = {
        "x": g["x"].transpose(1, 0, 2), "ctx": g["ctx_1024"].transpose(1, 0, 2), "mask": g["mask_SxS2_bk0"],
        "ident": np.eye(P, dtype=np.float32), "half_ones": half_ones,
        "head_mask": ((p[:, None] // DH) % QH == np.arange(QH)[None, :]).astype(np.float32),
        "turn_sign": np.where(p % DH < DH // 2, -1, 1).astype(np.float32)[:, None],
        "emb": np.tile(emb.T, (P // DH, PAIR)),
        "L0_attn_Wqkv": chunks(g["L0_attn_Wqkv"]), "L0_attn_Wturned": chunks(g["L0_attn_Wqkv"][:, turned]),
        "L0_attn_bqk": cols(g["L0_attn_bqkv"][:2 * D]), "L0_attn_bturned": cols(g["L0_attn_bqkv"][turned]),
        "L0_attn_bv": row(g["L0_attn_bqkv"][2 * D:]), "L0_attn_Wout": chunks(out_rows(g["L0_attn_Wout"])),
        "L0_attn_bout": row(g["L0_attn_bout"]),
        "L1_xattn_bqk": cols(g["L1_xattn_bq"], g["L1_xattn_bk"]), "L1_xattn_bv": row(g["L1_xattn_bv"]),
        "L1_xattn_bo": row(g["L1_xattn_bo"]), "L1_xattn_wo": chunks(out_rows(g["L1_xattn_wo"].T)),
        "L1_attn_W_out": chunks(out_rows(g["L1_attn_W_out"].reshape(D, D))),
    }
    a.update({
        "L0_xattn_Wq": chunks(g["L0_xattn_Wq"]), "L0_xattn_Wk": chunks(g["L0_xattn_Wk"]),
        "L0_xattn_Weq": chunks(g["L0_xattn_We"][:, :D].T), "L0_xattn_Wek": chunks(g["L0_xattn_We"][:, D:].T),
        "L0_xattn_Wv": chunks(g["L0_xattn_Wv"].T),
        "L0_xattn_b": cols(*(g[f"L0_xattn_b{n}"] for n in "qkev")),
        "L0_ffn_wi_W": chunks(g["L0_ffn_wi_W"].T), "L0_ffn_wo_W": chunks(g["L0_ffn_wo_W"].T),
        "L0_ffn_gA": chunks(np.concatenate([g["L0_ffn_gate_W"], g["L0_ffn_lora_A"].reshape(E * R, D)]).T),
        "L0_ffn_B": np.tile(g["L0_ffn_lora_B"].transpose(0, 2, 1).reshape(E * R, F), (3, 1)),
        "L0_ffn_gate_b": row(g["L0_ffn_gate_b"]), "L0_ffn_wi_b": cols(g["L0_ffn_wi_b"]), "L0_ffn_wo_b": row(g["L0_ffn_wo_b"]),
        "L1_ffn_W_fc": chunks(g["L1_ffn_W_fc"].T).reshape(P, -1), "L1_ffn_W_proj": chunks(g["L1_ffn_W_proj"].T).reshape(P, -1),
        "L1_ffn_ln_w": cols(g["L1_ffn_ln_w"]), "L1_ffn_ln_b": cols(g["L1_ffn_ln_b"]),
        "expert_of": np.broadcast_to((np.arange(E * R) // R).astype(np.float32), (P, E * R)),
    })
    for k in ("L1_attn_W_query", "L1_attn_W_key", "L1_attn_W_val"):
        a[k] = chunks(g[k].transpose(1, 0, 2).reshape(D, D))
    for k in ("L1_xattn_wq", "L1_xattn_wk", "L1_xattn_wv"):
        a[k] = chunks(g[k].T)
    return {k: np.ascontiguousarray(v) for k, v in a.items()}


def kernel(**inputs):
    import numpy as _np
    import concourse.bacc as _bacc
    from concourse import mybir as _mybir
    from concourse.bass_utils import run_bass_kernel_spmd as _run

    nc = _bacc.Bacc("TRN2", target_bir_lowering=False, num_devices=1)
    arrays, args = {}, {}
    for name, value in layout(inputs).items():
        arrays[f"in_{name}"] = value
        args[name] = nc.dram_tensor(f"in_{name}", value.shape, _mybir.dt.from_np(value.dtype), kind="ExternalInput").ap()
    out = nc.dram_tensor("out_x", (P, NB, D), FP32, kind="ExternalOutput").ap()
    decoder(nc, args, out)
    r = _run(nc, [arrays], core_ids=[0])
    return _np.ascontiguousarray(_np.asarray(r.results[0]["out_x"]).transpose(1, 0, 2))
```

```python
import numpy as np
import concourse.bass as bass
from concourse import mybir
from contextlib import ExitStack

FP32 = mybir.dt.float32
F32R = mybir.dt.float32r
BF16 = mybir.dt.bfloat16
U8 = mybir.dt.uint8
U32 = mybir.dt.uint32
ALU = mybir.AluOpType
ACT = mybir.ActivationFunctionType
AXX = mybir.AxisListType.X

P = 128
NB = 32
D = 256
KC = D // P
PAIR = 2
NG = NB // PAIR
TOK = PAIR * P
H, DH = 16, 16
QH = 4
NQ = H // QH
STEPS = PAIR * NQ
F = 1024
E, R = 8, 4
GATED = F + E + E * R
LN_EPS = 1e-5
LN_LINKS = 2 * PAIR + 1
ABSMEAN_EPS = 1e-6
X_SEQS = 4
X_LOADS = NB // X_SEQS
MASKED = -4.0e9


def at_least(eng, sem, value):
    if not isinstance(value, int) or value > 0:
        eng.wait_ge(sem, value)


def wait_apart(dve, link, value, mark):
    dve.wait_ge(link, value)
    dve.memset(mark[:], 0.0).then_inc(link, 1)


def cx_count(w, parity):
    return (w - parity) * 8 + 16


def f32(ap):
    return ap.bitcast(FP32)


class Names:

    def __init__(self, nc, ctx, stage, before=None):
        self.nc, self.ctx, self.stage, self.before = nc, ctx, stage, before
        self.sem_ctx, self.sems = ExitStack(), []

    def sb(self, name, shape, dt=FP32):
        return self.ctx.enter_context(self.nc.sbuf_tensor(f"{self.stage}_{name}", shape, dt))

    def ps(self, name):
        return self.ctx.enter_context(self.nc.psum_tensor(f"{self.stage}_{name}", [P, 512], FP32))

    def sem(self, name):
        handle = self.sem_ctx.enter_context(self.nc.semaphore(f"{self.stage}_{name}"))
        self.sems.append(handle)
        return handle

    def clear_before(self, pool):
        if self.before is not None:
            for handle in self.before.sems:
                pool.sem_clear(handle)

    def end(self):
        self.ctx.close()
        if self.before is not None:
            self.before.sem_ctx.close()


def three_pass(pe, out, w_hi, w_lo, m_hi, m_lo, chunks):
    last = None
    for k in range(chunks):
        for n, (w, m) in enumerate(((w_hi, m_hi), (w_lo, m_hi), (w_hi, m_lo))):
            last = pe.matmul(out, w(k), m(k), start=(k == 0 and n == 0), stop=(k == chunks - 1 and n == 2))
    return last


class Constants:

    def __init__(self, nm, a):
        self.from_dram = {k: a[k] for k in ("ident", "head_mask", "turn_sign")}
        self.tiles = {
            "ident": nm.sb("ident", [P, P]), "head_mask": nm.sb("head_mask", [P, QH]), "turn_sign": nm.sb("turn_sign", [P, 1]),
            "ones": nm.sb("ones", [P, P]), "minus_half": nm.sb("minus_half", [P, PAIR]), "ln_eps": nm.sb("ln_eps", [P, PAIR]),
            "ident_b": nm.sb("ident_b", [P, P], BF16), "neg_ident_b": nm.sb("neg_ident_b", [P, P], BF16),
        }
        self.loaded, self.ready = nm.sem("consts_loaded"), nm.sem("consts_ready")

    def load(self, sp):
        for k, src in self.from_dram.items():
            sp.dma_start(self.tiles[k][:], src).then_inc(self.loaded, 16)

    def prepare(self, dve):
        tiles = self.tiles
        dve.memset(tiles["minus_half"][:], -0.5)
        dve.memset(tiles["ln_eps"][:], LN_EPS)
        dve.memset(tiles["ones"][:], 1.0)
        dve.wait_ge(self.loaded, 16 * len(self.from_dram))
        dve.tensor_copy(tiles["ident_b"][:], tiles["ident"][:])
        dve.tensor_scalar(tiles["neg_ident_b"][:], tiles["ident"][:], -1.0, None, ALU.mult).then_inc(self.ready, 1)


class GroupNorm:

    def __init__(self, sems, stage, x_res, consts, buffers):
        self.x_res, self.minus_half, self.eps = x_res, consts["minus_half"], consts["ln_eps"]
        self.ident = consts["ident"]
        self.stats, self.moments, self.mark, self.var_eps, self.rstd, self.xn, self.hi, self.lo = buffers
        self.link, self.var_ok, self.rstd_ok, self.xn_ok, self.full, self.hi_ok, self.lo_ok = (
            sems.sem(f"{stage}_{n}") for n in ("ln_link", "var_ok", "rstd_ok", "xn_ok", "pt_full", "pt_hi", "pt_lo"))

    @staticmethod
    def buffers(nm, parity):
        return [nm.sb(f"{name}{parity}", shape, dt) for name, shape, dt in (
            ("stats", [P, PAIR, 6], FP32), ("moments", [P, PAIR, 2], FP32), ("ln_mark", [P, 1], FP32),
            ("var_eps", [P, PAIR], FP32), ("rstd", [P, PAIR], FP32), ("xn", [P, PAIR, D], FP32),
            ("xT_hi", [P, KC, TOK], F32R), ("xT_lo", [P, KC, TOK], F32R))]

    def x(self, w, b):
        return self.x_res[:, w * PAIR + b, :] if isinstance(w, int) else \
            self.x_res[:, bass.ds(w * PAIR + b, 1), :].rearrange("p b d -> p (b d)")

    def x_group(self, w):
        return self.x_res[:, w * PAIR:(w + 1) * PAIR, :] if isinstance(w, int) else \
            self.x_res[:, bass.ds(w * PAIR, PAIR), :]

    def dve_moments(self, dve, w):
        for b in range(PAIR):
            dve.bn_stats(self.stats[:, b, :], self.x(w, b)).then_inc(self.link, 1)
        wait_apart(dve, self.link, w * LN_LINKS + PAIR, self.mark)
        for b in range(PAIR):
            dve.bn_aggr(self.moments[:, b, :], self.stats[:, b, :]).then_inc(self.link, 1)

    def pool_rstd(self, pool, w):
        pool.wait_ge(self.link, (w + 1) * LN_LINKS)
        at_least(pool, self.xn_ok, w)
        pool.tensor_tensor(self.var_eps[:], self.moments[:, :, 1], self.eps[:], ALU.add).then_inc(self.var_ok, 1)
        pool.wait_ge(self.var_ok, w + 1)
        pool.tensor_tensor(self.rstd[:], self.var_eps[:], self.minus_half[:], ALU.pow).then_inc(self.rstd_ok, 1)

    def dve_normalise(self, dve, w):
        dve.wait_ge(self.rstd_ok, w + 1)
        at_least(dve, self.full, w)
        for b in range(PAIR):
            last = dve.tensor_scalar(self.xn[:, b, :], self.x(w, b), self.moments[:, b, 0:1], self.rstd[:, b:b + 1],
                                     ALU.subtract, ALU.mult)
        last.then_inc(self.xn_ok, 1)

    def pe_transpose(self, pe, w, bank):
        pe.wait_ge(self.xn_ok, w + 1)
        for c in range(KC):
            for b in range(PAIR):
                last = pe.transpose(bank[:, c * TOK + b * P:c * TOK + (b + 1) * P], self.xn[:, b, c * P:(c + 1) * P],
                                    self.ident[:])
        last.then_inc(self.full, 1)

    def act_high(self, act, w, bank, hi=None):
        act.wait_ge(self.full, w + 1)
        act.activation((self.hi if hi is None else hi)[:], chunked(bank), ACT.Copy).then_inc(self.hi_ok, 1)

    def dve_low(self, dve, w, bank, hi=None, lo=None):
        dve.wait_ge(self.hi_ok, w + 1)
        dve.tensor_tensor((self.lo if lo is None else lo)[:], chunked(bank), f32((self.hi if hi is None else hi)[:]),
                          ALU.subtract).then_inc(self.lo_ok, 1)


class Context:

    def __init__(self, sems, stage, ctx_dram, tiles):
        self.dram, self.tiles = ctx_dram, tiles
        self.loaded = [sems.sem(f"{stage}_cx_in{i}") for i in range(2)]

    def load(self, sp, w, parity):
        src = self.dram[:, w * PAIR:(w + 1) * PAIR, :] if isinstance(w, int) else self.dram[:, bass.ds(w * PAIR, PAIR), :]
        sp.dma_start(self.tiles[parity][:], src).then_inc(self.loaded[parity], 16)

    def load_first(self, sp):
        for w in range(2):
            self.load(sp, w, w)

    def load_rest(self, sp, transposed):
        with sp.Fori(1, NG // 2) as i:
            for parity in range(2):
                sp.wait_ge(transposed, i * 2 + parity - 1)
                self.load(sp, i * 2 + parity, parity)


class Arena:

    def __init__(self, *tensors, used=(0, 0)):
        self.tensors, self.used = tensors, list(used)

    def sb(self, shape, dt=FP32):
        kind, n = int(dt == F32R), int(np.prod(shape[1:]))
        tile = self.tensors[kind][0:shape[0], self.used[kind]:self.used[kind] + n]
        self.used[kind] += n
        if len(shape) == 3:
            return tile.rearrange("p (k n) -> p k n", k=shape[1])
        return tile.rearrange("p (b k n) -> p b k n", b=shape[1], k=shape[2]) if len(shape) == 4 else tile


class SplitWeights:

    def __init__(self, sems, stage):
        self.w_in, self.hi_ok, self.w_ok = (sems.sem(f"{stage}_{n}") for n in ("w_in", "w_hi_ok", "w_ok"))
        self.of, self.loads, self.pieces = stage, [], []

    def load(self, sp):
        for dst, src in self.loads:
            sp.dma_start(dst, src).then_inc(self.w_in, 16)

    def wait_in(self, eng):
        eng.wait_ge(self.w_in, 16 * len(self.loads))

    def act_piece(self, act, i):
        if i == 0:
            self.wait_in(act)
        self.high(act, i)

    def high(self, act, i):
        raw, hi, _ = self.pieces[i]
        act.activation(hi, raw, ACT.Copy).then_inc(self.hi_ok, 1)

    def dve_piece(self, dve, i):
        raw, hi, lo = self.pieces[i]
        dve.wait_ge(self.hi_ok, i + 1)
        dve.tensor_tensor(lo, raw, f32(hi), ALU.subtract).then_inc(self.w_ok, 1)

    def prepare_act(self, act):
        for i in range(len(self.pieces)):
            self.act_piece(act, i)

    def prepare_dve(self, dve):
        for i in range(len(self.pieces)):
            self.dve_piece(dve, i)

    def act_slot(self, act, slot, banks):
        if slot < len(self.pieces):
            self.act_piece(act, slot)

    def dve_slot(self, dve, slot, banks):
        if 1 <= slot <= len(self.pieces):
            self.dve_piece(dve, slot - 1)

    def pe_slot(self, pe, slot, banks, free):
        pass

    def wait_split(self, pe, pieces=None):
        pe.wait_ge(self.hi_ok, pieces or len(self.pieces))
        pe.wait_ge(self.w_ok, pieces or len(self.pieces))


class AttentionWeights(SplitWeights):

    def __init__(self, sems, stage, arena, w_dram, rows, rope=False):
        super().__init__(sems, stage)
        self.w_dram, self.rows, self.rope = w_dram, rows, rope
        self.hi, self.lo = arena.sb([P, KC, 4 * D], F32R), arena.sb([P, KC, 4 * D], F32R)
        self.bias_cols = self.row_v = self.row_o = self.q_mul = None
        if rows:
            self.bias_cols, self.row_v, self.row_o = arena.sb([P, 4]), arena.sb([P, PAIR, D]), arena.sb([P, PAIR, D])
            self.q_mul = arena.sb([P, TOK])
        if rope:
            self.w_fold, self.w_ahead = sems.sem(f"{stage}_w_fold"), sems.sem(f"{stage}_w_ahead")

    def stage(self, nm, turned=None):
        self.raw = nm.sb(f"{self.of}_raw", [P, KC, 4 * D])
        self.loads = [(self.raw[:, :, n * D:n * D + src.shape[2]], src) for n, src in self.w_dram]
        self.ahead = []
        into = {"bias_cols": self.bias_cols, "row_v": self.row_v, "row_o": self.row_o, "q_mul": self.q_mul}
        if self.rope:
            self.turned, self.bias_turned = turned, nm.sb("bias_turned", [P, 4])
            into.update({"w_turned": self.turned, "bias_turned": self.bias_turned})
        self.loads += [(into[k][:], src) for k, src in self.rows]
        if self.rope:
            dst, src = self.loads[0]
            first = [n for n, (k, _) in enumerate(self.rows) if k in ("w_turned", "bias_cols", "bias_turned")]
            rows = self.loads[len(self.w_dram):]
            self.ahead = [(dst[:, :, 0:2 * D], src[:, :, 0:2 * D])] + [rows[n] for n in first]
            self.loads = [(dst[:, :, 2 * D:], src[:, :, 2 * D:])] + self.loads[1:len(self.w_dram)] + \
                [rows[n] for n in range(len(rows)) if n not in first]
        halves = [(k, slice(n * 2 * D, (n + 1) * 2 * D)) for n in range(2) for k in range(KC)]
        self.pieces = [(self.raw[:, k, cols], self.hi[:, k, cols], self.lo[:, k, cols]) for k, cols in halves]

    def load(self, sp):
        for dst, src in self.ahead:
            sp.dma_start(dst, src).then_inc(self.w_ahead, 16)
        super().load(sp)

    def fold(self, dve, turn_sign):
        dve.wait_ge(self.w_ahead, 16 * len(self.ahead))
        new = self.raw[:, :, 0:2 * D].rearrange("p k (h e) -> p k h e", e=DH)
        turned = self.turned[:].rearrange("p k (h e) -> p k h e", e=DH)
        for k in range(KC):
            dve.tensor_tensor(new[:, k, :, 0:DH // 2], new[:, k, :, 0:DH // 2], turned[:, k, :, 0:DH // 2], ALU.subtract)
            dve.tensor_tensor(new[:, k, :, DH // 2:], new[:, k, :, DH // 2:], turned[:, k, :, DH // 2:], ALU.add)
        dve.scalar_tensor_tensor(self.bias_cols[:], self.bias_turned[:], turn_sign, self.bias_cols[:],
                                 op0=ALU.mult, op1=ALU.add).then_inc(self.w_fold, 1)

    def act_piece(self, act, i):
        if i == 0 and self.rope:
            act.wait_ge(self.w_fold, 1)
        if i == (KC if self.rope else 0):
            self.wait_in(act)
        self.high(act, i)


class RoutedWeights(SplitWeights):

    def __init__(self, sems, stage, arena, a):
        super().__init__(sems, stage)
        self.a = a
        self.wi_hi, self.wi_lo = arena.sb([P, KC, GATED], F32R), arena.sb([P, KC, GATED], F32R)
        self.wo_hi, self.wo_lo = arena.sb([P, F // P, D], F32R), arena.sb([P, F // P, D], F32R)
        self.b_parts = arena.sb([3 * E * R, F], F32R)
        self.gate_row, self.bias_i, self.row_o = arena.sb([P, PAIR, E]), arena.sb([P, F // P]), arena.sb([P, PAIR, D])
        self.expert_of = arena.sb([P, E * R])

    def stage(self, nm):
        ER = E * R
        wi, wo = nm.sb("routed_wi", [P, KC, GATED]), nm.sb("routed_wo", [P, F // P, D])
        b = nm.sb("routed_b", [3 * ER, F])
        self.loads = [(wi[:, :, 0:F], self.a["L0_ffn_wi_W"]), (wi[:, :, F:], self.a["L0_ffn_gA"]), (wo[:], self.a["L0_ffn_wo_W"]),
                      (b[:], self.a["L0_ffn_B"]), (self.gate_row[:], self.a["L0_ffn_gate_b"]),
                      (self.bias_i[:], self.a["L0_ffn_wi_b"]), (self.row_o[:], self.a["L0_ffn_wo_b"]),
                      (self.expert_of[:], self.a["expert_of"])]
        self.b = b
        half = F // P // 2
        self.pieces = [(wi[:, k, :], self.wi_hi[:, k, :], self.wi_lo[:, k, :]) for k in range(KC)]
        self.pieces += [(wo[:, n * half:(n + 1) * half, :], self.wo_hi[:, n * half:(n + 1) * half, :],
                         self.wo_lo[:, n * half:(n + 1) * half, :]) for n in range(2)]
        self.pieces.append((b[:], self.b_parts[:], None))

    def dve_piece(self, dve, i):
        if self.pieces[i][2] is not None:
            super().dve_piece(dve, i)
            return
        low = slice(E * R, 2 * E * R)
        dve.wait_ge(self.hi_ok, i + 1)
        dve.tensor_tensor(self.b_parts[low, :], self.b[low, :], f32(self.b_parts[low, :]), ALU.subtract).then_inc(self.w_ok, 1)


class EntangledWeights(SplitWeights):

    def __init__(self, sems, stage, arena, a):
        super().__init__(sems, stage)
        self.raw, self.bias_in = arena.sb([P, KC, 5 * D]), arena.sb([P, 4 * KC])
        self.bias_e = arena.sb([P, KC])
        self.hi, self.lo = arena.sb([P, KC, 3 * D], F32R), arena.sb([P, KC, 3 * D], F32R)
        self.folded = sems.sem(f"{stage}_folded")
        self.loads = [(self.raw[:, :, n * D:(n + 1) * D], a[f"L0_xattn_{k}"]) for n, k in enumerate(("Wq", "Wk", "Weq", "Wek", "Wv"))]
        self.loads.append((self.bias_in[:], a["L0_xattn_b"]))

    def stage(self, nm):
        pass

    def fold(self, pe, banks):
        self.wait_in(pe)
        w = self.raw
        for n in range(2):
            for m in range(KC):
                for k in range(KC):
                    pe.matmul(banks[n][:, m * D:(m + 1) * D], w[:, k, n * D + m * P:n * D + (m + 1) * P],
                              w[:, k, (2 + n) * D:(3 + n) * D], start=(k == 0), stop=(k == KC - 1))
        for m in range(KC):
            for j in range(2 * KC):
                n, k = j // KC, j % KC
                last = pe.matmul(banks[2][:, m:m + 1], w[:, k, (2 + n) * D + m * P:(2 + n) * D + (m + 1) * P],
                                 self.bias_in[:, n * KC + k:n * KC + k + 1], start=(j == 0), stop=(j == 2 * KC - 1))
        last.then_inc(self.folded, 1)

    def parts(self, banks):
        return [(chunked(banks[0]) if n == 0 else chunked(banks[1]) if n == 1 else self.raw[:, :, 4 * D:],
                 slice(n * D, (n + 1) * D)) for n in range(3)]

    def split_high(self, act, banks):
        act.wait_ge(self.folded, 1)
        self.wait_in(act)
        for src, cols in self.parts(banks):
            act.activation(self.hi[:, :, cols], src, ACT.Copy).then_inc(self.hi_ok, 1)

    def split_low(self, dve, banks):
        dve.wait_ge(self.folded, 1)
        self.wait_in(dve)
        dve.tensor_tensor(self.bias_e[:], self.bias_in[:, 2 * KC:3 * KC], banks[2][:, 0:KC], ALU.add)
        for n, (src, cols) in enumerate(self.parts(banks)):
            dve.wait_ge(self.hi_ok, n + 1)
            dve.tensor_tensor(self.lo[:, :, cols], src, f32(self.hi[:, :, cols]), ALU.subtract).then_inc(self.w_ok, 1)

    def pe_slot(self, pe, slot, banks, free):
        if slot == STEPS + 1:
            for sem, count in free:
                pe.wait_ge(sem, count)
            self.fold(pe, banks)

    def act_slot(self, act, slot, banks):
        if slot == 2 * STEPS - 1:
            self.split_high(act, banks)

    def dve_slot(self, dve, slot, banks):
        if slot == 2 * STEPS - 1:
            self.split_low(dve, banks)


class TernaryWeights(SplitWeights):

    def __init__(self, sems, stage, arena, a, ones):
        super().__init__(sems, stage)
        self.ones = ones
        self.raw = [arena.sb([P, KC * F]), arena.sb([P, F // P * D])]
        self.gain, self.offset = arena.sb([P, F // P]), arena.sb([P, F // P])
        self.sums, self.total, self.level = arena.sb([P, 4]), arena.sb([P, 2]), arena.sb([P, 2, 2])
        self.quant = [arena.sb([P, KC, F], F32R), arena.sb([P, F // P, D], F32R)]
        self.total_ok, self.level_ok, self.below_ok, self.quant_ok = (
            sems.sem(f"{stage}_{n}") for n in ("total_ok", "level_ok", "below_ok", "quant_ok"))
        self.loads = [(self.raw[0][:], a["L1_ffn_W_fc"]), (self.raw[1][:], a["L1_ffn_W_proj"]),
                      (self.gain[:], a["L1_ffn_ln_w"]), (self.offset[:], a["L1_ffn_ln_b"])]

    def stage(self, nm):
        half = KC * F // 2
        self.magnitudes = nm.sb("magnitudes", [P, half], BF16)
        self.pieces = [(self.raw[n // 2][:, n % 2 * half:(n % 2 + 1) * half], None, None) for n in range(4)]

    def act_piece(self, act, i):
        if i == 0:
            self.wait_in(act)
        else:
            act.wait_ge(self.hi_ok, i)
        act.activation(self.magnitudes[:], self.pieces[i][0], ACT.Abs, accum_out=self.sums[:, i:i + 1]).then_inc(self.hi_ok, 1)

    def add_up(self, pe, bank):
        pe.wait_ge(self.hi_ok, len(self.pieces))
        pe.matmul(bank[:, 0:4], self.ones[:], self.sums[:], start=True, stop=True).then_inc(self.total_ok, 1)

    def levels(self, dve, bank):
        level = self.level
        self.wait_in(dve)
        dve.wait_ge(self.total_ok, 1)
        dve.tensor_reduce(self.total[:], bank[:, 0:4].rearrange("p (n h) -> p n h", n=2), AXX, ALU.add).then_inc(self.level_ok, 1)
        dve.wait_ge(self.level_ok, 1)
        dve.tensor_scalar(level[:, :, 0], self.total[:], 1.0 / (F * D), ABSMEAN_EPS, ALU.mult, ALU.add).then_inc(self.level_ok, 1)
        dve.wait_ge(self.level_ok, 2)
        dve.tensor_scalar(level[:, :, 1], level[:, :, 0], -0.5, None, ALU.mult).then_inc(self.level_ok, 1)
        dve.wait_ge(self.level_ok, 3)
        dve.tensor_scalar(level[:, :, 0], level[:, :, 0], 0.5, None, ALU.mult).then_inc(self.level_ok, 1)

    def quantise(self, dve, i, above):
        n, half = i // 2, KC * F // 2
        raw = self.pieces[i][0]
        quant = self.quant[n].rearrange("p k n -> p (k n)")[:, i % 2 * half:(i % 2 + 1) * half]
        if not above:
            dve.wait_ge(self.level_ok, 4)
            dve.tensor_scalar(quant, raw, self.level[:, n, 1:2], None, ALU.is_lt).then_inc(self.below_ok, 1)
        else:
            dve.wait_ge(self.below_ok, i + 1)
            dve.scalar_tensor_tensor(quant, raw, self.level[:, n, 0:1], f32(quant), op0=ALU.is_gt,
                                     op1=ALU.subtract).then_inc(self.quant_ok, 1)

    def pe_slot(self, pe, slot, banks, free):
        if slot == len(self.pieces) + 1:
            pe.wait_ge(*free[0])
            self.add_up(pe, banks[0])

    def dve_slot(self, dve, slot, banks):
        first = len(self.pieces) + 2
        if slot == first:
            self.levels(dve, banks[0])
        elif first < slot <= first + 2 * len(self.pieces):
            self.quantise(dve, (slot - first - 1) // 2, (slot - first - 1) % 2 == 1)


def attention_stage(nc, name, before, norm, next_norm, consts, wt, following, spare, context=None, next_context=None, mask_dram=None,
                    rope=False, k_bias=False, v_bias=False, o_bias=False, x_dram=None, constants=None):
    nm = Names(nc, ExitStack(), name, before)
    sb, sem = nm.sb, nm.sem
    ident, ident_b, neg_ident_b, head_mask = (consts[k] for k in ("ident", "ident_b", "neg_ident_b", "head_mask"))

    probs = sb("probs", [P, 4, QH * P])
    if x_dram is not None:
        wt.stage(nm, probs[:, 0:KC, :])
    following.stage(nm)
    w_hi, w_lo, bias_cols, row_v, row_o, q_mul = wt.hi, wt.lo, wt.bias_cols, wt.row_v, wt.row_o, wt.q_mul
    WQ, WK, WV, WO = (slice(n * D, (n + 1) * D) for n in range(4))

    xT_hi, xT_lo = norm.hi, norm.lo
    q32 = sb("q32", [P, KC, TOK])
    k32 = sb("k32", [P, KC, TOK])
    q_lo = sb("q_lo", [P, KC, TOK])
    q_hi = [spare.sb([P, KC, TOK], F32R) for i in range(2)]
    k_hi = [spare.sb([P, KC, TOK], F32R) for i in range(2)]
    k_lo = [spare.sb([P, KC, TOK], F32R) for i in range(2)]
    qm_hi = [sb(f"qm_hi{i}", [P, KC, PAIR, QH, P], F32R) for i in range(2)]
    qm_lo = [sb(f"qm_lo{i}", [P, KC, PAIR, QH, P], F32R) for i in range(2)]
    km_hi = [sb(f"km_hi{i}", [P, KC, PAIR, QH, P], F32R) for i in range(2)]
    v_pad = [sb(f"v_pad{i}", [P, PAIR, H, 2 * DH]) for i in range(2)]
    row_max = sb("row_max", [P, 4, QH], FP32 if context is not None else BF16)
    av_raw = sb("av_raw", [P, NQ * P])
    inv_den = sb("inv_den", [P, H, 1])
    o_tok = sb("o_tok", [P, H, DH])
    o_hi = spare.sb([P, PAIR, KC, P], F32R)
    o_lo = spare.sb([P, PAIR, KC, P], F32R)

    S1 = [nm.ps(f"S1_{i}") for i in range(2)]
    S2 = [nm.ps(f"S2_{i}") for i in range(2)]
    AV = [nm.ps(f"AV_{i}") for i in range(2)]
    FA, FB = nm.ps("FA"), nm.ps("FB")
    NEXT_BANKS = FB, *S1

    cross = context is not None
    if cross:
        mask_link = sem("mask_link")
        cx, cx_in = context.tiles, context.loaded
        cT_hi = spare.sb([P, KC, TOK], F32R)
        cT_lo = spare.sb([P, KC, TOK], F32R)
        mask_u8 = sb("mask_u8", [P, P], U8)
        keep = sb("keep", [P, P])
        any_kept = sb("any_kept", [P, 1])
        add_mask32 = sb("add_mask32", [P, P])
        add_mask = sb("add_mask", [P, P], BF16)
        shifts = sb("shifts", [P, 4, QH, P], BF16)
        ctx_full, ctx_hi, ctx_lo, shift_ok = sem("ctx_full"), sem("ctx_hi"), sem("ctx_lo"), sem("shift_ok")
    kvT_hi, kvT_lo = (cT_hi, cT_lo) if cross else (xT_hi, xT_lo)

    x_first, x_rest, mask_in = sem("x_first"), sem("x_rest"), sem("mask_in")
    zeroed, setup, setup_pe = sem("zeroed"), sem("setup"), sem("setup_pe")
    xn_ok, biased = norm.xn_ok, sem("biased")
    q_full, q_free, qhi_ok, qlo_ok, qmhi_ok, qm_ok = (sem(n) for n in ("q_full", "q_free", "qhi_ok", "qlo_ok", "qmhi_ok", "qm_ok"))
    k_full, k_free, khi_ok, klo_ok, km_ok = (sem(n) for n in ("k_full", "k_free", "khi_ok", "klo_ok", "km_ok"))
    km_rest_ok = sem("km_rest_ok")
    v_full, v_free, out_full, out_free = sem("v_full"), sem("v_free"), sem("out_full"), sem("out_free")
    s1_full, max_ok, s2_full, exp_ok, av_full = (sem(n) for n in ("s1_full", "max_ok", "s2_full", "exp_ok", "av_full"))
    raw_ok, turned, inv_ok, otok_ok, back, ohi_ok, olo_ok = (
        sem(n) for n in ("raw_ok", "turned", "inv_ok", "otok_ok", "back", "ohi_ok", "olo_ok"))

    dve_q = rope or cross
    dve_k = rope

    def schedule(eng, group):
        for G in range(-1, 3):
            group(G, G % 2)
        with eng.Fori(1, (NG - 4) // 2) as i:
            group(i * 2 + 1, 1)
            group(i * 2 + 2, 0)
        for G in range(NG - 3, NG + 1):
            group(G, G % 2)

    def has_norm(G):
        return not isinstance(G, int) or G + 2 < NG

    def first_of_next(G):
        return isinstance(G, int) and G + 2 == NG

    def has_window(G):
        return not isinstance(G, int) or G + 1 < NG

    def has_transposes(G):
        return has_window(G) and (x_dram is not None or not isinstance(G, int) or G >= 0)

    def shared(w):
        return isinstance(w, int) and w < 2

    def has_step(G, t):
        return not isinstance(G, int) or 0 <= STEPS * G + t < STEPS * NG

    def whole(G):
        return not isinstance(G, int) or 0 <= G < NG

    def place(t):
        tt = t % STEPS
        c = (tt % NQ) // 2
        return tt // NQ, c, (tt + c) % 2, t < 0

    def heads(b):
        return AV[b][:, 0:D].rearrange("p (c t) -> p c t", c=KC)

    def per_head(bank, e):
        return bank[:].rearrange("p (b h e) -> p b h e", b=PAIR, e=e)

    with nc.Block() as block:

        @block.sync
        def _(sp):
            def load_x(n):
                part = slice(n * X_SEQS, (n + 1) * X_SEQS)
                sp.dma_start(norm.x_res[:, part, :], x_dram[:, part, :]).then_inc(x_first if n == 0 else x_rest, 16)
            if x_dram is not None:
                load_x(0)
                constants.load(sp)
                wt.load(sp)
            if cross:
                sp.dma_start(mask_u8[:], mask_dram).then_inc(mask_in, 16)
            if x_dram is not None:
                for n in range(1, X_LOADS):
                    load_x(n)
            if cross:
                following.load(sp)
                context.load_rest(sp, ctx_full)
            else:
                following.load(sp)
                if next_context is not None:
                    next_context.load_first(sp)

        @block.gpsimd
        def _(pool):
            for i in range(2):
                pool.memset(v_pad[i][:], 1.0).then_inc(zeroed, 1)
            if x_dram is not None:
                pool.wait_ge(constants.ready, 1)
            def add_bias(w):
                pool.wait_ge(xn_ok, w + 1)
                if isinstance(w, int) and w == 0:
                    wt.wait_in(pool)
                x = norm.x_group(w)
                pool.tensor_tensor(x, x, row_o[:], ALU.add).then_inc(biased, 1)

            def shift_step(G, t):
                T = G * STEPS + t
                pool.wait_ge(max_ok, T + 1)
                at_least(pool, s2_full, T - 3)
                pool.tensor_tensor(shifts[:, t % 4], add_mask[:].rearrange("p (o k) -> p o k", o=1).to_broadcast([P, QH, P]),
                                   row_max[:, t % 4, :].rearrange("p (h o) -> p h o", o=1).to_broadcast([P, QH, P]),
                                   ALU.subtract).then_inc(shift_ok, 1)

            def group(G, parity):
                if isinstance(G, int) and G < 0 and x_dram is not None:
                    norm.pool_rstd(pool, 0)
                for t in range(STEPS):
                    if cross and has_step(G, t):
                        shift_step(G, t)
                    if has_norm(G) and t == 2:
                        norm.pool_rstd(pool, G + 2)
                    if first_of_next(G) and t == 2:
                        next_norm.pool_rstd(pool, 0)
                    if o_bias and has_window(G) and t == 5:
                        add_bias(G + 1)
            schedule(pool, group)
            nm.clear_before(pool)

        @block.scalar
        def _(act):
            if x_dram is None:
                wt.wait_in(act)
            def exp_step(G, t, parity):
                T = G * STEPS + t
                act.wait_ge(s2_full, T + 1)
                at_least(act, av_full, T - 3)
                act.activation(probs[:, t % 4, :], S2[t % 2][:], ACT.Exp, scale=DH ** -0.5).then_inc(exp_ok, 1)

            def raw_heads(B, b):
                act.wait_ge(av_full, B * NQ + NQ)
                at_least(act, turned, B)
                act.activation(av_raw[:], AV[b][:], ACT.Copy).then_inc(raw_ok, 1)

            def out_high(B, G, b):
                act.wait_ge(back, B + 1)
                at_least(act, out_full, G)
                act.activation(o_hi[:, b], heads(b), ACT.Copy).then_inc(ohi_ok, 1)

            def masked(out, src, v):
                return act.activation(out[:, :, :, v, :], src[:].rearrange("p c (b t) -> p c b t", b=PAIR), ACT.Copy,
                                      scale=head_mask[:, v:v + 1])

            def take_q(w, wp):
                if not dve_q:
                    act.wait_ge(q_full, w + 1)
                    at_least(act, qm_ok, w)
                    act.activation(q32[:], FB[:].rearrange("p (c t) -> p c t", c=KC), ACT.Copy).then_inc(q_free, 1)
                act.wait_ge(q_free, w + 1)
                at_least(act, s1_full, (w - 1) * STEPS)
                act.activation(q_hi[wp][:], q32[:], ACT.Copy).then_inc(qhi_ok, 1)

            def take_k(w, wp):
                if not dve_k:
                    act.wait_ge(k_full, w + 1)
                    at_least(act, klo_ok, w)
                    for c in range(KC):
                        if not k_bias:
                            last = act.activation(k32[:, c], FA[:, c * TOK:(c + 1) * TOK], ACT.Copy)
                        else:
                            last = act.activation(k32[:, c], FA[:, c * TOK:(c + 1) * TOK], ACT.Identity,
                                                  bias=bias_cols[:, KC + c:KC + c + 1])
                    last.then_inc(k_free, 1)
                act.wait_ge(k_free, w + 1)
                if shared(w):
                    masked(km_hi[wp], k32, 0).then_inc(km_ok, 1)
                at_least(act, s2_full, (w - 1) * STEPS)
                act.activation(k_hi[wp][:], k32[:], ACT.Copy).then_inc(khi_ok, 1)

            def group(G, parity):
                w, wp = G + 1, 1 - parity
                for t in range(STEPS):
                    if t in (0, 4) and whole(G - 1):
                        raw_heads((G - 1) * PAIR + t // 4, t // 4)
                    if t in (2, 6) and whole(G - 1):
                        out_high((G - 1) * PAIR + t // 4, G - 1, t // 4)
                    if has_step(G, t - 2):
                        exp_step(G, t - 2, parity)
                    if t == 0 and whole(G):
                        masked(qm_hi[parity], q32, 3).then_inc(qmhi_ok, 1)
                    if isinstance(G, int) and G + 1 == NG and t == 1:
                        next_norm.act_high(act, 0, FA)
                    if has_window(G) and t == 1:
                        if has_transposes(G):
                            at_least(act, v_full, w)
                            norm.act_high(act, w, FA)
                        if x_dram is not None and isinstance(w, int) and w == 0:
                            wt.prepare_act(act)
                            wt.wait_in(act)
                            act.wait_ge(constants.ready, 1)
                        if cross:
                            act.wait_ge(ctx_full, w + 1)
                            act.activation(cT_hi[:], FB[:].rearrange("p (c t) -> p c t", c=KC),
                                           ACT.Copy).then_inc(ctx_hi, 1)
                    if cross and t == 3 and isinstance(G, int) and G < 0:
                        act.wait_ge(setup_pe, 1)
                        for b in range(PAIR):
                            last = act.activation(q_mul[:, b * P:(b + 1) * P], S1[1][:, 0:P], ACT.Copy)
                        last.then_inc(setup, 1)
                    if has_window(G) and t == 4:
                        take_q(w, wp)
                        at_least(act, s2_full, (w - 1) * STEPS)
                        if not (isinstance(w, int) and w == 0):
                            masked(qm_hi[wp], q32, 0)
                            masked(qm_hi[wp], q32, 1)
                    if has_window(G) and t == 5:
                        take_k(w, wp)
                        if not shared(w):
                            masked(km_hi[wp], k32, 0)
                    if has_window(G) and t == 6:
                        if not shared(w):
                            masked(km_hi[wp], k32, 1)
                            masked(km_hi[wp], k32, 2)
                    if has_window(G) and t == 7:
                        if not shared(w):
                            masked(km_hi[wp], k32, 3).then_inc(km_ok, 1)
                        if not v_bias:
                            act.wait_ge(v_full, w + 1)
                            at_least(act, av_full, (w - 1) * STEPS)
                            if isinstance(w, int):
                                at_least(act, zeroed, 2)
                            act.activation(v_pad[wp][:, :, :, 0:DH], per_head(FB, DH), ACT.Copy).then_inc(v_free, 1)
                        if isinstance(w, int) and w == 0:
                            masked(qm_hi[wp], q32, 0)
                            masked(qm_hi[wp], q32, 1)
                        masked(qm_hi[wp], q32, 2)
                    if isinstance(G, int) and G >= NG - 1:
                        following.act_slot(act, (G - NG + 1) * STEPS + t, NEXT_BANKS)
            schedule(act, group)

        @block.vector
        def _(dve):
            def moments_of(w):
                if x_dram is not None and isinstance(w, int) and w * PAIR < X_SEQS:
                    dve.wait_ge(x_first, 16)
                elif x_dram is not None and isinstance(w, int):
                    dve.wait_ge(x_rest, 16 * (X_LOADS - 1))
                norm.dve_moments(dve, w)

            if x_dram is not None:
                constants.prepare(dve)
            else:
                wt.wait_in(dve)

            def masks():
                dve.wait_ge(mask_in, 16)
                dve.tensor_copy(keep[:], mask_u8[:]).then_inc(mask_link, 1)
                dve.wait_ge(mask_link, 1)
                dve.tensor_reduce(any_kept[:], keep[:], AXX, ALU.max).then_inc(mask_link, 1)
                dve.tensor_scalar(add_mask32[:], keep[:], -1.0, -MASKED, ALU.add, ALU.mult).then_inc(mask_link, 1)
                dve.wait_ge(mask_link, 3)
                dve.tensor_scalar(add_mask32[:], add_mask32[:], any_kept[:], None, ALU.mult).then_inc(mask_link, 1)
                dve.wait_ge(mask_link, 4)
                dve.tensor_copy(add_mask[:], add_mask32[:]).then_inc(mask_link, 1)

            def max_step(G, t):
                T = G * STEPS + t
                dve.wait_ge(s1_full, T + 1)
                at_least(dve, s2_full, T - 3)
                dve.tensor_reduce(row_max[:, t % 4, :], S1[t % 2][:].rearrange("p (h k) -> p h k", h=QH),
                                  AXX, ALU.max).then_inc(max_ok, 1)

            def normalise(B, b):
                dve.wait_ge(turned, B + 1)
                rows = AV[b][:].rearrange("p (h e) -> p h e", h=H)
                dve.reciprocal(inv_den[:], rows[:, :, DH:DH + 1]).then_inc(inv_ok, 1)
                at_least(dve, back, B)
                dve.wait_ge(inv_ok, B + 1)
                dve.tensor_tensor(o_tok[:], rows[:, :, 0:DH], inv_den[:].to_broadcast([P, H, DH]), ALU.mult).then_inc(otok_ok, 1)

            def out_low(B, b):
                dve.wait_ge(ohi_ok, B + 1)
                dve.tensor_tensor(o_lo[:, b], heads(b), f32(o_hi[:, b]), ALU.subtract).then_inc(olo_ok, 1)

            def group(G, parity):
                w, wp = G + 1, 1 - parity
                for t in range(STEPS):
                    if t in (2, 6) and whole(G - 1):
                        out_low((G - 1) * PAIR + t // 4, t // 4)
                    if has_step(G, t):
                        max_step(G, t)
                    if t in (0, 4) and whole(G - 1):
                        normalise((G - 1) * PAIR + t // 4, t // 4)
                    if t == 0 and isinstance(G, int) and G < 0:
                        if x_dram is not None:
                            moments_of(0)
                            norm.dve_normalise(dve, 0)
                        moments_of(1)
                    if isinstance(G, int) and G + 1 == NG and t == 2:
                        next_norm.dve_low(dve, 0, FA)
                    if has_window(G) and t == 2:
                        if has_transposes(G):
                            norm.dve_low(dve, w, FA)
                        if x_dram is not None and isinstance(w, int) and w == 0:
                            wt.fold(dve, consts["turn_sign"][:])
                            wt.prepare_dve(dve)
                            wt.wait_in(dve)
                        if cross:
                            dve.wait_ge(ctx_hi, w + 1)
                            dve.tensor_tensor(cT_lo[:], FB[:].rearrange("p (c t) -> p c t", c=KC), f32(cT_hi[:]),
                                              ALU.subtract).then_inc(ctx_lo, 1)
                    if cross and t == 2 and isinstance(G, int) and G < 0:
                        masks()
                    if has_window(G) and t == 4 and dve_q:
                        dve.wait_ge(q_full, w + 1)
                        if cross and isinstance(w, int) and w == 0:
                            dve.wait_ge(setup, 1)
                        at_least(dve, qmhi_ok, w)
                        for c in range(KC):
                            last = dve.scalar_tensor_tensor(q32[:, c], FB[:, c * TOK:(c + 1) * TOK],
                                                            bias_cols[:, c:c + 1], q_mul[:], op0=ALU.add, op1=ALU.mult)
                        last.then_inc(q_free, 1)
                    if has_window(G) and t == 5:
                        if dve_k:
                            dve.wait_ge(k_full, w + 1)
                            at_least(dve, km_ok, w)
                            for c in range(KC):
                                last = dve.scalar_tensor_tensor(k32[:, c], FA[:, c * TOK:(c + 1) * TOK],
                                                                bias_cols[:, KC + c:KC + c + 1], q_mul[:],
                                                                op0=ALU.add, op1=ALU.mult)
                            last.then_inc(k_free, 1)
                        dve.wait_ge(qhi_ok, w + 1)
                        dve.tensor_tensor(q_lo[:], q32[:], f32(q_hi[wp][:]), ALU.subtract).then_inc(qlo_ok, 1)
                        at_least(dve, s2_full, (w - 1) * STEPS)
                    if has_window(G) and t == 6 and shared(w):
                        dve.wait_ge(k_free, w + 1)
                        for v in range(1, QH):
                            last = dve.tensor_scalar(km_hi[wp][:, :, :, v, :], k32[:].rearrange("p c (b t) -> p c b t", b=PAIR),
                                                     head_mask[:, v:v + 1], None, ALU.mult)
                        last.then_inc(km_rest_ok, 1)
                    if has_window(G) and t in (6, 7):
                        if t == 6:
                            dve.wait_ge(qlo_ok, w + 1)
                        for v in ((0, 1) if t == 6 else (2, 3)):
                            last = dve.tensor_scalar(qm_lo[wp][:, :, :, v, :],
                                                     q_lo[:].rearrange("p c (b t) -> p c b t", b=PAIR),
                                                     head_mask[:, v:v + 1], None, ALU.mult)
                        if t == 7:
                            last.then_inc(qm_ok, 1)
                    if has_window(G) and t == 7:
                        dve.wait_ge(khi_ok, w + 1)
                        dve.tensor_tensor(k_lo[wp][:], k32[:], f32(k_hi[wp][:]), ALU.subtract).then_inc(klo_ok, 1)
                        if v_bias:
                            dve.wait_ge(v_full, w + 1)
                            at_least(dve, av_full, (w - 1) * STEPS)
                            if isinstance(w, int):
                                dve.wait_ge(zeroed, 2)
                            last = dve.tensor_tensor(v_pad[wp][:, :, :, 0:DH], per_head(FB, DH),
                                                     row_v[:].rearrange("p b (h e) -> p b h e", e=DH), ALU.add)
                            last.then_inc(v_free, 1)
                    if has_norm(G) and t == 2 and not (isinstance(G, int) and G < 0):
                        moments_of(w + 1)
                    if has_norm(G) and t == 3:
                        norm.dve_normalise(dve, w + 1)
                    if first_of_next(G) and t == 2:
                        dve.wait_ge(out_free, 1)
                        next_norm.dve_moments(dve, 0)
                    if first_of_next(G) and t == 3:
                        next_norm.dve_normalise(dve, 0)
                    if t == 7 and whole(G - 1):
                        dve.wait_ge(out_full, G)
                        if o_bias:
                            dve.wait_ge(biased, G)
                        x = norm.x_group(G - 1)
                        dve.tensor_tensor(x, x, FA[:].rearrange("p (b d) -> p b d", b=PAIR), ALU.add).then_inc(out_free, 1)
                    if isinstance(G, int) and G >= NG - 1:
                        following.dve_slot(dve, (G - NG + 1) * STEPS + t, NEXT_BANKS)
            schedule(dve, group)

        @block.tensor
        def _(pe):
            def s1_step(G, t, parity):
                T = G * STEPS + t
                b, c, u, _ = place(t)
                rows64 = slice(64 * u, 64 * u + 64)
                if cross and isinstance(G, int) and G == 0 and t == 0:
                    pe.wait_ge(setup, 1)
                if t == 0:
                    pe.wait_ge(qhi_ok, G + 1)
                    pe.wait_ge(km_ok, G + 1)
                    if shared(G):
                        pe.wait_ge(km_rest_ok, G + 1)
                at_least(pe, max_ok, T - 1)
                last = pe.matmul(S1[t % 2][:], q_hi[parity][rows64, c, b * P:(b + 1) * P],
                                 km_hi[parity][rows64, c, b].rearrange("p h t -> p (h t)"), start=True, stop=not cross)
                if cross:
                    for v in range(QH):
                        last = pe.matmul(S1[t % 2][:, v * P:(v + 1) * P], ident_b[:], add_mask[:],
                                         start=False, stop=v == QH - 1)
                last.then_inc(s1_full, 1)

            def s2_step(G, t, parity):
                T = G * STEPS + t
                b, c, u, before = place(t)
                par = 1 - parity if before else parity
                rows64 = slice(64 * u, 64 * u + 64)
                tok = slice(b * P, (b + 1) * P)
                if t == 0:
                    pe.wait_ge(qmhi_ok, G + 1)
                    pe.wait_ge(qm_ok, G + 1)
                    pe.wait_ge(klo_ok, G + 1)
                at_least(pe, exp_ok, T - 1)
                bank = S2[t % 2]
                q_high = qm_hi[par][rows64, c, b].rearrange("p h t -> p (h t)")
                q_low = qm_lo[par][rows64, c, b].rearrange("p h t -> p (h t)")
                pe.matmul(bank[:], k_hi[par][rows64, c, tok], q_high, start=True, stop=False)
                pe.matmul(bank[:], k_hi[par][rows64, c, tok], q_low, start=False, stop=False)
                pe.matmul(bank[:], k_lo[par][rows64, c, tok], q_high, start=False, stop=False)
                pe.wait_ge(shift_ok if cross else max_ok, T + 1)
                for v in range(QH):
                    part = bank[:, v * P:(v + 1) * P]
                    if cross:
                        last = pe.matmul(part, shifts[:, t % 4, v, :], ident_b[:], start=False, stop=v == QH - 1)
                    else:
                        last = pe.matmul(part, row_max[:, t % 4, v:v + 1].to_broadcast([P, P]), neg_ident_b[:],
                                         start=False, stop=v == QH - 1)
                last.then_inc(s2_full, 1)

            def av_step(G, t, parity):
                T = G * STEPS + t
                b, c, u, before = place(t)
                par = 1 - parity if before else parity
                if t == 0:
                    pe.wait_ge(v_free, G + 1)
                if t % NQ == 0:
                    at_least(pe, olo_ok, G * PAIR + t // NQ - 1)
                pe.wait_ge(exp_ok, T + 1)
                r = 2 * c + u
                for v in range(QH):
                    last = pe.matmul(AV[b][32 * v:32 * v + 32, r * P:(r + 1) * P], v_pad[par][:, b, r * QH + v, :],
                                     probs[:, t % 4, v * P:(v + 1) * P], start=True, stop=True)
                last.then_inc(av_full, 1)

            def turn(B, b):
                pe.wait_ge(raw_ok, B + 1)
                for r in range(NQ):
                    last = pe.transpose(AV[b][:, r * P:(r + 1) * P], av_raw[:, r * P:(r + 1) * P], ident[:])
                last.then_inc(turned, 1)

            def turn_back(B, b):
                pe.wait_ge(otok_ok, B + 1)
                for c in range(KC):
                    last = pe.transpose(AV[b][:, c * P:(c + 1) * P],
                                        o_tok[:, c * H // KC:(c + 1) * H // KC, :].rearrange("p h e -> p (h e)"), ident[:])
                last.then_inc(back, 1)

            def project(bank, cols, hi, lo):
                for m in range(KC):
                    wcol = slice(cols.start + m * P, cols.start + (m + 1) * P)
                    last = three_pass(pe, bank[:, m * TOK:(m + 1) * TOK], lambda k: w_hi[:, k, wcol],
                                      lambda k: w_lo[:, k, wcol], lambda k: hi[:, k, :], lambda k: lo[:, k, :], KC)
                return last

            def group(G, parity):
                w = G + 1
                for t in range(STEPS):
                    if has_step(G, t):
                        s1_step(G, t, parity)
                    if has_step(G, t - 2):
                        s2_step(G, t - 2, parity)
                    if t in (0, 4) and whole(G - 1):
                        turn((G - 1) * PAIR + t // 4, t // 4)
                    if t in (1, 5) and whole(G - 1):
                        turn_back((G - 1) * PAIR + t // 4, t // 4)
                    if has_step(G, t - 4):
                        av_step(G, t - 4, parity)
                    if isinstance(G, int) and G + 1 == NG and t == 1:
                        pe.wait_ge(out_free, NG - 2)
                        pe.wait_ge(k_free, NG)
                        next_norm.pe_transpose(pe, 0, FA)
                    if has_window(G) and t == 1:
                        if has_transposes(G):
                            at_least(pe, out_free, w - 2)
                            at_least(pe, k_free, w)
                            norm.pe_transpose(pe, w, FA)
                        at_least(pe, v_free, w)
                        if cross:
                            pe.wait_ge(cx_in[1 - parity], 16 * ((w // 2) + 1) if isinstance(w, int) else cx_count(w, 1 - parity))
                            for c in range(KC):
                                for b in range(PAIR):
                                    last = pe.transpose(FB[:, c * TOK + b * P:c * TOK + (b + 1) * P],
                                                        cx[1 - parity][:, b, c * P:(c + 1) * P], ident[:])
                            last.then_inc(ctx_full, 1)
                    if has_window(G) and t == 3:
                        pe.wait_ge(norm.lo_ok, w + 1)
                        if cross:
                            pe.wait_ge(ctx_lo, w + 1)
                        if isinstance(w, int) and w == 0:
                            wt.wait_split(pe, KC)
                        project(FB, WQ, xT_hi, xT_lo).then_inc(q_full, 1)
                        if cross and isinstance(G, int) and G < 0:
                            pe.wait_ge(mask_link, 5)
                            pe.matmul(S1[1][:, 0:P], any_kept[:].to_broadcast([P, P]), ident[:], start=True,
                                      stop=True).then_inc(setup_pe, 1)
                    if has_window(G) and t == 4:
                        project(FA, WK, kvT_hi, kvT_lo).then_inc(k_full, 1)
                    if has_window(G) and t == 5:
                        pe.wait_ge(q_free, w + 1)
                        if isinstance(w, int) and w == 0:
                            wt.wait_split(pe)
                        for b in range(PAIR):
                            tok = slice(b * P, (b + 1) * P)
                            last = three_pass(pe, FB[:, b * D:(b + 1) * D], lambda k: kvT_hi[:, k, tok],
                                              lambda k: kvT_lo[:, k, tok], lambda k: w_hi[:, k, WV],
                                              lambda k: w_lo[:, k, WV], KC)
                        last.then_inc(v_full, 1)
                    if t == 7 and whole(G - 1):
                        pe.wait_ge(olo_ok, G * PAIR)
                        if has_window(G):
                            pe.wait_ge(k_free, w + 1)
                        else:
                            pe.wait_ge(next_norm.lo_ok, 1)
                            pe.wait_ge(out_free, G - 1)
                        for b in range(PAIR):
                            last = three_pass(pe, FA[:, b * D:(b + 1) * D], lambda k: o_hi[:, b, k, :],
                                              lambda k: o_lo[:, b, k, :], lambda k: w_hi[:, k, WO],
                                              lambda k: w_lo[:, k, WO], KC)
                        last.then_inc(out_full, 1)
                    if isinstance(G, int) and G >= NG - 1:
                        following.pe_slot(pe, (G - NG + 1) * STEPS + t, NEXT_BANKS, ((v_free, NG), (max_ok, NG * STEPS)))
            if x_dram is not None:
                pe.wait_ge(constants.ready, 1)
            schedule(pe, group)
    nm.end()
    return nm


class Normed:

    def __init__(self, nm, norm, next_norm, bank):
        self.norm, self.next, self.bank, self.lo_ok = norm, next_norm, bank, norm.lo_ok
        self.hi, self.lo = [norm.hi, nm.sb("xT_hi_odd", [P, KC, TOK], F32R)], [norm.lo, nm.sb("xT_lo_odd", [P, KC, TOK], F32R)]

    def own(self, w):
        return not isinstance(w, int) or 0 < w + 1 < NG

    def of_next(self, w):
        return self.next is not None and isinstance(w, int) and w + 1 == NG

    def pe_transpose(self, pe, w):
        if self.own(w) or self.of_next(w):
            pe.wait_ge(self.lo_ok, w + 1)
        if self.own(w):
            self.norm.pe_transpose(pe, w + 1, self.bank)
        elif self.of_next(w):
            self.next.pe_transpose(pe, 0, self.bank)

    def act_high(self, act, w, parity, used, per_group=1):
        if self.own(w):
            at_least(act, used, w * per_group)
            self.norm.act_high(act, w + 1, self.bank, self.hi[1 - parity])
        elif self.of_next(w):
            self.next.act_high(act, 0, self.bank)

    def dve_low(self, dve, w, parity):
        if self.own(w):
            self.norm.dve_low(dve, w + 1, self.bank, self.hi[1 - parity], self.lo[1 - parity])
        elif self.of_next(w):
            self.next.dve_low(dve, 0, self.bank)


def chunked(bank):
    return bank[:].rearrange("p (c t) -> p c t", c=KC)


def windows(eng, window, last=NG):
    for w in range(-2, 3):
        window(w, w % 2)
    with eng.Fori(1, (NG - 4) // 2) as i:
        window(i * 2 + 1, 1)
        window(i * 2 + 2, 0)
    for w in range(NG - 3, last + 1):
        window(w, w % 2)


def next_pieces(w, following):
    if not isinstance(w, int) or following is None or w < NG - 3:
        return range(0)
    return range(min(2 * (w - NG + 3), len(following.pieces)), min(2 * (w - NG + 4), len(following.pieces)))


def takes_moments(w):
    return not isinstance(w, int) or 1 < w + 2 < NG


def has_norm(w):
    return not isinstance(w, int) or 0 < w + 2 < NG


def starts(w):
    return isinstance(w, int) and w == 0


def first_of_next(w):
    return isinstance(w, int) and w + 2 == NG


def in_stage(w):
    return not isinstance(w, int) or 0 <= w < NG


def entangled_stage(nc, name, before, norm, next_norm, consts, context, wt, following):
    nm = Names(nc, ExitStack(), name, before)
    sb, sem = nm.sb, nm.sem
    PT, PC, ENT, VT, VTOK, SC, PP, OUT = (nm.ps(n) for n in ("PT", "PC", "ENT", "VT", "VTOK", "SC", "PP", "OUT"))
    ln = Normed(nm, norm, next_norm, PT)
    following.stage(nm)
    w_hi, w_lo, bias_in, bias_e = wt.hi, wt.lo, wt.bias_in, wt.bias_e
    cx, cx_in = context.tiles, context.loaded
    cT_hi = [sb(f"cT_hi{i}", [P, KC, TOK], F32R) for i in range(2)]
    cT_lo = [sb(f"cT_lo{i}", [P, KC, TOK], F32R) for i in range(2)]
    ent, vT = sb("ent", [P, KC, TOK]), sb("vT", [P, KC, TOK])
    v_tok = sb("v_tok", [P, PAIR, D])
    top, shift = sb("top", [P, PAIR]), sb("shift", [P, PAIR])
    probs, probsT = sb("probs", [P, PAIR, P]), sb("probsT", [P, PAIR, P])
    total, inv_total = sb("total", [P, PAIR]), sb("inv_total", [P, PAIR])
    pc_full, pc_hi, pc_lo = sem("pc_full"), sem("pc_hi"), sem("pc_lo")
    ent_full, ent_ok, vt_full, vt_ok = sem("ent_full"), sem("ent_ok"), sem("vt_full"), sem("vt_ok")
    vtok_full, vtok_ok, sc_full, top_ok, shift_ok = (sem(n) for n in ("vtok_full", "vtok_ok", "sc_full", "top_ok", "shift_ok"))
    exp_ok, inv_ok, pp_full, pp_ok, out_full, out_ok = (sem(n) for n in ("exp_ok", "inv_ok", "pp_full", "pp_ok", "out_full", "out_ok"))

    with nc.Block() as block:

        @block.sync
        def _(sp):

            following.load(sp)
            context.load_rest(sp, pc_full)

        @block.gpsimd
        def _(pool):
            with pool.Fori(1, NG) as w:
                norm.pool_rstd(pool, w)
            next_norm.pool_rstd(pool, 0)
            nm.clear_before(pool)

        @block.scalar
        def _(act):
            def window(w, parity):
                if in_stage(w - 1):
                    for b in range(PAIR):
                        act.wait_ge(shift_ok, w)
                        if b == 0:
                            at_least(act, pp_full, w - 1)
                        last = act.activation(probs[:, b, :], SC[:, b * P:(b + 1) * P], ACT.Exp, bias=shift[:, b:b + 1],
                                              scale=D ** -0.5, accum_out=total[:, b:b + 1])
                    last.then_inc(exp_ok, 1)
                ln.act_high(act, w, parity, vt_full)
                if in_stage(w + 1):
                    act.wait_ge(pc_full, w + 2)
                    act.activation(cT_hi[1 - parity][:], chunked(PC), ACT.Copy).then_inc(pc_hi, 1)
                if in_stage(w - 1):
                    act.wait_ge(pp_full, w)
                    at_least(act, out_full, w - 1)
                    act.activation(probsT[:].rearrange("p b t -> p (b t)"), PP[:, 0:TOK], ACT.Copy).then_inc(pp_ok, 1)
                if in_stage(w):
                    act.wait_ge(ent_full, w + 1)
                    at_least(act, sc_full, w)
                    for m in range(KC):
                        last = act.activation(ent[:, m, :], ENT[:, m * TOK:(m + 1) * TOK], ACT.Tanh, bias=bias_e[:, m:m + 1])
                    last.then_inc(ent_ok, 1)
                    act.wait_ge(vt_full, w + 1)
                    for m in range(KC):
                        last = act.activation(vT[:, m, :], VT[:, m * TOK:(m + 1) * TOK], ACT.Identity,
                                              bias=bias_in[:, 3 * KC + m:3 * KC + m + 1])
                    last.then_inc(vt_ok, 1)
                if in_stage(w):
                    act.wait_ge(vtok_full, w + 1)
                    at_least(act, out_full, w)
                    act.activation(v_tok[:].rearrange("p b d -> p (b d)"), VTOK[:], ACT.Copy).then_inc(vtok_ok, 1)
                for i in next_pieces(w, following):
                    following.act_piece(act, i)
            windows(act, window)

        @block.vector
        def _(dve):
            def window(w, parity):
                if in_stage(w - 1):
                    dve.wait_ge(sc_full, w)
                    at_least(dve, exp_ok, w - 1)
                    dve.tensor_reduce(top[:], SC[:, 0:TOK].rearrange("p (b t) -> p b t", b=PAIR), AXX, ALU.max).then_inc(top_ok, 1)
                    dve.wait_ge(top_ok, w)
                    dve.tensor_scalar(shift[:], top[:], -(D ** -0.5), None, ALU.mult).then_inc(shift_ok, 1)
                if isinstance(w, int) and w == -2:
                    norm.dve_moments(dve, 1)
                if takes_moments(w):
                    norm.dve_moments(dve, w + 2)
                if first_of_next(w):
                    dve.wait_ge(out_ok, 1)
                    next_norm.dve_moments(dve, 0)
                ln.dve_low(dve, w, parity)
                if in_stage(w + 1):
                    dve.wait_ge(pc_hi, w + 2)
                    dve.tensor_tensor(cT_lo[1 - parity][:], chunked(PC), f32(cT_hi[1 - parity][:]), ALU.subtract).then_inc(pc_lo, 1)
                if has_norm(w):
                    norm.dve_normalise(dve, w + 2)
                if first_of_next(w):
                    next_norm.dve_normalise(dve, 0)
                if in_stage(w - 1):
                    dve.wait_ge(exp_ok, w)
                    dve.reciprocal(inv_total[:], total[:]).then_inc(inv_ok, 1)
                    dve.wait_ge(inv_ok, w)
                    dve.wait_ge(out_full, w)
                    for b in range(PAIR):
                        last = dve.scalar_tensor_tensor(norm.x(w - 1, b), OUT[:, b * D:(b + 1) * D], inv_total[:, b:b + 1],
                                                        norm.x(w - 1, b), op0=ALU.mult, op1=ALU.add)
                    last.then_inc(out_ok, 1)
                for i in next_pieces(w, following):
                    following.dve_piece(dve, i)
            windows(dve, window)

        @block.tensor
        def _(pe):
            def transposes(w, parity):
                ln.pe_transpose(pe, w)
                if in_stage(w + 1):
                    pe.wait_ge(cx_in[1 - parity], 16 * ((w + 1) // 2 + 1) if isinstance(w, int) else cx_count(w + 1, 1 - parity))
                    at_least(pe, pc_lo, w + 1)
                    for c in range(KC):
                        for b in range(PAIR):
                            last = pe.transpose(PC[:, c * TOK + b * P:c * TOK + (b + 1) * P],
                                                cx[1 - parity][:, b, c * P:(c + 1) * P], consts["ident"][:])
                    last.then_inc(pc_full, 1)

            def window(w, parity):
                if in_stage(w - 1):
                    pe.wait_ge(vt_ok, w)
                    at_least(pe, exp_ok, w - 1)
                    for b in range(PAIR):
                        for k in range(KC):
                            last = pe.matmul(SC[:, b * P:(b + 1) * P], ent[:, k, b * P:(b + 1) * P],
                                             vT[:, k, b * P:(b + 1) * P], start=(k == 0), stop=(k == KC - 1))
                    last.then_inc(sc_full, 1)
                if not starts(w):
                    transposes(w, parity)
                if in_stage(w):
                    hi, lo, chi, clo = ln.hi[parity], ln.lo[parity], cT_hi[parity], cT_lo[parity]
                    if isinstance(w, int) and w == 0:
                        pe.wait_ge(wt.w_ok, 3)
                    pe.wait_ge(ln.lo_ok, w + 1)
                    pe.wait_ge(pc_lo, w + 1)
                    at_least(pe, ent_ok, w)
                    for m in range(KC):
                        eq, ek = slice(m * P, (m + 1) * P), slice(D + m * P, D + (m + 1) * P)
                        last = three_pass(pe, ENT[:, m * TOK:(m + 1) * TOK],
                                          lambda k: w_hi[:, k, eq] if k < KC else w_hi[:, k - KC, ek],
                                          lambda k: w_lo[:, k, eq] if k < KC else w_lo[:, k - KC, ek],
                                          lambda k: hi[:, k, :] if k < KC else chi[:, k - KC, :],
                                          lambda k: lo[:, k, :] if k < KC else clo[:, k - KC, :], 2 * KC)
                    last.then_inc(ent_full, 1)
                if starts(w):
                    transposes(w, parity)
                if in_stage(w - 1):
                    pe.wait_ge(exp_ok, w)
                    at_least(pe, pp_ok, w - 1)
                    for b in range(PAIR):
                        last = pe.transpose(PP[:, b * P:(b + 1) * P], probs[:, b, :], consts["ident"][:])
                    last.then_inc(pp_full, 1)
                if in_stage(w):
                    at_least(pe, vt_ok, w)
                    for m in range(KC):
                        ev = slice(2 * D + m * P, 2 * D + (m + 1) * P)
                        last = three_pass(pe, VT[:, m * TOK:(m + 1) * TOK], lambda k: w_hi[:, k, ev], lambda k: w_lo[:, k, ev],
                                          lambda k: chi[:, k, :], lambda k: clo[:, k, :], KC)
                    last.then_inc(vt_full, 1)
                if in_stage(w - 1):
                    pe.wait_ge(pp_ok, w)
                    pe.wait_ge(vtok_ok, w)
                    at_least(pe, out_ok, w - 1)
                    for b in range(PAIR):
                        last = pe.matmul(OUT[:, b * D:(b + 1) * D], probsT[:, b, :], v_tok[:, b, :], start=True, stop=True)
                    last.then_inc(out_full, 1)
                if in_stage(w):
                    pe.wait_ge(vt_ok, w + 1)
                    at_least(pe, vtok_ok, w)
                    for b in range(PAIR):
                        for c in range(KC):
                            last = pe.transpose(VTOK[:, b * D + c * P:b * D + (c + 1) * P],
                                                vT[:, c, b * P:(b + 1) * P], consts["ident"][:])
                    last.then_inc(vtok_full, 1)
            windows(pe, window)
    nm.end()
    return nm


def routed_stage(nc, name, before, norm, next_norm, consts, wt, following):
    FC = F // P
    ER = E * R
    GA = E + ER
    nm = Names(nc, ExitStack(), name, before)
    sb, sem = nm.sb, nm.sem
    PT, RT, LT, OUT = (nm.ps(n) for n in ("PT", "RT", "LT", "OUT"))
    HB = [nm.ps(f"HB{i}") for i in range(2)]
    ln = Normed(nm, norm, next_norm, PT)
    following.stage(nm)
    wi_hi, wi_lo, wo_hi, wo_lo, b_parts = wt.wi_hi, wt.wi_lo, wt.wo_hi, wt.wo_lo, wt.b_parts
    gate_row, bias_i, row_o, expert_of = wt.gate_row, wt.bias_i, wt.row_o, wt.expert_of
    route_mark = sb("route_mark", [P, 1])
    logits, top8 = sb("logits", [P, PAIR, E]), sb("top8", [P, PAIR, 8])
    top_at, top1 = sb("top_at", [P, PAIR, 8], U32), sb("top1", [P, PAIR])
    low32, low_hi = sb("low32", [P, PAIR, ER]), sb("low_hi", [P, PAIR, ER], F32R)
    low_parts = sb("low_parts", [P, PAIR, 3 * ER])
    lowT = [sb(f"lowT{i}", [3 * ER, TOK], F32R) for i in range(2)]
    h32 = [sb(f"h32_{i}", [P, 2 * TOK]) for i in range(2)]
    h_hi = [sb(f"h_hi{i}", [P, FC // 2, 2 * TOK], F32R) for i in range(2)]
    h_lo = [sb(f"h_lo{i}", [P, FC // 2, 2 * TOK], F32R) for i in range(2)]
    biased = sem("biased")
    rt_full, link, low_ok, lt_full, lt_ok = (sem(n) for n in ("rt_full", "link", "low_ok", "lt_full", "lt_ok"))
    hb_full, relu_ok, hhi_ok, hlo_ok, out_full, out_ok = (sem(n) for n in ("hb_full", "relu_ok", "hhi_ok", "hlo_ok", "out_full", "out_ok"))
    HALVES = FC // 2
    LINKS = 11

    with nc.Block() as block:

        @block.sync
        def _(sp):
            following.load(sp)

        @block.gpsimd
        def _(pool):
            wt.wait_in(pool)

            def add_bias(w):
                pool.wait_ge(norm.xn_ok, w + 1)
                pool.tensor_tensor(norm.x_group(w), norm.x_group(w), row_o[:], ALU.add).then_inc(biased, 1)
            add_bias(0)
            with pool.Fori(1, NG) as w:
                norm.pool_rstd(pool, w)
                add_bias(w)
            next_norm.pool_rstd(pool, 0)
            nm.clear_before(pool)

        @block.scalar
        def _(act):
            wt.wait_in(act)

            def window(w, parity):
                ln.act_high(act, w, parity, hb_full, HALVES)
                for n in range(HALVES):
                    if in_stage(w):
                        T = w * HALVES + n
                        act.wait_ge(hb_full, T + 1)
                        at_least(act, hlo_ok, T - 1)
                        for m in range(2):
                            f = 2 * n + m
                            last = act.activation(h32[n % 2][:, m * TOK:(m + 1) * TOK], HB[n % 2][:, m * TOK:(m + 1) * TOK],
                                                  ACT.Relu, bias=bias_i[:, f:f + 1])
                        last.then_inc(relu_ok, 1)
                        if n == 0:
                            at_least(act, out_full, w - 1)
                        act.wait_ge(relu_ok, T + 1)
                        act.activation(h_hi[parity][:, n, :], h32[n % 2][:], ACT.Copy).then_inc(hhi_ok, 1)
                if in_stage(w + 1):
                    act.wait_ge(lt_full, w + 2)
                    at_least(act, hb_full, w * HALVES)
                    act.activation(lowT[1 - parity][:], LT[0:3 * ER, 0:TOK], ACT.Copy).then_inc(lt_ok, 1)
                for i in next_pieces(w, following):
                    following.act_piece(act, i)
            windows(act, window)

        @block.vector
        def _(dve):
            wt.wait_in(dve)

            def route(w):
                done = [0]

                def step(*instructions, apart=False):
                    for ins in instructions:
                        done[0] += 1
                        ins.then_inc(link, 1)
                    if apart:
                        wait_apart(dve, link, w * LINKS + done[0], route_mark)
                        done[0] += 1
                    else:
                        dve.wait_ge(link, w * LINKS + done[0])
                dve.wait_ge(rt_full, w + 1)
                rt = RT[:, 0:PAIR * GA].rearrange("p (b n) -> p b n", b=PAIR)
                at_least(dve, lt_full, w)
                step(dve.tensor_tensor(logits[:], rt[:, :, 0:E], gate_row[:], ALU.add), apart=True)
                step(*(dve.max(top8[:, b, :], logits[:, b, :]) for b in range(PAIR)), apart=True)
                step(*(dve.max_index(top_at[:, b, :], top8[:, b, :], logits[:, b, :]) for b in range(PAIR)))
                step(dve.tensor_copy(top1[:], top_at[:, :, 0]))
                step(*(dve.scalar_tensor_tensor(low32[:, b, :], expert_of[:], top1[:, b:b + 1], rt[:, b, E:],
                                                op0=ALU.is_equal, op1=ALU.mult) for b in range(PAIR)))
                step(dve.tensor_copy(low_hi[:], low32[:]))
                dve.tensor_tensor(low_parts[:, :, 2 * ER:], low32[:], f32(low_hi[:]), ALU.subtract)
                dve.tensor_copy(low_parts[:, :, 0:ER], f32(low_hi[:]))
                dve.tensor_copy(low_parts[:, :, ER:2 * ER], f32(low_hi[:])).then_inc(low_ok, 1)

            def window(w, parity):
                ln.dve_low(dve, w, parity)
                for n in range(HALVES):
                    if in_stage(w):
                        T = w * HALVES + n
                        dve.wait_ge(hhi_ok, T + 1)
                        dve.tensor_tensor(h_lo[parity][:, n, :], h32[n % 2][:], f32(h_hi[parity][:, n, :]),
                                          ALU.subtract).then_inc(hlo_ok, 1)
                    if n == 0 and isinstance(w, int) and w == -2:
                        norm.dve_moments(dve, 1)
                    if n == 0 and takes_moments(w):
                        norm.dve_moments(dve, w + 2)
                    if n == 1 and has_norm(w):
                        norm.dve_normalise(dve, w + 2)
                    if n == 0 and first_of_next(w):
                        dve.wait_ge(out_ok, 1)
                        next_norm.dve_moments(dve, 0)
                    if n == 1 and first_of_next(w):
                        next_norm.dve_normalise(dve, 0)
                    if n == 2 and in_stage(w + 1):
                        route(w + 1)
                if in_stage(w - 1):
                    dve.wait_ge(out_full, w)
                    dve.wait_ge(biased, w)
                    dve.tensor_tensor(norm.x_group(w - 1), norm.x_group(w - 1),
                                      OUT[:].rearrange("p (b d) -> p b d", b=PAIR), ALU.add).then_inc(out_ok, 1)
                for i in next_pieces(w, following):
                    following.dve_piece(dve, i)
            windows(dve, window)

        @block.tensor
        def _(pe):
            wt.wait_split(pe)

            def gate(w, parity):
                hi, lo = ln.hi[parity], ln.lo[parity]
                pe.wait_ge(ln.lo_ok, w + 1)
                at_least(pe, low_ok, w)
                for b in range(PAIR):
                    tok = slice(b * P, (b + 1) * P)
                    last = three_pass(pe, RT[:, b * GA:(b + 1) * GA], lambda k: hi[:, k, tok], lambda k: lo[:, k, tok],
                                      lambda k: wi_hi[:, k, F:], lambda k: wi_lo[:, k, F:], KC)
                last.then_inc(rt_full, 1)

            def window(w, parity):
                ln.pe_transpose(pe, w)
                if in_stage(w):
                    hi, lo = ln.hi[parity], ln.lo[parity]
                    for n in range(HALVES):
                        if in_stage(w + 1) and n == HALVES - 1:
                            gate(w + 1, 1 - parity)
                        T = w * HALVES + n
                        at_least(pe, relu_ok, T - 1)
                        if n == 0:
                            pe.wait_ge(ln.lo_ok, w + 1)
                            pe.wait_ge(lt_ok, w + 1)
                        for m in range(2):
                            out = HB[n % 2][:, m * TOK:(m + 1) * TOK]
                            fs = slice((2 * n + m) * P, (2 * n + m + 1) * P)
                            for k in range(KC):
                                pe.matmul(out, wi_hi[:, k, fs], hi[:, k, :], start=(k == 0), stop=False)
                                pe.matmul(out, wi_lo[:, k, fs], hi[:, k, :], start=False, stop=False)
                                pe.matmul(out, wi_hi[:, k, fs], lo[:, k, :], start=False, stop=False)
                            last = pe.matmul(out, b_parts[:, fs], lowT[parity][:], start=False, stop=True)
                        last.then_inc(hb_full, 1)
                elif in_stage(w + 1):
                    gate(w + 1, 1 - parity)
                if in_stage(w - 1):
                    pe.wait_ge(hlo_ok, w * HALVES)
                    at_least(pe, out_ok, w - 1)
                    h, l = h_hi[1 - parity], h_lo[1 - parity]
                    for b in range(PAIR):
                        def chunk(t, k, b=b):
                            return t[:, k // 2, (k % 2) * TOK + b * P:(k % 2) * TOK + (b + 1) * P]
                        last = three_pass(pe, OUT[:, b * D:(b + 1) * D], lambda k: chunk(h, k), lambda k: chunk(l, k),
                                          lambda k: wo_hi[:, k, :], lambda k: wo_lo[:, k, :], FC)
                    last.then_inc(out_full, 1)
                if in_stage(w + 1):
                    pe.wait_ge(low_ok, w + 2)
                    at_least(pe, lt_ok, w + 1)
                    for b in range(PAIR):
                        last = pe.transpose(LT[0:3 * ER, b * P:(b + 1) * P], low_parts[:, b, :], consts["ident"][:])
                    last.then_inc(lt_full, 1)
            windows(pe, window)
    nm.end()
    return nm


def ternary_stage(nc, name, before, norm, consts, wt, out_dram, next_norm=None):
    FC = F // P
    HB_COLS = 512
    HALVES = F // HB_COLS
    nm = Names(nc, ExitStack(), name, before)
    sb, sem = nm.sb, nm.sem
    PT, OUT = nm.ps("PT"), nm.ps("OUT")
    HB = [nm.ps(f"HB{i}") for i in range(2)]
    ZT = [nm.ps(f"ZT{i}") for i in range(4)]
    ln = Normed(nm, norm, next_norm, PT)
    quant, quant_ok, gain, offset = wt.quant, wt.quant_ok, wt.gain, wt.offset
    hid = [[sb(f"hid{i}{b}", [P, F]) for b in range(PAIR)] for i in range(2)]
    z = [sb(f"z{b}", [P, F]) for b in range(PAIR)]
    h_stats, h_moments = sb("h_stats", [P, PAIR, HALVES, 6]), sb("h_moments", [P, PAIR, 2])
    h_var, h_rstd = sb("h_var", [P, PAIR]), sb("h_rstd", [P, PAIR])
    y32 = [sb(f"y32_{i}", [P, 2 * TOK]) for i in range(FC // 2)]
    y_hi = [sb(f"y_hi{i}", [P, FC // 2, 2 * TOK], F32R) for i in range(2)]
    y_lo = [sb(f"y_lo{i}", [P, FC // 2, 2 * TOK], F32R) for i in range(2)]
    hs_mark = sb("hs_mark", [P, 1])
    first_gelu = sb("first_gelu", [P, 1])
    hb_full, gelu_ok, hs_link, hvar_ok, hrstd_ok, z_ok = (
        sem(n) for n in ("hb_full", "gelu_ok", "hs_link", "hvar_ok", "hrstd_ok", "z_ok"))
    zt_full, y_ok, yhi_ok, out_full, out_ok, stored = (sem(n) for n in ("zt_full", "y_ok", "yhi_ok", "out_full", "out_ok", "stored"))
    ylo_ok = [sem("ylo_first_ok"), sem("ylo_last_ok")]
    PARTS = FC // 2
    FILLS = PAIR * HALVES
    LINKS = FILLS + 1 + PAIR

    def low_part(eng, w, n, parity):
        eng.wait_ge(yhi_ok, w * PARTS + n + 1)
        eng.tensor_tensor(y_lo[parity][:, n, :], y32[n][:], f32(y_hi[parity][:, n, :]), ALU.subtract).then_inc(ylo_ok[n // 2], 1)

    with nc.Block() as block:

        @block.sync
        def _(sp):

            def store(w):
                sp.wait_ge(out_ok, w + 1)
                dst = out_dram[:, w * PAIR:(w + 1) * PAIR, :] if isinstance(w, int) else \
                    out_dram[:, bass.ds(w * PAIR, PAIR), :]
                sp.dma_start(dst, norm.x_group(w)).then_inc(stored, 16)
            with sp.Fori(0, NG) as w:
                store(w)
            sp.wait_ge(stored, 16 * NG)

        @block.gpsimd
        def _(pool):
            def window(w, parity):
                if has_norm(w):
                    norm.pool_rstd(pool, w + 2)
                if in_stage(w - 1):
                    low_part(pool, w - 1, 0, 1 - parity)
                if in_stage(w - 1):
                    low_part(pool, w - 1, 1, 1 - parity)
                if in_stage(w):
                    pool.wait_ge(hs_link, w * LINKS + LINKS)
                    at_least(pool, z_ok, w * PAIR)
                    pool.tensor_tensor(h_var[:], h_moments[:, :, 1], consts["ln_eps"][:], ALU.add).then_inc(hvar_ok, 1)
                    pool.wait_ge(hvar_ok, w + 1)
                    pool.tensor_tensor(h_rstd[:], h_var[:], consts["minus_half"][:], ALU.pow).then_inc(hrstd_ok, 1)
            windows(pool, window)
            nm.clear_before(pool)

        @block.scalar
        def _(act):
            act.activation(first_gelu[:], consts["ones"][:, 0:1], ACT.Gelu)
            wt.wait_in(act)

            def activate(w, n, parity):
                at_least(act, z_ok, (w - 1) * PAIR)
                act.wait_ge(hb_full, w * FILLS + n + 1)
                act.activation(hid[parity][n // HALVES][:, (n % HALVES) * HB_COLS:(n % HALVES + 1) * HB_COLS],
                               HB[n % 2][:], ACT.Gelu).then_inc(gelu_ok, 1)

            def rescale(w, n, parity):
                T = w * PARTS + n
                act.wait_ge(zt_full, T + 1)
                at_least(act, ylo_ok[n // 2], (w - 1) * 2 + n % 2 + 1)
                for m in range(2):
                    f = 2 * n + m
                    last = act.activation(y32[n][:, m * TOK:(m + 1) * TOK], ZT[n][:, m * TOK:(m + 1) * TOK],
                                          ACT.Identity, bias=offset[:, f:f + 1], scale=gain[:, f:f + 1])
                last.then_inc(y_ok, 1)
                if n == 0:
                    at_least(act, out_full, w - 1)
                act.wait_ge(y_ok, T + 1)
                act.activation(y_hi[parity][:, n, :], y32[n][:], ACT.Copy).then_inc(yhi_ok, 1)

            def window(w, parity):
                ln.act_high(act, w, parity, hb_full, FILLS)
                if in_stage(w):
                    activate(w, 0, parity)
                for n in range(PARTS):
                    if in_stage(w) and n + 1 < FILLS:
                        activate(w, n + 1, parity)
                    if in_stage(w - 1):
                        rescale(w - 1, n, 1 - parity)
            windows(act, window)

        @block.vector
        def _(dve):
            wt.wait_in(dve)

            def spread(w, n, parity):
                dve.wait_ge(gelu_ok, w * FILLS + n + 1)
                b, half = n // HALVES, n % HALVES
                dve.bn_stats(h_stats[:, b, half, :], hid[parity][b][:, half * HB_COLS:(half + 1) * HB_COLS]).then_inc(hs_link, 1)

            def window(w, parity):
                ln.dve_low(dve, w, parity)
                if in_stage(w):
                    spread(w, 0, parity)
                    spread(w, 1, parity)
                if isinstance(w, int) and w == -2:
                    norm.dve_moments(dve, 1)
                if takes_moments(w):
                    norm.dve_moments(dve, w + 2)
                if in_stage(w - 2):
                    dve.wait_ge(out_full, w - 1)
                    dve.tensor_tensor(norm.x_group(w - 2), norm.x_group(w - 2),
                                      OUT[:].rearrange("p (b d) -> p b d", b=PAIR), ALU.add).then_inc(out_ok, 1)
                if has_norm(w):
                    norm.dve_normalise(dve, w + 2)
                if in_stage(w):
                    spread(w, 2, parity)
                    spread(w, 3, parity)
                    wait_apart(dve, hs_link, w * LINKS + FILLS, hs_mark)
                    for b in range(PAIR):
                        dve.bn_aggr(h_moments[:, b, :], h_stats[:, b].rearrange("p h s -> p (h s)")).then_inc(hs_link, 1)
                if in_stage(w - 1):
                    low_part(dve, w - 1, 2, 1 - parity)
                if in_stage(w):
                    dve.wait_ge(hrstd_ok, w + 1)
                    at_least(dve, zt_full, w * PARTS)
                    for b in range(PAIR):
                        dve.tensor_scalar(z[b][:], hid[parity][b][:], h_moments[:, b, 0:1], h_rstd[:, b:b + 1],
                                          ALU.subtract, ALU.mult).then_inc(z_ok, 1)
                if in_stage(w - 1):
                    low_part(dve, w - 1, 3, 1 - parity)
            windows(dve, window, NG + 1)

        @block.tensor
        def _(pe):
            def expand(w, n, parity):
                at_least(pe, gelu_ok, w * FILLS + n - 1)
                tok = slice((n // HALVES) * P, (n // HALVES + 1) * P)
                cols = slice((n % HALVES) * HB_COLS, (n % HALVES + 1) * HB_COLS)
                for k in range(KC):
                    pe.matmul(HB[n % 2][:], ln.hi[parity][:, k, tok], quant[0][:, k, cols], start=(k == 0), stop=False)
                    last = pe.matmul(HB[n % 2][:], ln.lo[parity][:, k, tok], quant[0][:, k, cols], start=False, stop=(k == KC - 1))
                last.then_inc(hb_full, 1)

            def turn(w, n):
                at_least(pe, y_ok, (w - 1) * PARTS + n + 1)
                for m in range(2):
                    for b in range(PAIR):
                        f = 2 * n + m
                        last = pe.transpose(ZT[n][:, m * TOK + b * P:m * TOK + (b + 1) * P], z[b][:, f * P:(f + 1) * P],
                                            consts["ident"][:])
                last.then_inc(zt_full, 1)

            def contract(w, parts, parity):
                if parts[0] == 0:
                    at_least(pe, out_ok, w)
                if isinstance(w, int) and w == 0:
                    pe.wait_ge(quant_ok, 4)
                for k in range(2 * parts[0], 2 * parts[-1] + 2):
                    part = k // 2
                    if k % 2 == 0:
                        pe.wait_ge(yhi_ok, w * PARTS + part + 1)
                        pe.wait_ge(ylo_ok[part // 2], w * 2 + part % 2 + 1)
                    for b in range(PAIR):
                        cols = slice((k % 2) * TOK + b * P, (k % 2) * TOK + (b + 1) * P)
                        for y in (y_hi[parity], y_lo[parity]):
                            last = pe.matmul(OUT[:, b * D:(b + 1) * D], y[:, part, cols], quant[1][:, k, :],
                                             start=(k == 0 and b == 0 and y is y_hi[parity]),
                                             stop=(k == FC - 1 and b == PAIR - 1 and y is y_lo[parity]))
                if parts[-1] == PARTS - 1:
                    last.then_inc(out_full, 1)

            def window(w, parity):
                if not starts(w):
                    ln.pe_transpose(pe, w)
                if in_stage(w):
                    pe.wait_ge(ln.lo_ok, w + 1)
                    if starts(w):
                        pe.wait_ge(quant_ok, 2)
                    expand(w, 0, parity)
                    expand(w, 1, parity)
                if starts(w):
                    ln.pe_transpose(pe, w)
                if in_stage(w - 2):
                    contract(w - 2, (0, 1), parity)
                if in_stage(w - 1):
                    pe.wait_ge(z_ok, w * PAIR)
                    turn(w - 1, 0)
                if in_stage(w):
                    expand(w, 2, parity)
                if in_stage(w - 2):
                    contract(w - 2, (2, 3), parity)
                if in_stage(w - 1):
                    turn(w - 1, 1)
                if in_stage(w):
                    expand(w, 3, parity)
                if in_stage(w - 1):
                    turn(w - 1, 2)
                    turn(w - 1, 3)
            windows(pe, window, NG + 1)
    nm.end()
    return nm


def decoder(nc, a, out):
    with ExitStack() as ctx:
        nm = Names(nc, ctx, "all")
        x_res = nm.sb("x_res", [P, NB, D])
        constants = Constants(nm, a)
        consts = constants.tiles

        odd = nm.sb("odd_weights", [P, 4 + 2 * PAIR * D + TOK]), nm.sb("odd_split", [P, 2 * KC * GATED + 2 * F * D // P + F], F32R)
        even = nm.sb("even_weights", [P, 2 * F * D // P + 2 * F // P + 10]), nm.sb("even_split", [P, 2 * KC * 4 * D], F32R)

        def spare():
            return Arena(*odd, used=(odd[0].shape[1], 2 * KC * 4 * D))
        L0_attn = AttentionWeights(nm, "a0", Arena(*odd), [(0, a["L0_attn_Wqkv"]), (3, a["L0_attn_Wout"])],
                                   [("bias_cols", a["L0_attn_bqk"]), ("row_v", a["L0_attn_bv"]), ("row_o", a["L0_attn_bout"]),
                                    ("q_mul", a["emb"]), ("w_turned", a["L0_attn_Wturned"]), ("bias_turned", a["L0_attn_bturned"])],
                                   rope=True)
        L0_xattn = EntangledWeights(nm, "b0", Arena(*even), a)
        L0_ffn = RoutedWeights(nm, "c0", Arena(*odd), a)
        L1_attn = AttentionWeights(nm, "a1", Arena(*even), [(0, a["L1_attn_W_query"]), (1, a["L1_attn_W_key"]),
                                                                (2, a["L1_attn_W_val"]), (3, a["L1_attn_W_out"])], [])
        L1_xattn = AttentionWeights(nm, "a2", Arena(*odd), [(0, a["L1_xattn_wq"]), (1, a["L1_xattn_wk"]),
                                                                 (2, a["L1_xattn_wv"]), (3, a["L1_xattn_wo"])],
                                    [("bias_cols", a["L1_xattn_bqk"]), ("row_v", a["L1_xattn_bv"]), ("row_o", a["L1_xattn_bo"])])
        L1_ffn = TernaryWeights(nm, "d1", Arena(*even), a, consts["ones"])
        cx_tiles = [nm.sb(f"cx{i}", [P, PAIR, D]) for i in range(2)]
        contexts = [Context(nm, name, a["ctx"], cx_tiles) for name in ("b0", "a2")]
        ln_buffers = [GroupNorm.buffers(nm, i) for i in range(2)]
        names = ("a0", "b0", "c0", "a1", "a2", "d1")
        norms = [GroupNorm(nm, name, x_res, consts, ln_buffers[n % 2]) for n, name in enumerate(names)]
        done = attention_stage(nc, "a0", None, norms[0], norms[1], consts, L0_attn, L0_xattn, spare(), rope=True, v_bias=True,
                        o_bias=True, x_dram=a["x"], constants=constants, next_context=contexts[0])
        done = entangled_stage(nc, "b0", done, norms[1], norms[2], consts, contexts[0], L0_xattn, L0_ffn)
        done = routed_stage(nc, "c0", done, norms[2], norms[3], consts, L0_ffn, L1_attn)
        done = attention_stage(nc, "a1", done, norms[3], norms[4], consts, L1_attn, L1_xattn, spare(),
                               next_context=contexts[1])
        done = attention_stage(nc, "a2", done, norms[4], norms[5], consts, L1_xattn, L1_ffn, spare(), context=contexts[1],
                        mask_dram=a["mask"], k_bias=True, v_bias=True, o_bias=True)
        done = ternary_stage(nc, "d1", done, norms[5], consts, L1_ffn, out)
        done.sem_ctx.close()
        nm.sem_ctx.close()


def layout(inputs):
    g = {k: np.asarray(v) for k, v in inputs.items()}

    def chunks(w):
        return w.reshape(-1, P, w.shape[1]).transpose(1, 0, 2)

    def cols(*bs):
        return np.concatenate([b.reshape(-1, P).T for b in bs], axis=1)

    def row(b, n=PAIR):
        return np.broadcast_to(b, (P, n, b.shape[0]))

    turned = np.array([h * DH + (2 * j + 1 if j < DH // 2 else 2 * (j - DH // 2)) for h in range(2 * H) for j in range(DH)])
    theta = np.float32(10000.0) ** (-np.arange(0, DH, 2, dtype=np.float32) / np.float32(DH))
    freqs = np.arange(P, dtype=np.float32)[:, None] * theta[None, :]
    emb = np.concatenate([np.sin(freqs), np.cos(freqs)], axis=-1).astype(np.float32)
    p = np.arange(P)
    a = {
        "x": g["x"].transpose(1, 0, 2), "ctx": g["ctx_1024"].transpose(1, 0, 2), "mask": g["mask_SxS2_bk0"],
        "ident": np.eye(P, dtype=np.float32),
        "head_mask": ((p[:, None] // DH) % QH == np.arange(QH)[None, :]).astype(np.float32),
        "turn_sign": np.where(p % DH < DH // 2, -1, 1).astype(np.float32)[:, None],
        "emb": np.tile(emb.T, (P // DH, PAIR)),
        "L0_attn_Wqkv": chunks(g["L0_attn_Wqkv"]), "L0_attn_Wturned": chunks(g["L0_attn_Wqkv"][:, turned]),
        "L0_attn_bqk": cols(g["L0_attn_bqkv"][:2 * D]), "L0_attn_bturned": cols(g["L0_attn_bqkv"][turned]),
        "L0_attn_bv": row(g["L0_attn_bqkv"][2 * D:]), "L0_attn_Wout": chunks(g["L0_attn_Wout"]),
        "L0_attn_bout": row(g["L0_attn_bout"]),
        "L1_xattn_bqk": cols(g["L1_xattn_bq"], g["L1_xattn_bk"]), "L1_xattn_bv": row(g["L1_xattn_bv"]),
        "L1_xattn_bo": row(g["L1_xattn_bo"]), "L1_xattn_wo": chunks(g["L1_xattn_wo"].T),
        "L1_attn_W_out": chunks(g["L1_attn_W_out"].reshape(D, D)),
    }
    a.update({
        "L0_xattn_Wq": chunks(g["L0_xattn_Wq"]), "L0_xattn_Wk": chunks(g["L0_xattn_Wk"]),
        "L0_xattn_Weq": chunks(g["L0_xattn_We"][:, :D].T), "L0_xattn_Wek": chunks(g["L0_xattn_We"][:, D:].T),
        "L0_xattn_Wv": chunks(g["L0_xattn_Wv"].T),
        "L0_xattn_b": cols(*(g[f"L0_xattn_b{n}"] for n in "qkev")),
        "L0_ffn_wi_W": chunks(g["L0_ffn_wi_W"].T), "L0_ffn_wo_W": chunks(g["L0_ffn_wo_W"].T),
        "L0_ffn_gA": chunks(np.concatenate([g["L0_ffn_gate_W"], g["L0_ffn_lora_A"].reshape(E * R, D)]).T),
        "L0_ffn_B": np.tile(g["L0_ffn_lora_B"].transpose(0, 2, 1).reshape(E * R, F), (3, 1)),
        "L0_ffn_gate_b": row(g["L0_ffn_gate_b"]), "L0_ffn_wi_b": cols(g["L0_ffn_wi_b"]), "L0_ffn_wo_b": row(g["L0_ffn_wo_b"]),
        "L1_ffn_W_fc": chunks(g["L1_ffn_W_fc"].T).reshape(P, -1), "L1_ffn_W_proj": chunks(g["L1_ffn_W_proj"].T).reshape(P, -1),
        "L1_ffn_ln_w": cols(g["L1_ffn_ln_w"]), "L1_ffn_ln_b": cols(g["L1_ffn_ln_b"]),
        "expert_of": np.broadcast_to((np.arange(E * R) // R).astype(np.float32), (P, E * R)),
    })
    for k in ("L1_attn_W_query", "L1_attn_W_key", "L1_attn_W_val"):
        a[k] = chunks(g[k].transpose(1, 0, 2).reshape(D, D))
    for k in ("L1_xattn_wq", "L1_xattn_wk", "L1_xattn_wv"):
        a[k] = chunks(g[k].T)
    return {k: np.ascontiguousarray(v) for k, v in a.items()}


def kernel(**inputs):
    import numpy as _np
    import concourse.bacc as _bacc
    from concourse import mybir as _mybir
    from concourse.bass_utils import run_bass_kernel_spmd as _run

    nc = _bacc.Bacc("TRN2", target_bir_lowering=False, num_devices=1)
    arrays, args = {}, {}
    for name, value in layout(inputs).items():
        arrays[f"in_{name}"] = value
        args[name] = nc.dram_tensor(f"in_{name}", value.shape, _mybir.dt.from_np(value.dtype), kind="ExternalInput").ap()
    out = nc.dram_tensor("out_x", (P, NB, D), FP32, kind="ExternalOutput").ap()
    decoder(nc, args, out)
    r = _run(nc, [arrays], core_ids=[0])
    return _np.ascontiguousarray(_np.asarray(r.results[0]["out_x"]).transpose(1, 0, 2))
```
